# Optimizing a Trainium2 kernel written in Bass

```python
import numpy as np
import jax
import jax.numpy as jnp

def _softmax(x, axis=-1):
    return jax.nn.softmax(x, axis=axis)

def _gelu(x):
    return jax.nn.gelu(x, approximate=True)

def _silu(x):
    return jax.nn.silu(x)

def _sigmoid(x):
    return jax.nn.sigmoid(x)

def _layernorm(x, axis=-1, eps=1e-05):
    m = jnp.mean(x, axis=axis, keepdims=True)
    v = jnp.var(x, axis=axis, keepdims=True)
    return (x - m) / jnp.sqrt(v + eps)

def _scatter_add(tgt, idx, src, axis=0):
    return tgt.at[idx].add(src)

def _segment_sum(src, seg, n):
    return jax.ops.segment_sum(src, seg, n)
kernel_name = 'mk_lm_tower_d1_tok_ids512_r4_940e83'

def setup_inputs(seed: int=0):
    np.random.seed(seed)
    _w = jnp.asarray

    def _rec_inputs():
        import jax
        import jax.numpy as jnp
        _rk = jax.random.key(seed)
        x = jax.random.randint(jax.random.fold_in(_rk, 1), (2, 2048), 0, 8000, jnp.int32)
        return x
    x = _rec_inputs()

    def _L0_tok_setup():
        import jax, jax.numpy as jnp
        import numpy as np
        EPS = 1e-05
        key = jax.random.key(seed)
        k1, k2, k3 = jax.random.split(key, 3)
        B, T, V, C, K = (8, 1024, 8000, 128, 3)
        tokens = jax.random.randint(k1, (B, T), 0, V, dtype=jnp.int64)
        embed_table = jax.random.normal(k2, (V, C), dtype=jnp.float32)
        conv_w = jax.random.normal(k3, (C, K), dtype=jnp.float32) * (1.0 / np.sqrt(K))
        gamma = jnp.ones((C,), dtype=jnp.float32)
        beta = jnp.zeros((C,), dtype=jnp.float32)
        return {'tokens': tokens, 'embed_table': embed_table, 'conv_w': conv_w, 'gamma': gamma, 'beta': beta}
    _L0_tok_all = _L0_tok_setup()
    _L0_tok_in = {k: v for k, v in _L0_tok_all.items() if k in ('embed_table', 'conv_w', 'gamma', 'beta')}
    del _L0_tok_all

    def _L0_attn_setup():
        import jax, jax.numpy as jnp
        import numpy as np
        B, L, D = (1, 512, 128)
        NL, N, K = (4, 16, 4)
        DI = 2 * D
        R = D // 16
        H = 4 * D

        def _ln(x, w, b, eps=1e-05):
            mu = x.mean(-1, keepdims=True)
            v = ((x - mu) ** 2).mean(-1, keepdims=True)
            return (x - mu) * jax.lax.rsqrt(v + eps) * w + b

        def _rms(x, w, eps=1e-05):
            return x * jax.lax.rsqrt((x * x).mean(-1, keepdims=True) + eps) * w

        def _ssm_scan(delta, Bm, Cm, u, A, Dp):

            def step(h, inp):
                d_t, b_t, c_t, u_t = inp
                dA = jnp.exp(d_t[..., None] * A)
                h = dA * h + (d_t * u_t)[..., None] * b_t[:, None, :]
                y = jnp.einsum('bdn,bn->bd', h, c_t)
                return (h, y)
            h0 = jnp.zeros((delta.shape[0], DI, N), delta.dtype)
            xs = (delta.swapaxes(0, 1), Bm.swapaxes(0, 1), Cm.swapaxes(0, 1), u.swapaxes(0, 1))
            _, ys = jax.lax.scan(step, h0, xs)
            return ys.swapaxes(0, 1) + u * Dp

        def _mamba(h, in_w, cw, cb, xw, dtw, dtb, A_log, Dp, ow):
            xz = h @ in_w.T
            x, z = jnp.split(xz, 2, axis=-1)
            xp = jnp.pad(x, ((0, 0), (K - 1, 0), (0, 0)))
            Ls = x.shape[1]
            x = sum((cw[:, k] * xp[:, k:k + Ls, :] for k in range(K))) + cb
            x = jax.nn.silu(x)
            dbc = x @ xw.T
            dt, Bm, Cm = (dbc[..., :R], dbc[..., R:R + N], dbc[..., R + N:])
            delta = jax.nn.softplus(dt @ dtw.T + dtb)
            A = -jnp.exp(A_log)
            y = _ssm_scan(delta, Bm, Cm, x, A, Dp)
            y = y * jax.nn.silu(z)
            return y @ ow.T

        def _forward(hidden_states, ln1_w, ln1_b, in_proj_w, conv_w, conv_b, x_proj_w, dt_proj_w, dt_proj_b, A_log, D_param, out_proj_w, block_norm_w, norm_f_w, ln2_w, ln2_b, fc1_w, fc1_b, fc2_w, fc2_b):
            shortcut = hidden_states
            h = _ln(hidden_states, ln1_w, ln1_b)
            residual = None
            for i in range(in_proj_w.shape[0]):
                residual = h if residual is None else h + residual
                hn = _rms(residual, block_norm_w[i])
                h = _mamba(hn, in_proj_w[i], conv_w[i], conv_b[i], x_proj_w[i], dt_proj_w[i], dt_proj_b[i], A_log[i], D_param[i], out_proj_w[i])
            h = _rms(h + residual, norm_f_w)
            h = shortcut + h
            x = _ln(h, ln2_w, ln2_b)
            x = jax.nn.gelu(x @ fc1_w.T + fc1_b)
            x = x @ fc2_w.T + fc2_b
            return h + x
        key = jax.random.key(seed)
        ks = jax.random.split(key, 9)
        s = 0.02
        return {'hidden_states': jax.random.normal(ks[0], (B, L, D), jnp.float32), 'ln1_w': jnp.ones((D,), jnp.float32), 'ln1_b': jnp.zeros((D,), jnp.float32), 'in_proj_w': jax.random.normal(ks[1], (NL, 2 * DI, D), jnp.float32) * s, 'conv_w': jax.random.normal(ks[2], (NL, DI, K), jnp.float32) * 0.3, 'conv_b': jnp.zeros((NL, DI), jnp.float32), 'x_proj_w': jax.random.normal(ks[3], (NL, R + 2 * N, DI), jnp.float32) * s, 'dt_proj_w': jax.random.normal(ks[4], (NL, DI, R), jnp.float32) * s, 'dt_proj_b': jax.random.uniform(ks[5], (NL, DI), jnp.float32, -4.0, -2.0), 'A_log': jnp.tile(jnp.log(jnp.arange(1, N + 1, dtype=jnp.float32)), (NL, DI, 1)), 'D_param': jnp.ones((NL, DI), jnp.float32), 'out_proj_w': jax.random.normal(ks[6], (NL, D, DI), jnp.float32) * s, 'block_norm_w': jnp.ones((NL, D), jnp.float32), 'norm_f_w': jnp.ones((D,), jnp.float32), 'ln2_w': jnp.ones((D,), jnp.float32), 'ln2_b': jnp.zeros((D,), jnp.float32), 'fc1_w': jax.random.normal(ks[7], (H, D), jnp.float32) * s, 'fc1_b': jnp.zeros((H,), jnp.float32), 'fc2_w': jax.random.normal(ks[8], (D, H), jnp.float32) * s, 'fc2_b': jnp.zeros((D,), jnp.float32)}
    _L0_attn_all = _L0_attn_setup()
    _L0_attn_in = {k: v for k, v in _L0_attn_all.items() if k in ('ln1_w', 'ln1_b', 'in_proj_w', 'conv_w', 'conv_b', 'x_proj_w', 'dt_proj_w', 'dt_proj_b', 'A_log', 'D_param', 'out_proj_w', 'block_norm_w', 'norm_f_w', 'ln2_w', 'ln2_b', 'fc1_w', 'fc1_b', 'fc2_w', 'fc2_b')}
    del _L0_attn_all

    def _L0_ffn_setup():
        import jax, jax.numpy as jnp
        import numpy as np
        B, S, D = (8, 1024, 128)
        H = 512
        O = 128
        E = 8
        TOP_K = 1
        key = jax.random.key(seed)
        ks = jax.random.split(key, 8)
        sc = 0.02
        return {'x': jax.random.normal(ks[0], (B, S, D), dtype=jnp.float32), 'Wr': jax.random.normal(ks[1], (D, E), dtype=jnp.float32) * sc, 'br': jnp.zeros((E,), dtype=jnp.float32), 'W1': jax.random.normal(ks[2], (E, D, H), dtype=jnp.float32) * sc, 'b1': jnp.zeros((E, H), dtype=jnp.float32), 'W2': jax.random.normal(ks[3], (E, H, O), dtype=jnp.float32) * sc, 'b2': jnp.zeros((E, O), dtype=jnp.float32)}
    _L0_ffn_all = _L0_ffn_setup()
    _L0_ffn_in = {k: v for k, v in _L0_ffn_all.items() if k in ('Wr', 'br', 'W1', 'b1', 'W2', 'b2')}
    del _L0_ffn_all
    return {'x': x, 'L0_tok_embed_table': _L0_tok_in['embed_table'], 'L0_tok_conv_w': _L0_tok_in['conv_w'], 'L0_tok_gamma': _L0_tok_in['gamma'], 'L0_tok_beta': _L0_tok_in['beta'], 'L0_attn_ln1_w': _L0_attn_in['ln1_w'], 'L0_attn_ln1_b': _L0_attn_in['ln1_b'], 'L0_attn_in_proj_w': _L0_attn_in['in_proj_w'], 'L0_attn_conv_w': _L0_attn_in['conv_w'], 'L0_attn_conv_b': _L0_attn_in['conv_b'], 'L0_attn_x_proj_w': _L0_attn_in['x_proj_w'], 'L0_attn_dt_proj_w': _L0_attn_in['dt_proj_w'], 'L0_attn_dt_proj_b': _L0_attn_in['dt_proj_b'], 'L0_attn_A_log': _L0_attn_in['A_log'], 'L0_attn_D_param': _L0_attn_in['D_param'], 'L0_attn_out_proj_w': _L0_attn_in['out_proj_w'], 'L0_attn_block_norm_w': _L0_attn_in['block_norm_w'], 'L0_attn_norm_f_w': _L0_attn_in['norm_f_w'], 'L0_attn_ln2_w': _L0_attn_in['ln2_w'], 'L0_attn_ln2_b': _L0_attn_in['ln2_b'], 'L0_attn_fc1_w': _L0_attn_in['fc1_w'], 'L0_attn_fc1_b': _L0_attn_in['fc1_b'], 'L0_attn_fc2_w': _L0_attn_in['fc2_w'], 'L0_attn_fc2_b': _L0_attn_in['fc2_b'], 'L0_ffn_Wr': _L0_ffn_in['Wr'], 'L0_ffn_br': _L0_ffn_in['br'], 'L0_ffn_W1': _L0_ffn_in['W1'], 'L0_ffn_b1': _L0_ffn_in['b1'], 'L0_ffn_W2': _L0_ffn_in['W2'], 'L0_ffn_b2': _L0_ffn_in['b2']}

def reference(x, L0_tok_embed_table, L0_tok_conv_w, L0_tok_gamma, L0_tok_beta, L0_attn_ln1_w, L0_attn_ln1_b, L0_attn_in_proj_w, L0_attn_conv_w, L0_attn_conv_b, L0_attn_x_proj_w, L0_attn_dt_proj_w, L0_attn_dt_proj_b, L0_attn_A_log, L0_attn_D_param, L0_attn_out_proj_w, L0_attn_block_norm_w, L0_attn_norm_f_w, L0_attn_ln2_w, L0_attn_ln2_b, L0_attn_fc1_w, L0_attn_fc1_b, L0_attn_fc2_w, L0_attn_fc2_b, L0_ffn_Wr, L0_ffn_br, L0_ffn_W1, L0_ffn_b1, L0_ffn_W2, L0_ffn_b2):
    import jax
    import jax.numpy as jnp

    def _L0_tok_ref(tokens, embed_table, conv_w, gamma, beta):
        import jax, jax.numpy as jnp
        import numpy as np
        EPS = 1e-05
        x = embed_table[tokens]
        B, T, C = x.shape
        K = conv_w.shape[1]
        xp = jnp.pad(x, ((0, 0), (K - 1, 0), (0, 0)))
        out = xp[:, 0:T, :] * conv_w[:, 0]
        for k in range(1, K):
            out = out + xp[:, k:k + T, :] * conv_w[:, k]
        mu = jnp.mean(out, axis=-1, keepdims=True)
        var = jnp.mean(jnp.square(out - mu), axis=-1, keepdims=True)
        y = (out - mu) * jax.lax.rsqrt(var + EPS) * gamma + beta
        return jax.nn.relu(y)

    def _L0_attn_ref(hidden_states, ln1_w, ln1_b, in_proj_w, conv_w, conv_b, x_proj_w, dt_proj_w, dt_proj_b, A_log, D_param, out_proj_w, block_norm_w, norm_f_w, ln2_w, ln2_b, fc1_w, fc1_b, fc2_w, fc2_b):
        import jax, jax.numpy as jnp
        import numpy as np
        B, L, D = (1, 512, 128)
        NL, N, K = (4, 16, 4)
        DI = 2 * D
        R = D // 16
        H = 4 * D

        def _ln(x, w, b, eps=1e-05):
            mu = x.mean(-1, keepdims=True)
            v = ((x - mu) ** 2).mean(-1, keepdims=True)
            return (x - mu) * jax.lax.rsqrt(v + eps) * w + b

        def _rms(x, w, eps=1e-05):
            return x * jax.lax.rsqrt((x * x).mean(-1, keepdims=True) + eps) * w

        def _ssm_scan(delta, Bm, Cm, u, A, Dp):

            def step(h, inp):
                d_t, b_t, c_t, u_t = inp
                dA = jnp.exp(d_t[..., None] * A)
                h = dA * h + (d_t * u_t)[..., None] * b_t[:, None, :]
                y = jnp.einsum('bdn,bn->bd', h, c_t)
                return (h, y)
            h0 = jnp.zeros((delta.shape[0], DI, N), delta.dtype)
            xs = (delta.swapaxes(0, 1), Bm.swapaxes(0, 1), Cm.swapaxes(0, 1), u.swapaxes(0, 1))
            _, ys = jax.lax.scan(step, h0, xs)
            return ys.swapaxes(0, 1) + u * Dp

        def _mamba(h, in_w, cw, cb, xw, dtw, dtb, A_log, Dp, ow):
            xz = h @ in_w.T
            x, z = jnp.split(xz, 2, axis=-1)
            xp = jnp.pad(x, ((0, 0), (K - 1, 0), (0, 0)))
            Ls = x.shape[1]
            x = sum((cw[:, k] * xp[:, k:k + Ls, :] for k in range(K))) + cb
            x = jax.nn.silu(x)
            dbc = x @ xw.T
            dt, Bm, Cm = (dbc[..., :R], dbc[..., R:R + N], dbc[..., R + N:])
            delta = jax.nn.softplus(dt @ dtw.T + dtb)
            A = -jnp.exp(A_log)
            y = _ssm_scan(delta, Bm, Cm, x, A, Dp)
            y = y * jax.nn.silu(z)
            return y @ ow.T

        def _forward(hidden_states, ln1_w, ln1_b, in_proj_w, conv_w, conv_b, x_proj_w, dt_proj_w, dt_proj_b, A_log, D_param, out_proj_w, block_norm_w, norm_f_w, ln2_w, ln2_b, fc1_w, fc1_b, fc2_w, fc2_b):
            shortcut = hidden_states
            h = _ln(hidden_states, ln1_w, ln1_b)
            residual = None
            for i in range(in_proj_w.shape[0]):
                residual = h if residual is None else h + residual
                hn = _rms(residual, block_norm_w[i])
                h = _mamba(hn, in_proj_w[i], conv_w[i], conv_b[i], x_proj_w[i], dt_proj_w[i], dt_proj_b[i], A_log[i], D_param[i], out_proj_w[i])
            h = _rms(h + residual, norm_f_w)
            h = shortcut + h
            x = _ln(h, ln2_w, ln2_b)
            x = jax.nn.gelu(x @ fc1_w.T + fc1_b)
            x = x @ fc2_w.T + fc2_b
            return h + x
        return _forward(hidden_states, ln1_w, ln1_b, in_proj_w, conv_w, conv_b, x_proj_w, dt_proj_w, dt_proj_b, A_log, D_param, out_proj_w, block_norm_w, norm_f_w, ln2_w, ln2_b, fc1_w, fc1_b, fc2_w, fc2_b)

    def _L0_ffn_ref(x, Wr, br, W1, b1, W2, b2):
        import jax, jax.numpy as jnp
        import numpy as np
        B, S, D = (8, 1024, 128)
        H = 512
        O = 128
        E = 8
        TOP_K = 1
        b, s, d = x.shape
        xf = x.reshape(-1, d)
        router_logits = xf @ Wr + br
        topk_logits, topk_idx = jax.lax.top_k(router_logits, TOP_K)
        topk_gates = jax.nn.softmax(topk_logits, axis=1)
        out = jnp.zeros((xf.shape[0], O), dtype=x.dtype)
        for k in range(TOP_K):
            idx_k = topk_idx[:, k]
            gate_k = topk_gates[:, k:k + 1]
            for e in range(E):
                h = jax.nn.relu(xf @ W1[e] + b1[e])
                oe = h @ W2[e] + b2[e]
                mask = (idx_k == e)[:, None]
                out = out + jnp.where(mask, gate_k * oe, 0.0)
        return out.reshape(b, s, O)
    h = _L0_tok_ref(x, L0_tok_embed_table, L0_tok_conv_w, L0_tok_gamma, L0_tok_beta)
    h = h + _L0_attn_ref(_layernorm(h, axis=-1), L0_attn_ln1_w, L0_attn_ln1_b, L0_attn_in_proj_w, L0_attn_conv_w, L0_attn_conv_b, L0_attn_x_proj_w, L0_attn_dt_proj_w, L0_attn_dt_proj_b, L0_attn_A_log, L0_attn_D_param, L0_attn_out_proj_w, L0_attn_block_norm_w, L0_attn_norm_f_w, L0_attn_ln2_w, L0_attn_ln2_b, L0_attn_fc1_w, L0_attn_fc1_b, L0_attn_fc2_w, L0_attn_fc2_b)
    h = h + _L0_ffn_ref(_layernorm(h, axis=-1), L0_ffn_Wr, L0_ffn_br, L0_ffn_W1, L0_ffn_b1, L0_ffn_W2, L0_ffn_b2)
    return h

_drawn_inputs = setup_inputs


def setup_inputs(seed=0):
    import zlib

    import numpy as np

    out = dict(_drawn_inputs(seed))
    spreads = {'L0_tok_gamma': (1.0, 0.2),
     'L0_tok_beta': (0.0, 0.1),
     'L0_attn_ln1_w': (1.0, 0.2),
     'L0_attn_ln1_b': (0.0, 0.1),
     'L0_attn_conv_b': (0.0, 0.8),
     'L0_attn_D_param': (1.0, 0.6),
     'L0_attn_block_norm_w': (1.0, 0.6),
     'L0_attn_norm_f_w': (1.0, 0.2),
     'L0_attn_ln2_w': (1.0, 0.6),
     'L0_attn_ln2_b': (0.0, 0.8),
     'L0_attn_fc1_b': (0.0, 0.786),
     'L0_attn_fc2_b': (0.0, 0.1),
     'L0_ffn_br': (0.0, 0.1),
     'L0_ffn_b1': (0.0, 0.708),
     'L0_ffn_b2': (0.0, 0.1)}
    factors = {'L0_attn_in_proj_w': 8.0,
     'L0_attn_conv_w': 8.0,
     'L0_attn_x_proj_w': 8.0,
     'L0_attn_dt_proj_w': 8.0,
     'L0_attn_dt_proj_b': 8.0,
     'L0_attn_A_log': 8.0,
     'L0_attn_out_proj_w': 8.0}
    for name, (base, spread) in spreads.items():
        noise = np.random.default_rng([zlib.crc32(name.encode()), seed]).standard_normal(out[name].shape)
        drawn = base * np.exp(spread * noise) if base else spread * noise
        out[name] = jnp.asarray(drawn.astype(out[name].dtype))
    for name, factor in factors.items():
        out[name] = (out[name] * factor).astype(out[name].dtype)
    return out
```

```python
from contextlib import ExitStack

import concourse.bass as bass
import numpy as np
from concourse import mybir

F32 = mybir.dt.float32
BF16 = mybir.dt.bfloat16
U32 = mybir.dt.uint32
ALU = mybir.AluOpType
ACT = mybir.ActivationFunctionType
AX = mybir.AxisListType.X
ds = bass.ds

P = 128
TC = 512
BATCH = 2
TOK = 4096
NCH = TOK // TC
CPB = NCH // BATCH
TT = TC // P
NL = 4
HV = 2
NS = 16
KC = 4
KT = 3
R = 8
DI = HV * P
UN = HV * NS
ITEMS = NL * NCH
E = 8
HB = 4
EPS = 1e-5
SMALL = 2.0 ** -12
SQRT_HALF = 0.5 ** 0.5
LOG_EXP = "natural_log_exp_and_others"

VEC = {}
_at = 0
for _name, _n in (("tok_w", KT), ("tok_gamma", 1), ("tok_beta", 1), ("ln1_w", 1), ("ln1_b", 1), ("norm_f", 1),
                  ("ln2_w", 1), ("ln2_b", 1), ("fc2_b", 1), ("block_norm", NL), ("fc1_b", HB),
                  ("conv_b", NL * HV), ("dt_b", NL * HV), ("D", NL * HV), ("b1", E * HB),
                  ("A", NL * HV * NS)):
    VEC[_name] = _at
    _at += _n
NVEC = _at
CON = {}
_at = 0
for _name, _n in (("ident", P), ("mean", P), ("center", P), ("pick", 2 * NS), ("keep", ITEMS), ("eps", 1), ("one", 1),
                  ("rank", E)):
    CON[_name] = _at
    _at += _n
NCON = _at

W_TAP, W_Z, W_X, W_DT = 0, KC * DI, KC * DI + DI, KC * DI + 2 * DI
NW = W_DT + DI

ND, NP = 4, 8
NB = 4
LEAD_B, LEAD_A, LAG = 3, 3, 4

CF = 11
FILLS = {0: [("C", 11), ("C", 12)], 1: [("C", 13)], 2: [("C", 14)], 3: [("C", 15)], 6: [("z", 0)], 7: [("z", 1)],
         10: [("x", 0)], 13: [("x", 1)], 16: [("xd", 0)], 18: [("dt", 0)], 25: [("dt", 1)], 28: [("stat", 0)]}
for _n in range(CF):
    FILLS.setdefault(21 + _n, []).append(("C", _n))
BANK_USES = [use for slot in sorted(FILLS) for use in FILLS[slot]]
BANK_AT = {use: k for k, use in enumerate(BANK_USES)}
NBU = len(BANK_USES)
FIRST_USES = ([("stat", -1)] + [(what, h) for what, h in BANK_USES if what in ("z", "x", "xd", "dt")]
              + [("C", n) for n in range(CF)] + [("stat", 0)])
FIRST_AT = {use: k for k, use in enumerate(FIRST_USES)}
LAST_AT = {use: k for k, use in enumerate([use for use in BANK_USES if use[0] == "C" and use[1] >= CF])}


def rounds(eng, one_round):
    one_round(0)
    with eng.Fori(1, CPB) as k:
        one_round(k)


def later(k):
    return not isinstance(k, int) or k > 0


def lm_tower(nc, tok, embed, vec, con, win_x, win_z, conv_w, xproj, dtw, outw, fc1, fc2, wr, br, w1, w2, b2, out):
    ctx = ExitStack()
    with ctx:
        def sb(name, shape, dt=F32):
            return ctx.enter_context(nc.sbuf_tensor(name, shape, dt))

        def sem(name):
            return ctx.enter_context(nc.semaphore(name))

        psum = ctx.enter_context(nc.psum_tensor("banks", [P, 8, TC], F32))

        def bank(b):
            return psum[:, b, :]

        h0_d = nc.dram_tensor("h0_scratch", [NCH, P, TC], F32, kind="Internal").ap()
        s_d = nc.dram_tensor("s_scratch", [NCH, P, TC], F32, kind="Internal").ap()
        w_d = nc.dram_tensor("front_scratch", [NL, P, NW], F32, kind="Internal").ap()

        V = sb("V", [P, NVEC])
        Cn = sb("Cn", [P, NCON])
        r = sb("r", [P, NCH, TC])
        ident = Cn[:, CON["ident"]:CON["ident"] + P]
        meanw = Cn[:, CON["mean"]:CON["mean"] + P]
        center = Cn[:, CON["center"]:CON["center"] + P]
        eps = Cn[:, CON["eps"]:CON["eps"] + 1]
        one = Cn[:, CON["one"]:CON["one"] + 1]

        def v(name, k=0):
            return V[:, VEC[name] + k:VEC[name] + k + 1]

        h_ring = sb("h_ring", [P, NS, TC])
        c_all = sb("c_all", [P, NS, TC])
        decay = sb("decay", [P, ND, TC])
        prod = sb("prod", [P, NP, TC])
        delta = sb("delta", [P, 2, HV, TC])
        du = sb("du", [P, 2, HV, TC])
        xs = sb("xs", [P, 2, HV, TC])
        zs = sb("zs", [P, 2, HV, TC])
        stack = sb("stack", [96, 2, TC], BF16)
        pick = sb("pick", [96, 2 * NS, P], BF16)
        wf = sb("wf", [P, NW])
        wo = sb("wo", [P, HV, P])
        hn = sb("hn", [P, KC - 1 + TC])
        h_init = sb("h_init", [P, HV, NS])
        sq = sb("sq", [P, TC])
        lnv = sb("lnv", [P, TC])
        rstd = sb("rstd", [P, TC])
        xd = sb("xd", [P, TC])
        rest = sb("rest", [96, TC])
        mid = sb("mid", [96, TC], BF16)
        ea = sb("ea", [P, HV, TC])
        pos = sb("pos", [P, HV, TC])
        w1p = sb("w1p", [P, HV, TC])
        lg = sb("lg", [P, HV, TC])
        small = sb("small", [P, HV, TC])
        small_pos = sb("small_pos", [P, HV, TC])
        yt = sb("yt", [P, TC])
        yz = sb("yz", [P, HV, TC])

        loaded = sem("loaded")
        gathered = [sem(f"gathered{s}") for s in range(2)]
        names0 = ["turned", "emb", "tap0", "tap1", "tap2", "cen", "sqd", "var", "logd", "rst", "scl", "h0_made",
                  "h0_kept", "s_kept", "hist"]
        q0 = {n: [sem(f"{n}_s{s}") for s in range(2)] for n in names0}
        folded = sem("folded")
        picked = sem("picked")
        neg_a = sem("neg_a")
        w_zero = sem("w_zero")
        w_in = sem("w_in")
        w_out = sem("w_out")
        r_ready = sem("r_ready")

        g_tok = h_ring[:, 0:4, :].rearrange("p (s t) c -> p s (t c)", s=2)[:, :, 0:TT * P]
        idx = sb("idx", [P, TOK // P], U32)
        emb = [h_ring[:, 4 + 2 * s:6 + 2 * s, :].rearrange("p a b -> p (a b)")[:, 0:KT - 1 + TC] for s in range(2)]
        ta = [h_ring[:, 8 + s, :] for s in range(2)]
        tb = [h_ring[:, 10 + s, :] for s in range(2)]
        s_sq = [h_ring[:, 12 + s, :] for s in range(2)]
        s_rs = [h_ring[:, 14 + s, :] for s in range(2)]
        s_ln = [decay[:, s, :] for s in range(2)]
        s_y = [decay[:, 2 + s, :] for s in range(2)]
        s_h0 = [prod[:, s, :] for s in range(2)]
        s_s = [prod[:, 2 + s, :] for s in range(2)]
        wx_all = c_all[:, :, :].rearrange("p a b -> p (a b)")[:, 0:NL * DI].rearrange("p (l d) -> p l d", l=NL)
        cw_all = c_all[:, :, :].rearrange("p a b -> p (a b)")[:, NL * DI:NL * DI * (1 + KC)]
        cw_all = cw_all.rearrange("p (l k d) -> p l k d", l=NL, k=KC)

        with nc.Block() as block:

            @block.sync
            def _(sp):
                sp.dma_start(V[:, :], vec).then_inc(loaded, 16)
                sp.dma_start(Cn[:, :], con).then_inc(loaded, 16)
                sp.dma_start(idx[:, :], tok).then_inc(w_in, 16)
                sp.dma_start(wx_all, win_x).then_inc(folded, 16)
                sp.dma_start(cw_all, conv_w.partition_broadcast(P)).then_inc(folded, 16)
                for l in range(NL):
                    sp.wait_ge(w_zero, l + 1)
                    sp.dma_start(wf[:, W_Z:W_Z + DI], win_z[:, l, :]).then_inc(w_out, 16)
                    for h in range(HV):
                        for rep in range(3):
                            sp.dma_start(wf[:, W_X + h * P + 32 * rep:W_X + h * P + 32 * rep + 32],
                                         xproj[l, :, h, R:R + 2 * NS]).then_inc(w_out, 16)
                        sp.dma_start(wf[:, W_X + h * P + 96:W_X + h * P + 96 + R], xproj[l, :, h, 0:R]).then_inc(w_out, 16)
                    sp.dma_start(wf[96:96 + R, W_DT:W_DT + DI], dtw[l, :, :]).then_inc(w_out, 16)
                    sp.wait_ge(w_out, (11 * l + 10) * 16)
                    sp.wait_ge(picked, l + 2)
                    sp.dma_start(w_d[l, :, :], wf[:, :]).then_inc(w_out, 16)
                    sp.wait_ge(w_out, (11 * l + 11) * 16)
                    sp.sem_inc(neg_a, 1)
                def one_round(k):
                    for s in range(2):
                        sp.wait_ge(q0["h0_made"][s], k + 1)
                        sp.dma_start(h0_d[k + s * CPB, :, :], s_h0[s])\
                          .then_inc(q0["h0_kept"][s], 16)
                        sp.wait_ge(q0["scl"][s], 3 * k + 2)
                        sp.dma_start(s_d[k + s * CPB, :, :], s_s[s])\
                          .then_inc(q0["s_kept"][s], 16)
                rounds(sp, one_round)
                for s in range(2):
                    sp.wait_ge(q0["h0_kept"][s], 16 * CPB)
                    sp.wait_ge(q0["s_kept"][s], 16 * CPB)

            @block.gpsimd
            def _(pool):
                pool.memset(hn[:, :], 0.0)
                pool.memset(h_init[:, :, :], 0.0)
                pool.wait_ge(w_in, 16)
                for k in range(CPB):
                    for s in range(2):
                        if k:
                            pool.wait_ge(q0["turned"][s], k)
                        for t in range(TT):
                            col = (k + s * CPB) * TT + t
                            pool.indirect_dma_start(
                                out=g_tok[:, s, t * P:(t + 1) * P], out_offset=None, in_=embed,
                                in_offset=bass.IndirectOffsetOnAxis(ap=idx[:, col:col + 1], axis=0))\
                                .then_inc(gathered[s], 16)

            @block.tensor
            def _(pe):
                pe.wait_ge(loaded, 32)
                def one_round(k):
                    for s in range(2):
                        pe.wait_ge(gathered[s], (k + 1) * 16 * TT)
                        for t in range(TT):
                            last = pe.transpose(bank(4 * s)[:, t * P:(t + 1) * P], g_tok[:, s, t * P:(t + 1) * P], ident)
                        last.then_inc(q0["turned"][s], 1)
                    for m, (src, ready, count) in enumerate(((ta, "tap2", k + 1), (s_h0, "h0_made", k + 1),
                                                             (s_s, "scl", 3 * k + 2)), 1):
                        for s in range(2):
                            pe.wait_ge(q0[ready][s], count)
                            pe.matmul(bank(4 * s + 1), center, src[s], start=True, stop=True)\
                              .then_inc(q0["cen"][s], 1)
                        for s in range(2):
                            pe.wait_ge(q0["sqd"][s], 3 * k + m)
                            pe.matmul(bank(4 * s + 2), meanw, s_sq[s], start=True, stop=True)\
                              .then_inc(q0["var"][s], 1)
                rounds(pe, one_round)

            @block.scalar
            def _(act):
                act.preload_act_table_set(LOG_EXP)
                act.wait_ge(loaded, 32)
                a_all = V[:, VEC["A"]:VEC["A"] + NL * HV * NS]
                act.activation(a_all, a_all, ACT.Exp).then_inc(picked, 1)
                def one_round(k):
                    for s in range(2):
                        act.wait_ge(q0["turned"][s], k + 1)
                        act.wait_ge(q0["hist"][s], k + 1)
                        act.activation(emb[s][:, KT - 1:KT - 1 + TC], bank(4 * s), ACT.Copy).then_inc(q0["emb"][s], 1)
                    for m in (1, 2, 3):
                        for s in range(2):
                            act.wait_ge(q0["cen"][s], 3 * k + m)
                            act.activation(s_sq[s], bank(4 * s + 1), ACT.Square).then_inc(q0["sqd"][s], 1)
                        for s in range(2):
                            act.wait_ge(q0["var"][s], 3 * k + m)
                            act.activation(s_ln[s], bank(4 * s + 2), ACT.Ln, bias=eps).then_inc(q0["logd"][s], 1)
                            act.wait_ge(q0["logd"][s], 3 * k + m)
                            act.activation(s_rs[s], s_ln[s], ACT.Exp, scale=-0.5).then_inc(q0["rst"][s], 1)
                        if m == 1:
                            for s in range(2):
                                act.wait_ge(q0["scl"][s], 3 * k + 1)
                                if later(k):
                                    act.wait_ge(q0["h0_kept"][s], 16 * k)
                                act.activation(s_h0[s], s_y[s], ACT.Relu, scale=v("tok_gamma"), bias=v("tok_beta"))\
                                   .then_inc(q0["h0_made"][s], 1)
                        if m == 3:
                            for s in range(2):
                                act.wait_ge(q0["scl"][s], 3 * k + 3)
                                act.activation(r[:, k + s * CPB, :], s_y[s],
                                               ACT.Identity, scale=v("ln1_w"), bias=v("ln1_b")).then_inc(r_ready, 1)
                rounds(act, one_round)

            @block.vector
            def _(dve):
                dve.wait_ge(loaded, 32)
                pk = Cn[0:96, CON["pick"]:CON["pick"] + 2 * NS]
                dve.tensor_copy(pick[:, :, :], pk.unsqueeze(2).to_broadcast([96, 2 * NS, P]))
                dve.memset(wf[:, W_X:NW], 0.0).then_inc(w_zero, 1)
                dve.wait_ge(picked, 1)
                a_all = V[:, VEC["A"]:VEC["A"] + NL * HV * NS]
                dve.tensor_scalar(a_all, a_all, -1.0, None, ALU.mult)
                dve.wait_ge(folded, 32)
                for l in range(NL):
                    if l:
                        dve.wait_ge(neg_a, l)
                    src = wx_all[:, l, :].unsqueeze(1).to_broadcast([P, KC, DI])
                    dve.tensor_tensor(wf[:, 0:KC * DI].rearrange("p (k d) -> p k d", k=KC), src, cw_all[:, l, :, :],
                                      ALU.mult).then_inc(picked, 1)
                    if l + 1 < NL:
                        dve.wait_ge(neg_a, l + 1)
                        dve.sem_inc(w_zero, 1)
                for s in range(2):
                    dve.memset(emb[s][:, TC:TC + KT - 1], 0.0).then_inc(q0["tap0"][s], 1)
                    dve.wait_ge(q0["tap0"][s], 1)
                def one_round(k):
                    for s in range(2):
                        if later(k):
                            if later(k):
                                dve.wait_ge(q0["tap2"][s], k)
                        dve.tensor_copy(emb[s][:, 0:KT - 1], emb[s][:, TC:TC + KT - 1]).then_inc(q0["hist"][s], 1)
                    for s in range(2):
                        dve.wait_ge(q0["emb"][s], k + 1)
                        dve.wait_ge(q0["hist"][s], k + 1)
                        dve.tensor_scalar(ta[s], emb[s][:, 0:TC], v("tok_w", 0), None, ALU.mult)\
                           .then_inc(q0["tap0"][s], 1)
                        dve.wait_ge(q0["tap0"][s], k + 2)
                        dve.scalar_tensor_tensor(tb[s], emb[s][:, 1:1 + TC], v("tok_w", 1), ta[s], ALU.mult, ALU.add)\
                           .then_inc(q0["tap1"][s], 1)
                        dve.wait_ge(q0["tap1"][s], k + 1)
                        dve.scalar_tensor_tensor(ta[s], emb[s][:, 2:2 + TC], v("tok_w", 2), tb[s], ALU.mult, ALU.add)\
                           .then_inc(q0["tap2"][s], 1)
                    for m in (1, 2, 3):
                        for s in range(2):
                            dve.wait_ge(q0["rst"][s], 3 * k + m)
                            if m == 2:
                                if later(k):
                                    dve.wait_ge(q0["s_kept"][s], 16 * k)
                            dve.tensor_tensor(s_s[s] if m == 2 else s_y[s], bank(4 * s + 1), s_rs[s], ALU.mult)\
                               .then_inc(q0["scl"][s], 1)
                rounds(dve, one_round)

        front_in = sem("front_in")
        out_in = sem("out_in")
        squared = sem("squared")
        logged = sem("logged")
        rstd_in = sem("rstd_in")
        hist_in = sem("hist_in")
        hn_in = sem("hn_in")
        z_in = sem("z_in")
        xs_in = sem("xs_in")
        xd_in = sem("xd_in")
        part_in = sem("part_in")
        stack_in = sem("stack_in")
        abs_in = sem("abs_in")
        exp_in = sem("exp_in")
        plus_in = sem("plus_in")
        ln_in = sem("ln_in")
        half_sq = sem("half_sq")
        small_in = sem("small_in")
        err_in = sem("err_in")
        base_in = sem("base_in")
        diff_in = sem("diff_in")
        chosen = sem("chosen")
        delta_in = sem("delta_in")
        du_in = sem("du_in")
        bank_full = sem("bank_full")
        bank_free = sem("bank_free")
        b_full = sem("b_full")
        decay_in = sem("decay_in")
        c_in = sem("c_in")
        drive_in = sem("drive_in")
        scanned = sem("scanned")
        kept = sem("kept")
        prod_in = sem("prod_in")
        prod_used = sem("prod_used")
        yt_in = sem("yt_in")
        yz_in = sem("yz_in")
        o_full = sem("o_full")

        def col(t, k):
            return t[:, ds(k, 1)] if not isinstance(k, int) else t[:, k:k + 1]

        def par(t, i, h):
            return t[:, i % 2, h, :]

        def par2(t, i):
            return t[:, i % 2, :, :]

        def chunk(i):
            return r[:, i % NCH, :]

        def place(i, use):
            if isinstance(i, int) and i in (-1, ITEMS - 1):
                return (FIRST_AT if i < 0 else LAST_AT)[use]
            return BANK_AT[use]

        def fill(i, use):
            if isinstance(i, int) and i < 0:
                return place(i, use)
            return NBU * i + len(FIRST_USES) + place(i, use)

        def shared(i, use):
            return bank(6 + place(i, use) % 2)

        Y, BB = (0, 1), (2, 3, 4, 5)

        with nc.Block() as block:

            @block.sync
            def _(sp):
                def load(j):
                    l = j // NCH
                    if not isinstance(j, int) or j > 0:
                        sp.wait_ge(bank_full, fill(j - 2, ("dt", 1)) + 1)
                    src = w_d[l, :, :]
                    sp.dma_start(wf[:, :], src).then_inc(front_in, 16)

                def load_out(j):
                    l = j // NCH
                    if not isinstance(j, int) or j > 0:
                        sp.wait_ge(o_full, j)
                    src = outw[l, :, :]
                    sp.dma_start(wo[:, :, :].rearrange("p h n -> p (h n)"), src).then_inc(out_in, 16)

                load(0)
                load_out(0)
                load(1)
                with sp.Fori(1, ITEMS - 1) as j:
                    load(j + 1)
                    load_out(j)
                load_out(ITEMS - 1)

            @block.tensor
            def _(pe):
                def take(i, use):
                    f = fill(i, use)
                    if not isinstance(f, int) or f >= 2:
                        pe.wait_ge(bank_free, f - 1)

                def bring(i, u):
                    g = UN * i + u
                    h, n = (u % UN) // NS, u % NS
                    ii = i + u // UN
                    if u % UN == 0:
                        pe.wait_ge(stack_in, ii + 1)
                    if not isinstance(g, int) or g >= NB:
                        pe.wait_ge(scanned, g - NB + 1)
                    pe.matmul(bank(BB[u % NB]), pick[:, n, :], par_s(ii), start=True, stop=True).then_inc(b_full, 1)

                def par_s(i):
                    return stack[:, i % 2, :]

                def bring_c(i, j, n, use):
                    take(i, use)
                    if n == 0:
                        pe.wait_ge(stack_in, j + 1)
                    pe.matmul(shared(i, use), pick[:, NS + n, :], par_s(j), start=True, stop=True)\
                      .then_inc(bank_full, 1)

                def add_up(i, u):
                    g, h, n = UN * i + u, u // NS, u % NS
                    if n == 0 and h == 0 and (not isinstance(i, int) or i > 0):
                        pe.wait_ge(yt_in, 2 * i - 1)
                    if n == 0 and h == 1 and (not isinstance(i, int) or i > 0):
                        pe.wait_ge(r_ready, NCH + i)
                    pe.wait_ge(prod_in, g + 1)
                    pe.matmul(bank(Y[h]), ident, prod[:, u % NP, :], start=(n == 0), stop=(n == NS - 1)).then_inc(prod_used, 1)

                def project(i):
                    pe.wait_ge(yz_in, 2 * i + 2)
                    pe.wait_ge(out_in, 16 * (i + 1))
                    for h in range(HV):
                        mm = pe.matmul(bank(Y[1]), wo[:, h, :], yz[:, h, :], start=(h == 0), stop=(h == HV - 1))
                    mm.then_inc(o_full, 1)

                def front(i, step):
                    j = i + 1
                    what, h = step[0], step[1]
                    if what == "stat":
                        take(i, step)
                        pe.wait_ge(squared, j + h + 2)
                        pe.matmul(shared(i, step), meanw, sq[:, :], start=True, stop=True).then_inc(bank_full, 1)
                    elif what == "z":
                        take(i, ("z", h))
                        if h == 0:
                            pe.wait_ge(hn_in, j + 1)
                            pe.wait_ge(front_in, 16 * (j + 1))
                        pe.matmul(shared(i, ("z", h)), wf[:, W_Z + h * P:W_Z + h * P + P], hn[:, KC - 1:KC - 1 + TC],
                                  start=True, stop=True).then_inc(bank_full, 1)
                    elif what == "x":
                        k = step[2]
                        if k == 0:
                            take(i, ("x", h))
                        o = W_TAP + k * DI + h * P
                        mm = pe.matmul(shared(i, ("x", h)), wf[:, o:o + P], hn[:, k:k + TC],
                                       start=(k == 0), stop=(k == KC - 1))
                        if k == KC - 1:
                            mm.then_inc(bank_full, 1)
                    elif what == "xd":
                        if h == 0:
                            take(i, ("xd", 0))
                            pe.wait_ge(xs_in, 2 * j + 2)
                        mm = pe.matmul(shared(i, ("xd", 0)), wf[:, W_X + h * P:W_X + h * P + P], par(xs, j, h),
                                       start=(h == 0), stop=(h == HV - 1))
                        if h == HV - 1:
                            mm.then_inc(bank_full, 1)
                    elif what == "dt":
                        take(i, ("dt", h))
                        if h == 0:
                            pe.wait_ge(xd_in, j + 1)
                        pe.matmul(shared(i, ("dt", h)), wf[:, W_DT + h * P:W_DT + h * P + P], xd[:, :],
                                  start=True, stop=True).then_inc(bank_full, 1)

                FRONT = {6: [("z", 0)], 7: [("z", 1)], 15: [("xd", 0)], 16: [("xd", 1)], 18: [("dt", 0)],
                         25: [("dt", 1)], 28: [("stat", 0)]}
                for h in range(HV):
                    for k, slot in enumerate((8, 9, 10, 10)):
                        FRONT.setdefault(slot + 3 * h, []).append(("x", h, k))

                def body(i, first, last):
                    for u in range(UN):
                        w = u - LAG
                        if w >= 0:
                            add_up(i, w)
                        elif not first:
                            add_up(i - 1, w + UN)
                        if u + LEAD_B < UN or not last:
                            bring(i, u + LEAD_B)
                        if not last:
                            for step in FRONT.get(u, []):
                                front(i, step)
                        for use in FILLS.get(u, []):
                            if use[0] == "C" and (use[1] >= CF or not last):
                                bring_c(i, i if use[1] >= CF else i + 1, use[1], use)
                        if u == 12 and not first:
                            project(i - 1)

                front(-1, ("stat", -1))
                for slot in sorted(FRONT):
                    for step in FRONT[slot]:
                        if step[0] != "stat":
                            front(-1, step)
                for n in range(CF):
                    bring_c(-1, 0, n, ("C", n))
                front(-1, ("stat", 0))
                for u in range(LEAD_B):
                    bring(0, u)
                body(0, True, False)
                with pe.Fori(1, ITEMS - 1) as i:
                    body(i, False, False)
                body(ITEMS - 1, False, True)
                for u in range(UN - LAG, UN):
                    add_up(ITEMS - 1, u)
                project(ITEMS - 1)

            @block.scalar
            def _(act):
                def decays(i, u):
                    g, h, n = UN * i + u, (u % UN) // NS, u % NS
                    ii = i + u // UN
                    if n == 0:
                        act.wait_ge(delta_in, HV * ii + h + 1)
                    if not isinstance(g, int) or g >= ND:
                        act.wait_ge(scanned, g - ND + 1)
                    act.activation(decay[:, u % ND, :], par(delta, ii, h), ACT.Exp,
                                   scale=col(V, VEC["A"] + (ii // NCH) * UN + h * NS + n)).then_inc(decay_in, 1)

                def copy_c(i, j, n, use):
                    act.wait_ge(bank_full, fill(i, use) + 1)
                    if not isinstance(j, int) or j > 0:
                        act.wait_ge(prod_in, UN * (j - 1) + NS + n + 1)
                    act.activation(c_all[:, n, :], shared(i, use), ACT.Copy).then_inc(c_in, 1)
                    act.wait_ge(c_in, NS * j + n + 1)
                    act.sem_inc(bank_free, 1)

                def front(i, step):
                    what, h = step
                    j = i + 1
                    l = j // NCH
                    if what == "square":
                        act.wait_ge(r_ready, j + h + 2)
                        act.activation(sq[:, :], chunk(j + h + 1), ACT.Square).then_inc(squared, 1)
                    elif what == "stat":
                        act.wait_ge(bank_full, fill(i, step) + 1)
                        act.activation(lnv[:, :], shared(i, step), ACT.Ln, bias=eps).then_inc(bank_free, 1)
                        act.wait_ge(bank_free, fill(i, step) + 1)
                        act.activation(rstd[:, :], lnv[:, :], ACT.Exp, scale=-0.5).then_inc(rstd_in, 1)
                    elif what == "z":
                        if h == 0 and (not isinstance(j, int) or j > 1):
                            act.wait_ge(yz_in, 2 * j - 2)
                        act.wait_ge(bank_full, fill(i, ("z", h)) + 1)
                        act.activation(par(zs, j, h), shared(i, ("z", h)), ACT.Copy).then_inc(bank_free, 1)
                    elif what == "silu":
                        for h in range(HV):
                            act.wait_ge(bank_full, fill(i, ("x", h)) + 1)
                            act.activation(par(xs, j, h), shared(i, ("x", h)), ACT.Silu,
                                           bias=col(V, VEC["conv_b"] + l * HV + h)).then_inc(xs_in, 1)
                            act.wait_ge(xs_in, 2 * j + h + 1)
                            act.sem_inc(bank_free, 1)
                        act.activation(par2(zs, j), par2(zs, j), ACT.Silu).then_inc(z_in, 1)
                        act.preload_act_table_set(LOG_EXP)
                    elif what == "xd":
                        act.wait_ge(bank_full, fill(i, ("xd", 0)) + 1)
                        act.activation(xd[:, :], shared(i, ("xd", 0)), ACT.Copy).then_inc(xd_in, 1)
                        act.wait_ge(xd_in, j + 1)
                        act.sem_inc(bank_free, 1)
                    elif what == "dt":
                        act.wait_ge(bank_full, fill(i, ("dt", h)) + 1)
                        if not isinstance(j, int) or j > 0:
                            act.wait_ge(delta_in, HV * (j - 1) + h + 1)
                        dtb = col(V, VEC["dt_b"] + l * HV + h)
                        act.activation(ea[:, h, :], shared(i, ("dt", h)), ACT.Abs, bias=dtb).then_inc(abs_in, 1)
                        act.activation(pos[:, h, :], shared(i, ("dt", h)), ACT.Relu, bias=dtb).then_inc(bank_free, 1)
                    elif what == "exp":
                        act.wait_ge(abs_in, HV * j + h + 1)
                        act.activation(ea[:, h, :], ea[:, h, :], ACT.Exp, scale=-1.0).then_inc(exp_in, 1)
                        act.wait_ge(exp_in, HV * j + h + 1)
                        act.activation(small[:, h, :], ea[:, h, :], ACT.Square, scale=SQRT_HALF).then_inc(half_sq, 1)
                    elif what == "ln":
                        act.wait_ge(plus_in, HV * j + h + 1)
                        act.activation(lg[:, h, :], w1p[:, h, :], ACT.Ln).then_inc(ln_in, 1)

                FRONT = {14: [("silu", 0)], 17: [("xd", 0)], 19: [("dt", 0)], 20: [("exp", 0)], 22: [("ln", 0)],
                         26: [("dt", 1)], 27: [("exp", 1), ("square", 0)], 29: [("ln", 1)]}

                def body(i, first, last):
                    for u in range(UN):
                        if u + LEAD_A < UN or not last:
                            decays(i, u + LEAD_A)
                        if u == 0 and not first:
                            copy_c(i - 1, i, CF - 1, ("C", CF - 1))
                        for use in FILLS.get(u - 1, []):
                            if use[0] == "C" and (use[1] >= CF or not last):
                                copy_c(i, i if use[1] >= CF else i + 1, use[1], use)
                            elif use[0] in ("stat", "z", "dt") and use != ("dt", 0) and not last:
                                front(i, use)
                        if not last:
                            for step in FRONT.get(u, []):
                                if step != ("dt", 1):
                                    front(i, step)

                act.preload_act_table_set(LOG_EXP)
                front(-1, ("square", -1))
                front(-1, ("stat", -1))
                for h in range(HV):
                    front(-1, ("z", h))
                front(-1, ("silu", 0))
                front(-1, ("xd", 0))
                for h in range(HV):
                    front(-1, ("dt", h))
                for h in range(HV):
                    front(-1, ("exp", h))
                for h in range(HV):
                    front(-1, ("ln", h))
                front(-1, ("square", 0))
                for n in range(CF):
                    copy_c(-1, 0, n, ("C", n))
                front(-1, ("stat", 0))
                for u in range(LEAD_A):
                    decays(0, u)
                body(0, True, False)
                with act.Fori(1, ITEMS - 1) as i:
                    body(i, False, False)
                body(ITEMS - 1, False, True)

            @block.vector
            def _(dve):
                def drive(i, u):
                    g, h = UN * i + u, (u % UN) // NS
                    ii = i + u // UN
                    if u % NS == 0:
                        dve.wait_ge(du_in, HV * ii + h + 1)
                    dve.wait_ge(b_full, g + 1)
                    dve.tensor_tensor(bank(BB[u % NB]), par(du, ii, h), bank(BB[u % NB]), ALU.mult).then_inc(drive_in, 1)

                def scan(i, u, keeps):
                    g, h, n = UN * i + u, u // NS, u % NS
                    dve.wait_ge(decay_in, g + 1)
                    dve.wait_ge(drive_in, g + 1)
                    if not isinstance(g, int) or g >= NS:
                        dve.wait_ge(prod_in, g - NS + 1)
                    if n == 0 and (not isinstance(g, int) or g > 0):
                        dve.wait_ge(kept, 2 * i + h if h == 0 or keeps else 2 * i)
                    dve.tensor_tensor_scan(h_ring[:, n, :], decay[:, u % ND, :], bank(BB[u % NB]),
                                           h_init[:, h, n:n + 1], ALU.mult, ALU.add).then_inc(scanned, 1)

                def keep(i, h):
                    j = i + 1
                    dve.wait_ge(scanned, UN * i + NS * (h + 1))
                    dve.tensor_scalar(h_init[:, h, :], h_ring[:, :, TC - 1:TC].rearrange("p n a -> p (n a)"),
                                      col(Cn, CON["keep"] + j), None, ALU.mult).then_inc(kept, 1)

                def gate(i, h):
                    dve.wait_ge(prod_used, UN * i + NS * (h + 1))
                    dve.scalar_tensor_tensor(yt[:, :], par(xs, i, h), col(V, VEC["D"] + (i // NCH) * HV + h),
                                             bank(Y[h]), ALU.mult, ALU.add).then_inc(yt_in, 1)
                    dve.wait_ge(yt_in, 2 * i + h + 1)
                    if h == 0 and (not isinstance(i, int) or i > 0):
                        dve.wait_ge(o_full, i)
                    dve.tensor_tensor(yz[:, h, :], yt[:, :], par(zs, i, h), ALU.mult).then_inc(yz_in, 1)

                def residual(i):
                    dve.wait_ge(o_full, i + 1)
                    dve.tensor_tensor(chunk(i), chunk(i), bank(Y[1]), ALU.add).then_inc(r_ready, 1)

                def front(i, step, h=0):
                    j = i + 1
                    l = j // NCH
                    if step == "hn":
                        if not isinstance(j, int) or j > 0:
                            dve.wait_ge(bank_full, fill(i - 1, ("x", 1)) + 1)
                        dve.tensor_scalar(hn[:, 0:KC - 1], hn[:, TC:TC + KC - 1], col(Cn, CON["keep"] + j), None,
                                          ALU.mult).then_inc(hist_in, 1)
                        dve.wait_ge(hist_in, j + 1)
                        dve.wait_ge(rstd_in, j + 1)
                        dve.scalar_tensor_tensor(hn[:, KC - 1:KC - 1 + TC], chunk(j), col(V, VEC["block_norm"] + l),
                                                 rstd[:, :], ALU.mult, ALU.mult).then_inc(hn_in, 1)
                    elif step == "hi":
                        dve.wait_ge(xd_in, j + 1)
                        dve.tensor_copy(par_s(j, 0, 96), xd[0:96, :]).then_inc(part_in, 1)
                    elif step == "rest":
                        dve.wait_ge(part_in, 3 * j + 1)
                        dve.tensor_tensor(rest[:, :], xd[0:96, :], par_s(j, 0, 96), ALU.subtract).then_inc(part_in, 1)
                    elif step == "mid":
                        dve.wait_ge(part_in, 3 * j + 2)
                        dve.tensor_copy(mid[:, :], rest[:, :]).then_inc(part_in, 1)
                    elif step == "lo":
                        dve.wait_ge(part_in, 3 * j + 3)
                        dve.tensor_copy(par_s(j, 32, 64), mid[32:64, :])
                        dve.tensor_tensor(par_s(j, 64, 96), rest[64:96, :], mid[64:96, :], ALU.subtract)\
                           .then_inc(stack_in, 1)
                    elif step == "plus":
                        dve.wait_ge(exp_in, HV * j + h + 1)
                        dve.tensor_scalar(w1p[:, h, :], ea[:, h, :], 1.0, None, ALU.add).then_inc(plus_in, 1)
                    elif step == "err":
                        dve.wait_ge(ln_in, HV * j + h + 1)
                        dve.scalar_tensor_tensor(w1p[:, h, :], w1p[:, h, :], -1.0, ea[:, h, :], ALU.add, ALU.subtract)\
                           .then_inc(err_in, 1)
                    elif step == "diff":
                        dve.wait_ge(base_in, HV * j + h + 1)
                        dve.tensor_tensor(lg[:, h, :], lg[:, h, :], w1p[:, h, :], ALU.subtract).then_inc(diff_in, 1)
                    elif step == "choose":
                        dve.wait_ge(diff_in, HV * j + h + 1)
                        dve.scalar_tensor_tensor(lg[:, h, :], ea[:, h, :], SMALL, lg[:, h, :], ALU.is_ge, ALU.mult)\
                           .then_inc(chosen, 1)
                    elif step == "delta":
                        dve.wait_ge(chosen, HV * j + h + 1)
                        dve.tensor_tensor(par(delta, j, h), lg[:, h, :], small_pos[:, h, :], ALU.add)\
                           .then_inc(delta_in, 1)
                    elif step == "du":
                        dve.wait_ge(delta_in, HV * j + h + 1)
                        dve.tensor_tensor(par(du, j, h), par(delta, j, h), par(xs, j, h), ALU.mult).then_inc(du_in, 1)

                def par_s(i, a, b):
                    return stack[a:b, i % 2, :]

                FRONT = {1: [("hn", 0)], 18: [("hi", 0)], 19: [("rest", 0)], 20: [("mid", 0)],
                         21: [("lo", 0), ("plus", 0)], 23: [("err", 0)], 25: [("diff", 0)], 26: [("choose", 0)],
                         27: [("delta", 0)], 28: [("du", 0), ("plus", 1)], 30: [("err", 1)]}
                LATE = {2: "diff", 3: "choose", 4: "delta", 5: "du"}

                def body(i, first, last):
                    for u in range(UN):
                        if u + 1 < UN or not last:
                            drive(i, u + 1)
                        if u == 0 and not first:
                            keep(i - 1, 1)
                        if u == NS and not last:
                            keep(i, 0)
                        scan(i, u, not last)
                        if u in LATE and not first:
                            front(i - 1, LATE[u], 1)
                        if u == 6 and not first:
                            gate(i - 1, 1)
                        if u == 14 and not first:
                            residual(i - 1)
                        if u == 22:
                            gate(i, 0)
                        if not last:
                            for step, h in FRONT.get(u, []):
                                front(i, step, h)

                for slot in sorted(FRONT):
                    for step, h in FRONT[slot]:
                        front(-1, step, h)
                for step in LATE.values():
                    front(-1, step, 1)
                drive(0, 0)
                body(0, True, False)
                with dve.Fori(1, ITEMS - 1) as i:
                    body(i, False, False)
                body(ITEMS - 1, False, True)
                gate(ITEMS - 1, 1)
                residual(ITEMS - 1)

            @block.gpsimd
            def _(pool):
                def weigh(i, u):
                    g, h, n = UN * i + u, u // NS, u % NS
                    if h == 0:
                        pool.wait_ge(c_in, NS * i + n + 1)
                    pool.wait_ge(scanned, g + 1)
                    if not isinstance(g, int) or g >= NP:
                        pool.wait_ge(prod_used, g - NP + 1)
                    pool.tensor_tensor(prod[:, u % NP, :], h_ring[:, n, :], c_all[:, n, :], ALU.mult).then_inc(prod_in, 1)

                def front(i, step, h):
                    j = i + 1
                    if step == "small":
                        pool.wait_ge(half_sq, HV * j + h + 1)
                        pool.tensor_tensor(small[:, h, :], ea[:, h, :], small[:, h, :], ALU.subtract)\
                            .then_inc(small_in, 1)
                    elif step == "small_pos":
                        pool.wait_ge(small_in, HV * j + h + 1)
                        pool.tensor_tensor(small_pos[:, h, :], small[:, h, :], pos[:, h, :], ALU.add)
                    elif step == "base":
                        pool.wait_ge(err_in, HV * j + h + 1)
                        pool.tensor_tensor(w1p[:, h, :], w1p[:, h, :], small[:, h, :], ALU.add).then_inc(base_in, 1)

                FRONT = {21: ("small", 0), 22: ("small_pos", 0), 23: ("base", 0), 28: ("small", 1),
                         29: ("small_pos", 1), 30: ("base", 1)}

                def body(i, last):
                    for u in range(UN):
                        weigh(i, u)
                        if not last and u in FRONT:
                            front(i, *FRONT[u])

                for slot in sorted(FRONT):
                    front(-1, *FRONT[slot])
                body(0, False)
                with pool.Fori(1, ITEMS - 1) as i:
                    body(i, False)
                body(ITEMS - 1, True)

        tail(nc, ctx, sem, bank, v, V, Cn, r, ident, meanw, center, eps, h0_d, s_d, fc1, fc2, wr, br, w1, w2, b2, out,
             h_ring, c_all, decay, prod, delta, du, xs, zs, sb)


def tail(nc, ctx, sem, bank, v, V, Cn, r, ident, meanw, center, eps, h0_d, s_d, fc1, fc2, wr, br, w1, w2, b2, out,
         h_ring, c_all, decay, prod, delta, du, xs, zs, sb):
    names = ["s_in", "h0_in", "sqd", "var", "rst", "logd", "cen", "scl", "hid", "hsum", "mlp1", "g_in", "mlp2", "a1", "h1",
             "xn", "out_kept", "rt", "lgt", "mx", "eq", "rk", "rm", "oh", "oht", "ohs", "b2f", "acc0", "th1",
             "res", "up", "rl", "dn", "wt", "ac"]
    q = {n: [sem(f"t_{n}_s{s}") for s in range(2)] for n in names}
    w_loaded = sem("t_w_loaded")

    flat = c_all[:, :, :].rearrange("p a b -> p (a b)")
    w1_s = flat[:, 0:E * HB * P].rearrange("p (e n) -> p e n", e=E)
    w2_s = flat[:, E * HB * P:2 * E * HB * P].rearrange("p (e k o) -> p e k o", e=E, k=HB)
    fc1_s = decay[:, 0, :]
    fc2_s = decay[:, 1, :].rearrange("p (k o) -> p k o", k=HB)
    wr_s = decay[:, 2, 0:E]
    br_s = decay[:, 2, E:2 * E]
    b2_s = decay[0:E, 3, 0:P]
    D = [delta[:, s, :, :] for s in range(2)]
    s_in = [D[s][:, 0, :] for s in range(2)]
    h0_in = [D[s][:, 1, :] for s in range(2)]
    sqb = [du[:, s, 0, :] for s in range(2)]
    lnb = [du[:, s, 1, :] for s in range(2)]
    rsb = [xs[:, s, 0, :] for s in range(2)]
    tmp = [xs[:, s, 1, :] for s in range(2)]
    hsum = [zs[:, s, 0, :] for s in range(2)]
    xn = [zs[:, s, 1, :] for s in range(2)]
    gel = [h_ring[:, 4 * s:4 * s + 4, :] for s in range(2)]
    hid = [h_ring[:, 8 + 4 * s:12 + 4 * s, :] for s in range(2)]
    h1 = [prod[:, s, :] for s in range(2)]
    acc = [prod[:, 2 + s, :] for s in range(2)]
    route = sb("route", [P, 2, 6, TT, E])
    top = sb("top", [P, 2, 2, TT])
    oht = sb("oht", [E, 2, TC])
    lg = [route[:, s, 0] for s in range(2)]
    eq = [route[:, s, 1] for s in range(2)]
    rk = [route[:, s, 2] for s in range(2)]
    oh = [route[:, s, 3] for s in range(2)]
    rank = Cn[:, CON["rank"]:CON["rank"] + E].unsqueeze(1).to_broadcast([P, TT, E])

    def chunk_d(t, k, s):
        return t[k + s * CPB, :, :]

    def chunk(k, s):
        return r[:, k + s * CPB, :]

    with nc.Block() as block:

        @block.sync
        def _(sp):
            sp.dma_start(fc1_s, fc1).then_inc(w_loaded, 16)
            sp.dma_start(fc2_s, fc2).then_inc(w_loaded, 16)
            sp.dma_start(wr_s, wr).then_inc(w_loaded, 16)
            sp.dma_start(br_s, br.partition_broadcast(P)).then_inc(w_loaded, 16)
            sp.dma_start(b2_s, b2).then_inc(w_loaded, 16)
            sp.dma_start(w1_s, w1).then_inc(w_loaded, 16)
            sp.dma_start(w2_s, w2).then_inc(w_loaded, 16)
            def one_round(k):
                for s in range(2):
                    if later(k):
                        sp.wait_ge(q["a1"][s], k)
                    if later(k):
                        sp.wait_ge(q["h1"][s], k)
                    sp.dma_start(s_in[s], chunk_d(s_d, k, s)).then_inc(q["s_in"][s], 16)
                    sp.dma_start(h0_in[s], chunk_d(h0_d, k, s)).then_inc(q["h0_in"][s], 16)
                for s in range(2):
                    sp.wait_ge(q["res"][s], k + 1)
                    sp.dma_start(out[k + s * CPB, :, :, :].rearrange("t p c -> p t c"),
                                 acc[s].rearrange("p (t c) -> p t c", t=TT)).then_inc(q["out_kept"][s], 16)
            rounds(sp, one_round)
            for s in range(2):
                sp.wait_ge(q["out_kept"][s], 16 * CPB)

        @block.tensor
        def _(pe):
            pe.wait_ge(w_loaded, 7 * 16)
            def one_round(k):
                def each(ready, f, count=None):
                    for s in range(2):
                        pe.wait_ge(q[ready][s], k + 1 if count is None else count)
                        f(s)
                each("sqd", lambda s: pe.matmul(bank(4 * s + 2), meanw, sqb[s], start=True, stop=True)
                     .then_inc(q["var"][s], 1), 3 * k + 1)
                each("hsum", lambda s: pe.matmul(bank(4 * s + 1), center, hsum[s], start=True, stop=True)
                     .then_inc(q["cen"][s], 1))
                each("sqd", lambda s: pe.matmul(bank(4 * s + 2), meanw, sqb[s], start=True, stop=True)
                     .then_inc(q["var"][s], 1), 3 * k + 2)
                for s in range(2):
                    pe.wait_ge(q["xn"][s], k + 1)
                    for b in range(HB):
                        if b >= 2:
                            pe.wait_ge(q["g_in"][s], HB * k + b - 1)
                        pe.matmul(bank(4 * s + (0, 3)[b % 2]), fc1_s[:, b * P:(b + 1) * P], tmp[s], start=True,
                                  stop=True).then_inc(q["mlp1"][s], 1)
                for s in range(2):
                    for b in range(HB):
                        pe.wait_ge(q["g_in"][s], HB * k + b + 1)
                        mm = pe.matmul(bank(4 * s + 2), fc2_s[:, b, :], gel[s][:, b, :], start=(b == 0),
                                       stop=(b == HB - 1))
                    mm.then_inc(q["mlp2"][s], 1)
                each("h1", lambda s: pe.matmul(bank(4 * s + 1), center, h1[s], start=True, stop=True)
                     .then_inc(q["cen"][s], 1))
                each("sqd", lambda s: pe.matmul(bank(4 * s + 2), meanw, sqb[s], start=True, stop=True)
                     .then_inc(q["var"][s], 1), 3 * k + 3)
                for s in range(2):
                    pe.wait_ge(q["scl"][s], 2 * k + 2)
                    for t in range(TT):
                        mm = pe.matmul(bank(4 * s)[:, t * E:(t + 1) * E], xn[s][:, t * P:(t + 1) * P], wr_s,
                                       start=True, stop=True)
                    mm.then_inc(q["rt"][s], 1)
                for s in range(2):
                    pe.wait_ge(q["oh"][s], k + 1)
                    for t in range(TT):
                        mm = pe.transpose(bank(4 * s + 1)[0:E, t * P:(t + 1) * P], oh[s][:, t, :], ident)
                    mm.then_inc(q["oht"][s], 1)
                for s in range(2):
                    pe.wait_ge(q["ohs"][s], k + 1)
                    for t in range(TT):
                        mm = pe.matmul(bank(4 * s + 2)[:, t * P:(t + 1) * P], oht[:, s, t * P:(t + 1) * P], b2_s,
                                       start=True, stop=True)
                    mm.then_inc(q["b2f"][s], 1)
                for s in range(2):
                    pe.wait_ge(q["ohs"][s], k + 1)
                    for t in range(TT):
                        mm = pe.transpose(bank(4 * s + 1)[:, t * P:(t + 1) * P], h1[s][:, t * P:(t + 1) * P], ident)
                    mm.then_inc(q["th1"][s], 1)

                def up(s, e, b):
                    n = e * HB + b
                    if n >= 2:
                        pe.wait_ge(q["rl"][s], E * HB * k + n - 1)
                    pe.matmul(bank(4 * s + (0, 3)[n % 2]), w1_s[:, e, b * P:(b + 1) * P], xn[s], start=True,
                              stop=True).then_inc(q["up"][s], 1)

                def down(s, e):
                    pe.wait_ge(q["rl"][s], E * HB * k + HB * (e + 1))
                    if e == 0:
                        pe.wait_ge(q["acc0"][s], k + 1)
                    else:
                        pe.wait_ge(q["wt"][s], E * k + e)
                    for t in range(TT):
                        for b in range(HB):
                            mm = pe.matmul(bank(4 * s + 2)[:, t * P:(t + 1) * P], hid[s][:, b, t * P:(t + 1) * P],
                                           w2_s[:, e, b, :], start=(b == 0), stop=(b == HB - 1))
                    mm.then_inc(q["dn"][s], 1)

                for e in range(E + 1):
                    for s in range(2):
                        if s == 0 and e < E:
                            for b in range(HB):
                                up(0, e, b)
                        if s == 1 and e < E:
                            for b in range(HB):
                                up(1, e, b)
                        if e < E:
                            down(s, e)
            rounds(pe, one_round)

        @block.scalar
        def _(act):
            def one_round(k):
                act.preload_act_table_set(LOG_EXP)
                def rs(m, s):
                    act.wait_ge(q["var"][s], 3 * k + m + 1)
                    act.activation(lnb[s], bank(4 * s + 2), ACT.Ln, bias=eps).then_inc(q["logd"][s], 1)
                    act.wait_ge(q["logd"][s], 3 * k + m + 1)
                    act.activation(rsb[s], lnb[s], ACT.Exp, scale=-0.5).then_inc(q["rst"][s], 1)

                def square(m, s):
                    act.wait_ge(q["cen"][s], 2 * k + m)
                    act.activation(sqb[s], bank(4 * s + 1), ACT.Square).then_inc(q["sqd"][s], 1)

                for s in range(2):
                    if later(k):
                        act.wait_ge(q["res"][s], k)
                    act.activation(sqb[s], chunk(k, s), ACT.Square).then_inc(q["sqd"][s], 1)
                for s in range(2):
                    rs(0, s)
                for s in range(2):
                    square(1, s)
                for s in range(2):
                    rs(1, s)
                for s in range(2):
                    act.wait_ge(q["scl"][s], 2 * k + 1)
                    act.activation(tmp[s], xn[s], ACT.Identity, scale=v("ln2_w"), bias=v("ln2_b"))\
                       .then_inc(q["xn"][s], 1)
                for s in range(2):
                    for b in range(HB):
                        act.wait_ge(q["mlp1"][s], HB * k + b + 1)
                        act.activation(gel[s][:, b, :], bank(4 * s + (0, 3)[b % 2]), ACT.Gelu_apprx_tanh,
                                       bias=v("fc1_b", b)).then_inc(q["g_in"][s], 1)
                act.preload_act_table_set(LOG_EXP)
                for s in range(2):
                    square(2, s)
                for s in range(2):
                    rs(2, s)
                for s in range(2):
                    act.wait_ge(q["oht"][s], k + 1)
                    act.activation(oht[:, s, :], bank(4 * s + 1)[0:E, :], ACT.Copy).then_inc(q["ohs"][s], 1)
                for e in range(E):
                    for s in range(2):
                        for b in range(HB):
                            n = e * HB + b
                            act.wait_ge(q["up"][s], E * HB * k + n + 1)
                            if b == 0 and e > 0:
                                act.wait_ge(q["dn"][s], E * k + e)
                            act.activation(hid[s][:, b, :], bank(4 * s + (0, 3)[n % 2]), ACT.Relu,
                                           bias=v("b1", n)).then_inc(q["rl"][s], 1)
            rounds(act, one_round)

        @block.vector
        def _(dve):
            dve.wait_ge(w_loaded, 7 * 16)
            def one_round(k):
                def each(f):
                    for s in range(2):
                        f(s)

                def hidden(s):
                    dve.wait_ge(q["rst"][s], 3 * k + 1)
                    dve.scalar_tensor_tensor(tmp[s], chunk(k, s), v("norm_f"), rsb[s], ALU.mult, ALU.mult)\
                       .then_inc(q["hid"][s], 1)

                def hsums(s):
                    dve.wait_ge(q["hid"][s], k + 1)
                    dve.wait_ge(q["s_in"][s], 16 * (k + 1))
                    dve.tensor_tensor(hsum[s], tmp[s], s_in[s], ALU.add).then_inc(q["hsum"][s], 1)

                def scaled(m, dst):
                    def f(s):
                        dve.wait_ge(q["rst"][s], 3 * k + m + 1)
                        dve.tensor_tensor(dst[s], bank(4 * s + 1), rsb[s], ALU.mult).then_inc(q["scl"][s], 1)
                    return f

                def a1(s):
                    dve.wait_ge(q["mlp2"][s], k + 1)
                    dve.scalar_tensor_tensor(hsum[s], bank(4 * s + 2), v("fc2_b"), hsum[s], ALU.add, ALU.add)\
                       .then_inc(q["a1"][s], 1)

                def h1s(s):
                    dve.wait_ge(q["a1"][s], k + 1)
                    dve.wait_ge(q["h0_in"][s], 16 * (k + 1))
                    dve.tensor_tensor(h1[s], hsum[s], h0_in[s], ALU.add).then_inc(q["h1"][s], 1)

                each(hidden)
                each(hsums)
                each(scaled(1, xn))
                each(a1)
                each(h1s)
                each(scaled(2, xn))
                for s in range(2):
                    dve.wait_ge(q["rt"][s], k + 1)
                    dve.tensor_tensor(lg[s], bank(4 * s)[:, 0:TT * E].rearrange("p (t e) -> p t e", t=TT),
                                      br_s.unsqueeze(1).to_broadcast([P, TT, E]), ALU.add).then_inc(q["lgt"][s], 1)
                    dve.wait_ge(q["lgt"][s], k + 1)
                    dve.reduce_max(top[:, s, 0, :], lg[s], AX).then_inc(q["mx"][s], 1)
                    dve.wait_ge(q["mx"][s], k + 1)
                    dve.tensor_tensor(eq[s], lg[s], top[:, s, 0, :].unsqueeze(2).to_broadcast([P, TT, E]),
                                      ALU.is_equal).then_inc(q["eq"][s], 1)
                    dve.wait_ge(q["eq"][s], k + 1)
                    dve.tensor_tensor(rk[s], eq[s], rank, ALU.mult).then_inc(q["rk"][s], 1)
                    dve.wait_ge(q["rk"][s], k + 1)
                    dve.reduce_max(top[:, s, 1, :], rk[s], AX).then_inc(q["rm"][s], 1)
                    dve.wait_ge(q["rm"][s], k + 1)
                    dve.tensor_tensor(oh[s], rk[s], top[:, s, 1, :].unsqueeze(2).to_broadcast([P, TT, E]),
                                      ALU.is_equal).then_inc(q["oh"][s], 1)
                for s in range(2):
                    dve.wait_ge(q["b2f"][s], k + 1)
                    if later(k):
                        dve.wait_ge(q["out_kept"][s], 16 * k)
                    dve.tensor_copy(acc[s], bank(4 * s + 2)).then_inc(q["acc0"][s], 1)
                for e in range(E):
                    for s in range(2):
                        dve.wait_ge(q["dn"][s], E * k + e + 1)
                        dve.tensor_tensor(tmp[s].rearrange("p (t c) -> p t c", t=TT),
                                          bank(4 * s + 2).rearrange("p (t c) -> p t c", t=TT),
                                          oh[s][:, :, e:e + 1].to_broadcast([P, TT, P]), ALU.mult)\
                           .then_inc(q["wt"][s], 1)
                        dve.wait_ge(q["wt"][s], E * k + e + 1)
                        dve.tensor_tensor(acc[s], acc[s], tmp[s], ALU.add).then_inc(q["ac"][s], 1)
                        dve.wait_ge(q["ac"][s], E * k + e + 1)
                for s in range(2):
                    dve.wait_ge(q["th1"][s], k + 1)
                    dve.tensor_tensor(acc[s], acc[s], bank(4 * s + 1), ALU.add).then_inc(q["res"][s], 1)
            rounds(dve, one_round)


def kernel(**inputs):
    import concourse.bacc as _bacc
    from concourse.bass_utils import run_bass_kernel_spmd as _run

    a = {k: np.asarray(x) for k, x in inputs.items()}

    def cols(x):
        return x.reshape(-1, P).T

    pre = "L0_attn_"
    vec = np.concatenate([
        a["L0_tok_conv_w"], cols(a["L0_tok_gamma"]), cols(a["L0_tok_beta"]), cols(a[pre + "ln1_w"]),
        cols(a[pre + "ln1_b"]), cols(a[pre + "norm_f_w"]), cols(a[pre + "ln2_w"]), cols(a[pre + "ln2_b"]),
        cols(a[pre + "fc2_b"]), cols(a[pre + "block_norm_w"]), cols(a[pre + "fc1_b"]), cols(a[pre + "conv_b"]),
        cols(a[pre + "dt_proj_b"]), cols(a[pre + "D_param"]), cols(a["L0_ffn_b1"]),
        a[pre + "A_log"].reshape(NL, HV, P, NS).transpose(2, 0, 1, 3).reshape(P, NL * HV * NS)], axis=1)
    con = np.zeros((P, NCON), np.float32)
    con[:, CON["ident"]:CON["ident"] + P] = np.eye(P)
    con[:, CON["mean"]:CON["mean"] + P] = 1.0 / P
    con[:, CON["center"]:CON["center"] + P] = np.eye(P) - 1.0 / P
    con[:, CON["pick"]:CON["pick"] + 2 * NS] = np.arange(P)[:, None] % (2 * NS) == np.arange(2 * NS)[None, :]
    con[:, CON["keep"]:CON["keep"] + ITEMS] = np.arange(ITEMS)[None, :] % CPB != 0
    con[:, CON["eps"]] = EPS
    con[:, CON["one"]] = 1.0
    con[:, CON["rank"]:CON["rank"] + E] = E - np.arange(E)[None, :]

    win = a[pre + "in_proj_w"].transpose(2, 0, 1)
    arrays = {
        "tok": a["x"].reshape(TOK // P, P).T.view(np.uint32) if a["x"].dtype == np.int32 else a["x"].reshape(TOK // P, P).T,
        "embed": a["L0_tok_embed_table"],
        "vec": vec,
        "con": con,
        "win_x": win[:, :, 0:DI],
        "win_z": win[:, :, DI:2 * DI],
        "conv_w": a[pre + "conv_w"].transpose(0, 2, 1),
        "xproj": a[pre + "x_proj_w"].reshape(NL, R + 2 * NS, HV, P).transpose(0, 3, 2, 1),
        "dtw": a[pre + "dt_proj_w"].transpose(0, 2, 1),
        "outw": a[pre + "out_proj_w"].reshape(NL, P, HV, P).transpose(0, 3, 2, 1).reshape(NL, P, HV * P),
        "fc1": a[pre + "fc1_w"].T,
        "fc2": a[pre + "fc2_w"].reshape(P, HB, P).transpose(2, 1, 0),
        "wr": a["L0_ffn_Wr"],
        "br": a["L0_ffn_br"],
        "w1": a["L0_ffn_W1"].transpose(1, 0, 2),
        "w2": a["L0_ffn_W2"].reshape(E, HB, P, P).transpose(2, 0, 1, 3),
        "b2": a["L0_ffn_b2"],
    }
    arrays = {f"in_{k}": np.ascontiguousarray(x) for k, x in arrays.items()}
    nc = _bacc.Bacc("TRN2", target_bir_lowering=False, num_devices=1)
    args = [nc.dram_tensor(k, x.shape, mybir.dt.from_np(x.dtype), kind="ExternalInput").ap() for k, x in arrays.items()]
    args.append(nc.dram_tensor("out_0", (NCH, TT, P, P), F32, kind="ExternalOutput").ap())
    lm_tower(nc, *args)
    res = _run(nc, [arrays], core_ids=[0])
    return res.results[0]["out_0"].reshape(BATCH, TOK // BATCH, P)
```

```python
from contextlib import ExitStack

import concourse.bass as bass
import numpy as np
from concourse import mybir

F32 = mybir.dt.float32
BF16 = mybir.dt.bfloat16
U32 = mybir.dt.uint32
ALU = mybir.AluOpType
ACT = mybir.ActivationFunctionType
AX = mybir.AxisListType.X
ds = bass.ds

P = 128
TC = 512
BATCH = 2
TOK = 4096
NCH = TOK // TC
CPB = NCH // BATCH
TT = TC // P
NL = 4
HV = 2
NS = 16
KC = 4
KT = 3
R = 8
DI = HV * P
UN = HV * NS
ITEMS = NL * NCH
E = 8
HB = 4
EPS = 1e-5
SMALL = 2.0 ** -12
SQRT_HALF = 0.5 ** 0.5
LOG_EXP = "natural_log_exp_and_others"

VEC = {}
_at = 0
for _name, _n in (("tok_w", KT), ("tok_gamma", 1), ("tok_beta", 1), ("ln1_w", 1), ("ln1_b", 1), ("norm_f", 1),
                  ("ln2_w", 1), ("ln2_b", 1), ("fc2_b", 1), ("block_norm", NL), ("fc1_b", HB),
                  ("conv_b", NL * HV), ("dt_b", NL * HV), ("D", NL * HV),
                  ("A", NL * HV * NS)):
    VEC[_name] = _at
    _at += _n
NVEC = _at
CON = {}
_at = 0
for _name, _n in (("ident", P), ("mean", P), ("center", P), ("pick", 2 * NS), ("keep", ITEMS), ("eps", 1), ("one", 1),
                  ("rank", E)):
    CON[_name] = _at
    _at += _n
NCON = _at

ET = 256
NT = TOK // ET + E - 1
RT = TOK // P
NX = 2 * HB * P + HB + P
SORT = {}
_at = 0
for _name, _n in (("ones", P), ("before", P), ("multiple", TOK // ET), ("number", NT), ("row", 1), ("restart", E * RT)):
    SORT[_name] = _at
    _at += _n
NSORT = _at

W_TAP, W_Z, W_X, W_DT = 0, KC * DI, KC * DI + DI, KC * DI + 2 * DI
NW = W_DT + DI

ND, NP = 4, 8
NB = 4
LEAD_B, LEAD_A, LAG = 3, 3, 4

CF = 11
FILLS = {0: [("C", 11), ("C", 12)], 1: [("C", 13)], 2: [("C", 14)], 3: [("C", 15)], 6: [("z", 0)], 7: [("z", 1)],
         10: [("x", 0)], 13: [("x", 1)], 16: [("xd", 0)], 18: [("dt", 0)], 25: [("dt", 1)], 28: [("stat", 0)]}
for _n in range(CF):
    FILLS.setdefault(21 + _n, []).append(("C", _n))
BANK_USES = [use for slot in sorted(FILLS) for use in FILLS[slot]]
BANK_AT = {use: k for k, use in enumerate(BANK_USES)}
NBU = len(BANK_USES)
FIRST_USES = ([("stat", -1)] + [(what, h) for what, h in BANK_USES if what in ("z", "x", "xd", "dt")]
              + [("C", n) for n in range(CF)] + [("stat", 0)])
FIRST_AT = {use: k for k, use in enumerate(FIRST_USES)}
LAST_AT = {use: k for k, use in enumerate([use for use in BANK_USES if use[0] == "C" and use[1] >= CF])}


def rounds(eng, one_round):
    one_round(0)
    with eng.Fori(1, CPB) as k:
        one_round(k)


def later(k):
    return not isinstance(k, int) or k > 0


def lm_tower(nc, tok, embed, vec, con, sort, win_x, win_z, conv_w, xproj, dtw, outw, fc1, fc2, wr, br, wexp, out):
    ctx = ExitStack()
    with ctx:
        def sb(name, shape, dt=F32):
            return ctx.enter_context(nc.sbuf_tensor(name, shape, dt))

        def sem(name):
            return ctx.enter_context(nc.semaphore(name))

        psum = ctx.enter_context(nc.psum_tensor("banks", [P, 8, TC], F32))

        def bank(b):
            return psum[:, b, :]

        h0_d = nc.dram_tensor("h0_scratch", [NCH, P, TC], F32, kind="Internal").ap()
        s_d = nc.dram_tensor("s_scratch", [NCH, P, TC], F32, kind="Internal").ap()
        x_d = nc.dram_tensor("sorted_scratch", [NT * ET, P], F32, kind="Internal").ap()
        y_d = nc.dram_tensor("results_scratch", [NT * ET, P], F32, kind="Internal").ap()
        w_d = nc.dram_tensor("front_scratch", [NL, P, NW], F32, kind="Internal").ap()

        V = sb("V", [P, NVEC])
        Cn = sb("Cn", [P, NCON])
        r = sb("r", [P, NCH, TC])
        ident = Cn[:, CON["ident"]:CON["ident"] + P]
        meanw = Cn[:, CON["mean"]:CON["mean"] + P]
        center = Cn[:, CON["center"]:CON["center"] + P]
        eps = Cn[:, CON["eps"]:CON["eps"] + 1]
        one = Cn[:, CON["one"]:CON["one"] + 1]

        def v(name, k=0):
            return V[:, VEC[name] + k:VEC[name] + k + 1]

        h_ring = sb("h_ring", [P, NS, TC])
        c_all = sb("c_all", [P, NS, TC])
        decay = sb("decay", [P, ND, TC])
        prod = sb("prod", [P, NP, TC])
        delta = sb("delta", [P, 2, HV, TC])
        du = sb("du", [P, 2, HV, TC])
        xs = sb("xs", [P, 2, HV, TC])
        zs = sb("zs", [P, 2, HV, TC])
        stack = sb("stack", [96, 2, TC], BF16)
        pick = sb("pick", [96, 2 * NS, P], BF16)
        wf = sb("wf", [P, NW])
        wo = sb("wo", [P, HV, P])
        hn = sb("hn", [P, KC - 1 + TC])
        h_init = sb("h_init", [P, HV, NS])
        sq = sb("sq", [P, TC])
        lnv = sb("lnv", [P, TC])
        rstd = sb("rstd", [P, TC])
        xd = sb("xd", [P, TC])
        rest = sb("rest", [96, TC])
        mid = sb("mid", [96, TC], BF16)
        ea = sb("ea", [P, HV, TC])
        pos = sb("pos", [P, HV, TC])
        w1p = sb("w1p", [P, HV, TC])
        lg = sb("lg", [P, HV, TC])
        small = sb("small", [P, HV, TC])
        small_pos = sb("small_pos", [P, HV, TC])
        yt = sb("yt", [P, TC])
        yz = sb("yz", [P, HV, TC])

        loaded = sem("loaded")
        gathered = [sem(f"gathered{s}") for s in range(2)]
        names0 = ["turned", "emb", "tap0", "tap1", "tap2", "cen", "sqd", "var", "logd", "rst", "scl", "h0_made",
                  "h0_kept", "s_kept", "hist"]
        q0 = {n: [sem(f"{n}_s{s}") for s in range(2)] for n in names0}
        folded = sem("folded")
        picked = sem("picked")
        neg_a = sem("neg_a")
        w_zero = sem("w_zero")
        w_in = sem("w_in")
        w_out = sem("w_out")
        r_ready = sem("r_ready")

        g_tok = h_ring[:, 0:4, :].rearrange("p (s t) c -> p s (t c)", s=2)[:, :, 0:TT * P]
        idx = sb("idx", [P, TOK // P], U32)
        emb = [h_ring[:, 4 + 2 * s:6 + 2 * s, :].rearrange("p a b -> p (a b)")[:, 0:KT - 1 + TC] for s in range(2)]
        ta = [h_ring[:, 8 + s, :] for s in range(2)]
        tb = [h_ring[:, 10 + s, :] for s in range(2)]
        s_sq = [h_ring[:, 12 + s, :] for s in range(2)]
        s_rs = [h_ring[:, 14 + s, :] for s in range(2)]
        s_ln = [decay[:, s, :] for s in range(2)]
        s_y = [decay[:, 2 + s, :] for s in range(2)]
        s_h0 = [prod[:, s, :] for s in range(2)]
        s_s = [prod[:, 2 + s, :] for s in range(2)]
        wx_all = c_all[:, :, :].rearrange("p a b -> p (a b)")[:, 0:NL * DI].rearrange("p (l d) -> p l d", l=NL)
        cw_all = c_all[:, :, :].rearrange("p a b -> p (a b)")[:, NL * DI:NL * DI * (1 + KC)]
        cw_all = cw_all.rearrange("p (l k d) -> p l k d", l=NL, k=KC)

        with nc.Block() as block:

            @block.sync
            def _(sp):
                sp.dma_start(V[:, :], vec).then_inc(loaded, 16)
                sp.dma_start(Cn[:, :], con).then_inc(loaded, 16)
                sp.dma_start(idx[:, :], tok).then_inc(w_in, 16)
                sp.dma_start(wx_all, win_x).then_inc(folded, 16)
                sp.dma_start(cw_all, conv_w.partition_broadcast(P)).then_inc(folded, 16)
                for l in range(NL):
                    sp.wait_ge(w_zero, l + 1)
                    sp.dma_start(wf[:, W_Z:W_Z + DI], win_z[:, l, :]).then_inc(w_out, 16)
                    for h in range(HV):
                        for rep in range(3):
                            sp.dma_start(wf[:, W_X + h * P + 32 * rep:W_X + h * P + 32 * rep + 32],
                                         xproj[l, :, h, R:R + 2 * NS]).then_inc(w_out, 16)
                        sp.dma_start(wf[:, W_X + h * P + 96:W_X + h * P + 96 + R], xproj[l, :, h, 0:R]).then_inc(w_out, 16)
                    sp.dma_start(wf[96:96 + R, W_DT:W_DT + DI], dtw[l, :, :]).then_inc(w_out, 16)
                    sp.wait_ge(w_out, (11 * l + 10) * 16)
                    sp.wait_ge(picked, l + 2)
                    sp.dma_start(w_d[l, :, :], wf[:, :]).then_inc(w_out, 16)
                    sp.wait_ge(w_out, (11 * l + 11) * 16)
                    sp.sem_inc(neg_a, 1)
                def one_round(k):
                    for s in range(2):
                        sp.wait_ge(q0["h0_made"][s], k + 1)
                        sp.dma_start(h0_d[k + s * CPB, :, :], s_h0[s])\
                          .then_inc(q0["h0_kept"][s], 16)
                        sp.wait_ge(q0["scl"][s], 3 * k + 2)
                        sp.dma_start(s_d[k + s * CPB, :, :], s_s[s])\
                          .then_inc(q0["s_kept"][s], 16)
                rounds(sp, one_round)
                for s in range(2):
                    sp.wait_ge(q0["h0_kept"][s], 16 * CPB)
                    sp.wait_ge(q0["s_kept"][s], 16 * CPB)

            @block.gpsimd
            def _(pool):
                pool.memset(hn[:, :], 0.0)
                pool.memset(h_init[:, :, :], 0.0)
                pool.wait_ge(w_in, 16)
                for k in range(CPB):
                    for s in range(2):
                        if k:
                            pool.wait_ge(q0["turned"][s], k)
                        for t in range(TT):
                            col = (k + s * CPB) * TT + t
                            pool.indirect_dma_start(
                                out=g_tok[:, s, t * P:(t + 1) * P], out_offset=None, in_=embed,
                                in_offset=bass.IndirectOffsetOnAxis(ap=idx[:, col:col + 1], axis=0))\
                                .then_inc(gathered[s], 16)

            @block.tensor
            def _(pe):
                pe.wait_ge(loaded, 32)
                def one_round(k):
                    for s in range(2):
                        pe.wait_ge(gathered[s], (k + 1) * 16 * TT)
                        for t in range(TT):
                            last = pe.transpose(bank(4 * s)[:, t * P:(t + 1) * P], g_tok[:, s, t * P:(t + 1) * P], ident)
                        last.then_inc(q0["turned"][s], 1)
                    for m, (src, ready, count) in enumerate(((ta, "tap2", k + 1), (s_h0, "h0_made", k + 1),
                                                             (s_s, "scl", 3 * k + 2)), 1):
                        for s in range(2):
                            pe.wait_ge(q0[ready][s], count)
                            pe.matmul(bank(4 * s + 1), center, src[s], start=True, stop=True)\
                              .then_inc(q0["cen"][s], 1)
                        for s in range(2):
                            pe.wait_ge(q0["sqd"][s], 3 * k + m)
                            pe.matmul(bank(4 * s + 2), meanw, s_sq[s], start=True, stop=True)\
                              .then_inc(q0["var"][s], 1)
                rounds(pe, one_round)

            @block.scalar
            def _(act):
                act.preload_act_table_set(LOG_EXP)
                act.wait_ge(loaded, 32)
                a_all = V[:, VEC["A"]:VEC["A"] + NL * HV * NS]
                act.activation(a_all, a_all, ACT.Exp).then_inc(picked, 1)
                def one_round(k):
                    for s in range(2):
                        act.wait_ge(q0["turned"][s], k + 1)
                        act.wait_ge(q0["hist"][s], k + 1)
                        act.activation(emb[s][:, KT - 1:KT - 1 + TC], bank(4 * s), ACT.Copy).then_inc(q0["emb"][s], 1)
                    for m in (1, 2, 3):
                        for s in range(2):
                            act.wait_ge(q0["cen"][s], 3 * k + m)
                            act.activation(s_sq[s], bank(4 * s + 1), ACT.Square).then_inc(q0["sqd"][s], 1)
                        for s in range(2):
                            act.wait_ge(q0["var"][s], 3 * k + m)
                            act.activation(s_ln[s], bank(4 * s + 2), ACT.Ln, bias=eps).then_inc(q0["logd"][s], 1)
                            act.wait_ge(q0["logd"][s], 3 * k + m)
                            act.activation(s_rs[s], s_ln[s], ACT.Exp, scale=-0.5).then_inc(q0["rst"][s], 1)
                        if m == 1:
                            for s in range(2):
                                act.wait_ge(q0["scl"][s], 3 * k + 1)
                                if later(k):
                                    act.wait_ge(q0["h0_kept"][s], 16 * k)
                                act.activation(s_h0[s], s_y[s], ACT.Relu, scale=v("tok_gamma"), bias=v("tok_beta"))\
                                   .then_inc(q0["h0_made"][s], 1)
                        if m == 3:
                            for s in range(2):
                                act.wait_ge(q0["scl"][s], 3 * k + 3)
                                act.activation(r[:, k + s * CPB, :], s_y[s],
                                               ACT.Identity, scale=v("ln1_w"), bias=v("ln1_b")).then_inc(r_ready, 1)
                rounds(act, one_round)

            @block.vector
            def _(dve):
                dve.wait_ge(loaded, 32)
                pk = Cn[0:96, CON["pick"]:CON["pick"] + 2 * NS]
                dve.tensor_copy(pick[:, :, :], pk.unsqueeze(2).to_broadcast([96, 2 * NS, P]))
                dve.memset(wf[:, W_X:NW], 0.0).then_inc(w_zero, 1)
                dve.wait_ge(picked, 1)
                a_all = V[:, VEC["A"]:VEC["A"] + NL * HV * NS]
                dve.tensor_scalar(a_all, a_all, -1.0, None, ALU.mult)
                dve.wait_ge(folded, 32)
                for l in range(NL):
                    if l:
                        dve.wait_ge(neg_a, l)
                    src = wx_all[:, l, :].unsqueeze(1).to_broadcast([P, KC, DI])
                    dve.tensor_tensor(wf[:, 0:KC * DI].rearrange("p (k d) -> p k d", k=KC), src, cw_all[:, l, :, :],
                                      ALU.mult).then_inc(picked, 1)
                    if l + 1 < NL:
                        dve.wait_ge(neg_a, l + 1)
                        dve.sem_inc(w_zero, 1)
                for s in range(2):
                    dve.memset(emb[s][:, TC:TC + KT - 1], 0.0).then_inc(q0["tap0"][s], 1)
                    dve.wait_ge(q0["tap0"][s], 1)
                def one_round(k):
                    for s in range(2):
                        if later(k):
                            if later(k):
                                dve.wait_ge(q0["tap2"][s], k)
                        dve.tensor_copy(emb[s][:, 0:KT - 1], emb[s][:, TC:TC + KT - 1]).then_inc(q0["hist"][s], 1)
                    for s in range(2):
                        dve.wait_ge(q0["emb"][s], k + 1)
                        dve.wait_ge(q0["hist"][s], k + 1)
                        dve.tensor_scalar(ta[s], emb[s][:, 0:TC], v("tok_w", 0), None, ALU.mult)\
                           .then_inc(q0["tap0"][s], 1)
                        dve.wait_ge(q0["tap0"][s], k + 2)
                        dve.scalar_tensor_tensor(tb[s], emb[s][:, 1:1 + TC], v("tok_w", 1), ta[s], ALU.mult, ALU.add)\
                           .then_inc(q0["tap1"][s], 1)
                        dve.wait_ge(q0["tap1"][s], k + 1)
                        dve.scalar_tensor_tensor(ta[s], emb[s][:, 2:2 + TC], v("tok_w", 2), tb[s], ALU.mult, ALU.add)\
                           .then_inc(q0["tap2"][s], 1)
                    for m in (1, 2, 3):
                        for s in range(2):
                            dve.wait_ge(q0["rst"][s], 3 * k + m)
                            if m == 2:
                                if later(k):
                                    dve.wait_ge(q0["s_kept"][s], 16 * k)
                            dve.tensor_tensor(s_s[s] if m == 2 else s_y[s], bank(4 * s + 1), s_rs[s], ALU.mult)\
                               .then_inc(q0["scl"][s], 1)
                rounds(dve, one_round)

        front_in = sem("front_in")
        out_in = sem("out_in")
        squared = sem("squared")
        logged = sem("logged")
        rstd_in = sem("rstd_in")
        hist_in = sem("hist_in")
        hn_in = sem("hn_in")
        z_in = sem("z_in")
        xs_in = sem("xs_in")
        xd_in = sem("xd_in")
        part_in = sem("part_in")
        stack_in = sem("stack_in")
        abs_in = sem("abs_in")
        exp_in = sem("exp_in")
        plus_in = sem("plus_in")
        ln_in = sem("ln_in")
        half_sq = sem("half_sq")
        small_in = sem("small_in")
        err_in = sem("err_in")
        base_in = sem("base_in")
        diff_in = sem("diff_in")
        chosen = sem("chosen")
        delta_in = sem("delta_in")
        du_in = sem("du_in")
        bank_full = sem("bank_full")
        bank_free = sem("bank_free")
        b_full = sem("b_full")
        decay_in = sem("decay_in")
        c_in = sem("c_in")
        drive_in = sem("drive_in")
        scanned = sem("scanned")
        kept = sem("kept")
        prod_in = sem("prod_in")
        prod_used = sem("prod_used")
        yt_in = sem("yt_in")
        yz_in = sem("yz_in")
        o_full = sem("o_full")

        def col(t, k):
            return t[:, ds(k, 1)] if not isinstance(k, int) else t[:, k:k + 1]

        def par(t, i, h):
            return t[:, i % 2, h, :]

        def par2(t, i):
            return t[:, i % 2, :, :]

        def chunk(i):
            return r[:, i % NCH, :]

        def place(i, use):
            if isinstance(i, int) and i in (-1, ITEMS - 1):
                return (FIRST_AT if i < 0 else LAST_AT)[use]
            return BANK_AT[use]

        def fill(i, use):
            if isinstance(i, int) and i < 0:
                return place(i, use)
            return NBU * i + len(FIRST_USES) + place(i, use)

        def shared(i, use):
            return bank(6 + place(i, use) % 2)

        Y, BB = (0, 1), (2, 3, 4, 5)

        with nc.Block() as block:

            @block.sync
            def _(sp):
                def load(j):
                    l = j // NCH
                    if not isinstance(j, int) or j > 0:
                        sp.wait_ge(bank_full, fill(j - 2, ("dt", 1)) + 1)
                    src = w_d[l, :, :]
                    sp.dma_start(wf[:, :], src).then_inc(front_in, 16)

                def load_out(j):
                    l = j // NCH
                    if not isinstance(j, int) or j > 0:
                        sp.wait_ge(o_full, j)
                    src = outw[l, :, :]
                    sp.dma_start(wo[:, :, :].rearrange("p h n -> p (h n)"), src).then_inc(out_in, 16)

                load(0)
                load_out(0)
                load(1)
                with sp.Fori(1, ITEMS - 1) as j:
                    load(j + 1)
                    load_out(j)
                load_out(ITEMS - 1)

            @block.tensor
            def _(pe):
                def take(i, use):
                    f = fill(i, use)
                    if not isinstance(f, int) or f >= 2:
                        pe.wait_ge(bank_free, f - 1)

                def bring(i, u):
                    g = UN * i + u
                    h, n = (u % UN) // NS, u % NS
                    ii = i + u // UN
                    if u % UN == 0:
                        pe.wait_ge(stack_in, ii + 1)
                    if not isinstance(g, int) or g >= NB:
                        pe.wait_ge(scanned, g - NB + 1)
                    pe.matmul(bank(BB[u % NB]), pick[:, n, :], par_s(ii), start=True, stop=True).then_inc(b_full, 1)

                def par_s(i):
                    return stack[:, i % 2, :]

                def bring_c(i, j, n, use):
                    take(i, use)
                    if n == 0:
                        pe.wait_ge(stack_in, j + 1)
                    pe.matmul(shared(i, use), pick[:, NS + n, :], par_s(j), start=True, stop=True)\
                      .then_inc(bank_full, 1)

                def add_up(i, u):
                    g, h, n = UN * i + u, u // NS, u % NS
                    if n == 0 and h == 0 and (not isinstance(i, int) or i > 0):
                        pe.wait_ge(yt_in, 2 * i - 1)
                    if n == 0 and h == 1 and (not isinstance(i, int) or i > 0):
                        pe.wait_ge(r_ready, NCH + i)
                    pe.wait_ge(prod_in, g + 1)
                    pe.matmul(bank(Y[h]), ident, prod[:, u % NP, :], start=(n == 0), stop=(n == NS - 1)).then_inc(prod_used, 1)

                def project(i):
                    pe.wait_ge(yz_in, 2 * i + 2)
                    pe.wait_ge(out_in, 16 * (i + 1))
                    for h in range(HV):
                        mm = pe.matmul(bank(Y[1]), wo[:, h, :], yz[:, h, :], start=(h == 0), stop=(h == HV - 1))
                    mm.then_inc(o_full, 1)

                def front(i, step):
                    j = i + 1
                    what, h = step[0], step[1]
                    if what == "stat":
                        take(i, step)
                        pe.wait_ge(squared, j + h + 2)
                        pe.matmul(shared(i, step), meanw, sq[:, :], start=True, stop=True).then_inc(bank_full, 1)
                    elif what == "z":
                        take(i, ("z", h))
                        if h == 0:
                            pe.wait_ge(hn_in, j + 1)
                            pe.wait_ge(front_in, 16 * (j + 1))
                        pe.matmul(shared(i, ("z", h)), wf[:, W_Z + h * P:W_Z + h * P + P], hn[:, KC - 1:KC - 1 + TC],
                                  start=True, stop=True).then_inc(bank_full, 1)
                    elif what == "x":
                        k = step[2]
                        if k == 0:
                            take(i, ("x", h))
                        o = W_TAP + k * DI + h * P
                        mm = pe.matmul(shared(i, ("x", h)), wf[:, o:o + P], hn[:, k:k + TC],
                                       start=(k == 0), stop=(k == KC - 1))
                        if k == KC - 1:
                            mm.then_inc(bank_full, 1)
                    elif what == "xd":
                        if h == 0:
                            take(i, ("xd", 0))
                            pe.wait_ge(xs_in, 2 * j + 2)
                        mm = pe.matmul(shared(i, ("xd", 0)), wf[:, W_X + h * P:W_X + h * P + P], par(xs, j, h),
                                       start=(h == 0), stop=(h == HV - 1))
                        if h == HV - 1:
                            mm.then_inc(bank_full, 1)
                    elif what == "dt":
                        take(i, ("dt", h))
                        if h == 0:
                            pe.wait_ge(xd_in, j + 1)
                        pe.matmul(shared(i, ("dt", h)), wf[:, W_DT + h * P:W_DT + h * P + P], xd[:, :],
                                  start=True, stop=True).then_inc(bank_full, 1)

                FRONT = {6: [("z", 0)], 7: [("z", 1)], 15: [("xd", 0)], 16: [("xd", 1)], 18: [("dt", 0)],
                         25: [("dt", 1)], 28: [("stat", 0)]}
                for h in range(HV):
                    for k, slot in enumerate((8, 9, 10, 10)):
                        FRONT.setdefault(slot + 3 * h, []).append(("x", h, k))

                def body(i, first, last):
                    for u in range(UN):
                        w = u - LAG
                        if w >= 0:
                            add_up(i, w)
                        elif not first:
                            add_up(i - 1, w + UN)
                        if u + LEAD_B < UN or not last:
                            bring(i, u + LEAD_B)
                        if not last:
                            for step in FRONT.get(u, []):
                                front(i, step)
                        for use in FILLS.get(u, []):
                            if use[0] == "C" and (use[1] >= CF or not last):
                                bring_c(i, i if use[1] >= CF else i + 1, use[1], use)
                        if u == 12 and not first:
                            project(i - 1)

                front(-1, ("stat", -1))
                for slot in sorted(FRONT):
                    for step in FRONT[slot]:
                        if step[0] != "stat":
                            front(-1, step)
                for n in range(CF):
                    bring_c(-1, 0, n, ("C", n))
                front(-1, ("stat", 0))
                for u in range(LEAD_B):
                    bring(0, u)
                body(0, True, False)
                with pe.Fori(1, ITEMS - 1) as i:
                    body(i, False, False)
                body(ITEMS - 1, False, True)
                for u in range(UN - LAG, UN):
                    add_up(ITEMS - 1, u)
                project(ITEMS - 1)

            @block.scalar
            def _(act):
                def decays(i, u):
                    g, h, n = UN * i + u, (u % UN) // NS, u % NS
                    ii = i + u // UN
                    if n == 0:
                        act.wait_ge(delta_in, HV * ii + h + 1)
                    if not isinstance(g, int) or g >= ND:
                        act.wait_ge(scanned, g - ND + 1)
                    act.activation(decay[:, u % ND, :], par(delta, ii, h), ACT.Exp,
                                   scale=col(V, VEC["A"] + (ii // NCH) * UN + h * NS + n)).then_inc(decay_in, 1)

                def copy_c(i, j, n, use):
                    act.wait_ge(bank_full, fill(i, use) + 1)
                    if not isinstance(j, int) or j > 0:
                        act.wait_ge(prod_in, UN * (j - 1) + NS + n + 1)
                    act.activation(c_all[:, n, :], shared(i, use), ACT.Copy).then_inc(c_in, 1)
                    act.wait_ge(c_in, NS * j + n + 1)
                    act.sem_inc(bank_free, 1)

                def front(i, step):
                    what, h = step
                    j = i + 1
                    l = j // NCH
                    if what == "square":
                        act.wait_ge(r_ready, j + h + 2)
                        act.activation(sq[:, :], chunk(j + h + 1), ACT.Square).then_inc(squared, 1)
                    elif what == "stat":
                        act.wait_ge(bank_full, fill(i, step) + 1)
                        act.activation(lnv[:, :], shared(i, step), ACT.Ln, bias=eps).then_inc(bank_free, 1)
                        act.wait_ge(bank_free, fill(i, step) + 1)
                        act.activation(rstd[:, :], lnv[:, :], ACT.Exp, scale=-0.5).then_inc(rstd_in, 1)
                    elif what == "z":
                        if h == 0 and (not isinstance(j, int) or j > 1):
                            act.wait_ge(yz_in, 2 * j - 2)
                        act.wait_ge(bank_full, fill(i, ("z", h)) + 1)
                        act.activation(par(zs, j, h), shared(i, ("z", h)), ACT.Copy).then_inc(bank_free, 1)
                    elif what == "silu":
                        for h in range(HV):
                            act.wait_ge(bank_full, fill(i, ("x", h)) + 1)
                            act.activation(par(xs, j, h), shared(i, ("x", h)), ACT.Silu,
                                           bias=col(V, VEC["conv_b"] + l * HV + h)).then_inc(xs_in, 1)
                            act.wait_ge(xs_in, 2 * j + h + 1)
                            act.sem_inc(bank_free, 1)
                        act.activation(par2(zs, j), par2(zs, j), ACT.Silu).then_inc(z_in, 1)
                        act.preload_act_table_set(LOG_EXP)
                    elif what == "xd":
                        act.wait_ge(bank_full, fill(i, ("xd", 0)) + 1)
                        act.activation(xd[:, :], shared(i, ("xd", 0)), ACT.Copy).then_inc(xd_in, 1)
                        act.wait_ge(xd_in, j + 1)
                        act.sem_inc(bank_free, 1)
                    elif what == "dt":
                        act.wait_ge(bank_full, fill(i, ("dt", h)) + 1)
                        if not isinstance(j, int) or j > 0:
                            act.wait_ge(delta_in, HV * (j - 1) + h + 1)
                        dtb = col(V, VEC["dt_b"] + l * HV + h)
                        act.activation(ea[:, h, :], shared(i, ("dt", h)), ACT.Abs, bias=dtb).then_inc(abs_in, 1)
                        act.activation(pos[:, h, :], shared(i, ("dt", h)), ACT.Relu, bias=dtb).then_inc(bank_free, 1)
                    elif what == "exp":
                        act.wait_ge(abs_in, HV * j + h + 1)
                        act.activation(ea[:, h, :], ea[:, h, :], ACT.Exp, scale=-1.0).then_inc(exp_in, 1)
                        act.wait_ge(exp_in, HV * j + h + 1)
                        act.activation(small[:, h, :], ea[:, h, :], ACT.Square, scale=SQRT_HALF).then_inc(half_sq, 1)
                    elif what == "ln":
                        act.wait_ge(plus_in, HV * j + h + 1)
                        act.activation(lg[:, h, :], w1p[:, h, :], ACT.Ln).then_inc(ln_in, 1)

                FRONT = {14: [("silu", 0)], 17: [("xd", 0)], 19: [("dt", 0)], 20: [("exp", 0)], 22: [("ln", 0)],
                         26: [("dt", 1)], 27: [("exp", 1), ("square", 0)], 29: [("ln", 1)]}

                def body(i, first, last):
                    for u in range(UN):
                        if u + LEAD_A < UN or not last:
                            decays(i, u + LEAD_A)
                        if u == 0 and not first:
                            copy_c(i - 1, i, CF - 1, ("C", CF - 1))
                        for use in FILLS.get(u - 1, []):
                            if use[0] == "C" and (use[1] >= CF or not last):
                                copy_c(i, i if use[1] >= CF else i + 1, use[1], use)
                            elif use[0] in ("stat", "z", "dt") and use != ("dt", 0) and not last:
                                front(i, use)
                        if not last:
                            for step in FRONT.get(u, []):
                                if step != ("dt", 1):
                                    front(i, step)

                act.preload_act_table_set(LOG_EXP)
                front(-1, ("square", -1))
                front(-1, ("stat", -1))
                for h in range(HV):
                    front(-1, ("z", h))
                front(-1, ("silu", 0))
                front(-1, ("xd", 0))
                for h in range(HV):
                    front(-1, ("dt", h))
                for h in range(HV):
                    front(-1, ("exp", h))
                for h in range(HV):
                    front(-1, ("ln", h))
                front(-1, ("square", 0))
                for n in range(CF):
                    copy_c(-1, 0, n, ("C", n))
                front(-1, ("stat", 0))
                for u in range(LEAD_A):
                    decays(0, u)
                body(0, True, False)
                with act.Fori(1, ITEMS - 1) as i:
                    body(i, False, False)
                body(ITEMS - 1, False, True)

            @block.vector
            def _(dve):
                def drive(i, u):
                    g, h = UN * i + u, (u % UN) // NS
                    ii = i + u // UN
                    if u % NS == 0:
                        dve.wait_ge(du_in, HV * ii + h + 1)
                    dve.wait_ge(b_full, g + 1)
                    dve.tensor_tensor(bank(BB[u % NB]), par(du, ii, h), bank(BB[u % NB]), ALU.mult).then_inc(drive_in, 1)

                def scan(i, u, keeps):
                    g, h, n = UN * i + u, u // NS, u % NS
                    dve.wait_ge(decay_in, g + 1)
                    dve.wait_ge(drive_in, g + 1)
                    if not isinstance(g, int) or g >= NS:
                        dve.wait_ge(prod_in, g - NS + 1)
                    if n == 0 and (not isinstance(g, int) or g > 0):
                        dve.wait_ge(kept, 2 * i + h if h == 0 or keeps else 2 * i)
                    dve.tensor_tensor_scan(h_ring[:, n, :], decay[:, u % ND, :], bank(BB[u % NB]),
                                           h_init[:, h, n:n + 1], ALU.mult, ALU.add).then_inc(scanned, 1)

                def keep(i, h):
                    j = i + 1
                    dve.wait_ge(scanned, UN * i + NS * (h + 1))
                    dve.tensor_scalar(h_init[:, h, :], h_ring[:, :, TC - 1:TC].rearrange("p n a -> p (n a)"),
                                      col(Cn, CON["keep"] + j), None, ALU.mult).then_inc(kept, 1)

                def gate(i, h):
                    dve.wait_ge(prod_used, UN * i + NS * (h + 1))
                    dve.scalar_tensor_tensor(yt[:, :], par(xs, i, h), col(V, VEC["D"] + (i // NCH) * HV + h),
                                             bank(Y[h]), ALU.mult, ALU.add).then_inc(yt_in, 1)
                    dve.wait_ge(yt_in, 2 * i + h + 1)
                    if h == 0 and (not isinstance(i, int) or i > 0):
                        dve.wait_ge(o_full, i)
                    dve.tensor_tensor(yz[:, h, :], yt[:, :], par(zs, i, h), ALU.mult).then_inc(yz_in, 1)

                def residual(i):
                    dve.wait_ge(o_full, i + 1)
                    dve.tensor_tensor(chunk(i), chunk(i), bank(Y[1]), ALU.add).then_inc(r_ready, 1)

                def front(i, step, h=0):
                    j = i + 1
                    l = j // NCH
                    if step == "hn":
                        if not isinstance(j, int) or j > 0:
                            dve.wait_ge(bank_full, fill(i - 1, ("x", 1)) + 1)
                        dve.tensor_scalar(hn[:, 0:KC - 1], hn[:, TC:TC + KC - 1], col(Cn, CON["keep"] + j), None,
                                          ALU.mult).then_inc(hist_in, 1)
                        dve.wait_ge(hist_in, j + 1)
                        dve.wait_ge(rstd_in, j + 1)
                        dve.scalar_tensor_tensor(hn[:, KC - 1:KC - 1 + TC], chunk(j), col(V, VEC["block_norm"] + l),
                                                 rstd[:, :], ALU.mult, ALU.mult).then_inc(hn_in, 1)
                    elif step == "hi":
                        dve.wait_ge(xd_in, j + 1)
                        dve.tensor_copy(par_s(j, 0, 96), xd[0:96, :]).then_inc(part_in, 1)
                    elif step == "rest":
                        dve.wait_ge(part_in, 3 * j + 1)
                        dve.tensor_tensor(rest[:, :], xd[0:96, :], par_s(j, 0, 96), ALU.subtract).then_inc(part_in, 1)
                    elif step == "mid":
                        dve.wait_ge(part_in, 3 * j + 2)
                        dve.tensor_copy(mid[:, :], rest[:, :]).then_inc(part_in, 1)
                    elif step == "lo":
                        dve.wait_ge(part_in, 3 * j + 3)
                        dve.tensor_copy(par_s(j, 32, 64), mid[32:64, :])
                        dve.tensor_tensor(par_s(j, 64, 96), rest[64:96, :], mid[64:96, :], ALU.subtract)\
                           .then_inc(stack_in, 1)
                    elif step == "plus":
                        dve.wait_ge(exp_in, HV * j + h + 1)
                        dve.tensor_scalar(w1p[:, h, :], ea[:, h, :], 1.0, None, ALU.add).then_inc(plus_in, 1)
                    elif step == "err":
                        dve.wait_ge(ln_in, HV * j + h + 1)
                        dve.scalar_tensor_tensor(w1p[:, h, :], w1p[:, h, :], -1.0, ea[:, h, :], ALU.add, ALU.subtract)\
                           .then_inc(err_in, 1)
                    elif step == "diff":
                        dve.wait_ge(base_in, HV * j + h + 1)
                        dve.tensor_tensor(lg[:, h, :], lg[:, h, :], w1p[:, h, :], ALU.subtract).then_inc(diff_in, 1)
                    elif step == "choose":
                        dve.wait_ge(diff_in, HV * j + h + 1)
                        dve.scalar_tensor_tensor(lg[:, h, :], ea[:, h, :], SMALL, lg[:, h, :], ALU.is_ge, ALU.mult)\
                           .then_inc(chosen, 1)
                    elif step == "delta":
                        dve.wait_ge(chosen, HV * j + h + 1)
                        dve.tensor_tensor(par(delta, j, h), lg[:, h, :], small_pos[:, h, :], ALU.add)\
                           .then_inc(delta_in, 1)
                    elif step == "du":
                        dve.wait_ge(delta_in, HV * j + h + 1)
                        dve.tensor_tensor(par(du, j, h), par(delta, j, h), par(xs, j, h), ALU.mult).then_inc(du_in, 1)

                def par_s(i, a, b):
                    return stack[a:b, i % 2, :]

                FRONT = {1: [("hn", 0)], 18: [("hi", 0)], 19: [("rest", 0)], 20: [("mid", 0)],
                         21: [("lo", 0), ("plus", 0)], 23: [("err", 0)], 25: [("diff", 0)], 26: [("choose", 0)],
                         27: [("delta", 0)], 28: [("du", 0), ("plus", 1)], 30: [("err", 1)]}
                LATE = {2: "diff", 3: "choose", 4: "delta", 5: "du"}

                def body(i, first, last):
                    for u in range(UN):
                        if u + 1 < UN or not last:
                            drive(i, u + 1)
                        if u == 0 and not first:
                            keep(i - 1, 1)
                        if u == NS and not last:
                            keep(i, 0)
                        scan(i, u, not last)
                        if u in LATE and not first:
                            front(i - 1, LATE[u], 1)
                        if u == 6 and not first:
                            gate(i - 1, 1)
                        if u == 14 and not first:
                            residual(i - 1)
                        if u == 22:
                            gate(i, 0)
                        if not last:
                            for step, h in FRONT.get(u, []):
                                front(i, step, h)

                for slot in sorted(FRONT):
                    for step, h in FRONT[slot]:
                        front(-1, step, h)
                for step in LATE.values():
                    front(-1, step, 1)
                drive(0, 0)
                body(0, True, False)
                with dve.Fori(1, ITEMS - 1) as i:
                    body(i, False, False)
                body(ITEMS - 1, False, True)
                gate(ITEMS - 1, 1)
                residual(ITEMS - 1)

            @block.gpsimd
            def _(pool):
                def weigh(i, u):
                    g, h, n = UN * i + u, u // NS, u % NS
                    if h == 0:
                        pool.wait_ge(c_in, NS * i + n + 1)
                    pool.wait_ge(scanned, g + 1)
                    if not isinstance(g, int) or g >= NP:
                        pool.wait_ge(prod_used, g - NP + 1)
                    pool.tensor_tensor(prod[:, u % NP, :], h_ring[:, n, :], c_all[:, n, :], ALU.mult).then_inc(prod_in, 1)

                def front(i, step, h):
                    j = i + 1
                    if step == "small":
                        pool.wait_ge(half_sq, HV * j + h + 1)
                        pool.tensor_tensor(small[:, h, :], ea[:, h, :], small[:, h, :], ALU.subtract)\
                            .then_inc(small_in, 1)
                    elif step == "small_pos":
                        pool.wait_ge(small_in, HV * j + h + 1)
                        pool.tensor_tensor(small_pos[:, h, :], small[:, h, :], pos[:, h, :], ALU.add)
                    elif step == "base":
                        pool.wait_ge(err_in, HV * j + h + 1)
                        pool.tensor_tensor(w1p[:, h, :], w1p[:, h, :], small[:, h, :], ALU.add).then_inc(base_in, 1)

                FRONT = {21: ("small", 0), 22: ("small_pos", 0), 23: ("base", 0), 28: ("small", 1),
                         29: ("small_pos", 1), 30: ("base", 1)}

                def body(i, last):
                    for u in range(UN):
                        weigh(i, u)
                        if not last and u in FRONT:
                            front(i, *FRONT[u])

                for slot in sorted(FRONT):
                    front(-1, *FRONT[slot])
                body(0, False)
                with pool.Fori(1, ITEMS - 1) as i:
                    body(i, False)
                body(ITEMS - 1, True)

        tail(nc, ctx, sem, bank, v, V, Cn, r, ident, meanw, center, eps, h0_d, s_d, x_d, y_d, sort, fc1, fc2, wr, br, wexp, out,
             h_ring, c_all, decay, prod, delta, du, xs, zs, sb)


def tail(nc, ctx, sem, bank, v, V, Cn, r, ident, meanw, center, eps, h0_d, s_d, x_d, y_d, sort, fc1, fc2, wr, br, wexp, out,
         h_ring, c_all, decay, prod, delta, du, xs, zs, sb):
    names = ["s_in", "h0_in", "sqd", "var", "rst", "logd", "cen", "scl", "hid", "hsum", "mlp1", "g_in", "mlp2", "a1", "h1",
             "xn", "rt", "route", "turned", "flat"]
    q = {n: [sem(f"t_{n}_s{s}") for s in range(2)] for n in names}
    w_loaded = sem("t_w_loaded")
    zero_in = sem("zero_in")
    zeroed = sem("zeroed")

    fc1_s = decay[:, 0, :]
    fc2_s = decay[:, 1, :].rearrange("p (k o) -> p k o", k=HB)
    wr_s = decay[:, 2, 0:E]
    br_s = decay[:, 2, E:2 * E]
    zero = decay[:, 3, 0:P]
    So = prod[:, 2:4, :].rearrange("p a b -> p (a b)")[:, 0:NSORT]
    D = [delta[:, s, :, :] for s in range(2)]
    s_in = [D[s][:, 0, :] for s in range(2)]
    h0_in = [D[s][:, 1, :] for s in range(2)]
    sqb = [du[:, s, 0, :] for s in range(2)]
    lnb = [du[:, s, 1, :] for s in range(2)]
    rsb = [xs[:, s, 0, :] for s in range(2)]
    tmp = [xs[:, s, 1, :] for s in range(2)]
    hsum = [zs[:, s, 0, :] for s in range(2)]
    xn = [zs[:, s, 1, :] for s in range(2)]
    gel = [h_ring[:, 4 * s:4 * s + 4, :] for s in range(2)]
    h1 = [prod[:, s, :] for s in range(2)]
    xn_tok = c_all[:, 0:NCH, :]
    h1_tok = c_all[:, NCH:2 * NCH, :]
    route = sb("route", [P, 2, 3, TT, E])
    top = sb("top", [P, 2, NCH, TT])
    one_hot = sb("one_hot", [P, NCH, TT * E])
    lg = [route[:, s, 0] for s in range(2)]
    eq = [route[:, s, 1] for s in range(2)]
    rk = [route[:, s, 2] for s in range(2)]
    rank = Cn[:, CON["rank"]:CON["rank"] + E].unsqueeze(1).to_broadcast([P, TT, E])

    def chunk_d(t, k, s):
        return t[k + s * CPB, :, :]

    def chunk(k, s):
        return r[:, k + s * CPB, :]

    with nc.Block() as block:

        @block.sync
        def _(sp):
            sp.dma_start(fc1_s, fc1).then_inc(w_loaded, 16)
            sp.dma_start(fc2_s, fc2).then_inc(w_loaded, 16)
            sp.dma_start(wr_s, wr).then_inc(w_loaded, 16)
            sp.dma_start(br_s, br.partition_broadcast(P)).then_inc(w_loaded, 16)
            sp.dma_start(So, sort).then_inc(w_loaded, 16)
            sp.wait_ge(zero_in, 1)
            sp.dma_start(x_d.rearrange("(p n) c -> p n c", p=P), zero.unsqueeze(1).to_broadcast([P, NT * ET // P, P]))\
              .then_inc(zeroed, 16)
            def one_round(k):
                for s in range(2):
                    if later(k):
                        sp.wait_ge(q["a1"][s], k)
                        sp.wait_ge(q["h1"][s], k)
                    sp.dma_start(s_in[s], chunk_d(s_d, k, s)).then_inc(q["s_in"][s], 16)
                    sp.dma_start(h0_in[s], chunk_d(h0_d, k, s)).then_inc(q["h0_in"][s], 16)
            rounds(sp, one_round)
            sp.wait_ge(zeroed, 16)

        @block.tensor
        def _(pe):
            pe.wait_ge(w_loaded, 5 * 16)
            def one_round(k):
                def each(ready, f, count=None):
                    for s in range(2):
                        pe.wait_ge(q[ready][s], k + 1 if count is None else count)
                        f(s)
                each("sqd", lambda s: pe.matmul(bank(4 * s + 2), meanw, sqb[s], start=True, stop=True)
                     .then_inc(q["var"][s], 1), 3 * k + 1)
                each("hsum", lambda s: pe.matmul(bank(4 * s + 1), center, hsum[s], start=True, stop=True)
                     .then_inc(q["cen"][s], 1))
                each("sqd", lambda s: pe.matmul(bank(4 * s + 2), meanw, sqb[s], start=True, stop=True)
                     .then_inc(q["var"][s], 1), 3 * k + 2)
                for s in range(2):
                    pe.wait_ge(q["xn"][s], k + 1)
                    for b in range(HB):
                        if b >= 2:
                            pe.wait_ge(q["g_in"][s], HB * k + b - 1)
                        pe.matmul(bank(4 * s + (0, 3)[b % 2]), fc1_s[:, b * P:(b + 1) * P], tmp[s], start=True,
                                  stop=True).then_inc(q["mlp1"][s], 1)
                for s in range(2):
                    for b in range(HB):
                        pe.wait_ge(q["g_in"][s], HB * k + b + 1)
                        mm = pe.matmul(bank(4 * s + 2), fc2_s[:, b, :], gel[s][:, b, :], start=(b == 0),
                                       stop=(b == HB - 1))
                    mm.then_inc(q["mlp2"][s], 1)
                each("h1", lambda s: pe.matmul(bank(4 * s + 1), center, h1[s], start=True, stop=True)
                     .then_inc(q["cen"][s], 1))
                each("sqd", lambda s: pe.matmul(bank(4 * s + 2), meanw, sqb[s], start=True, stop=True)
                     .then_inc(q["var"][s], 1), 3 * k + 3)
                for s in range(2):
                    pe.wait_ge(q["scl"][s], 2 * k + 2)
                    for t in range(TT):
                        mm = pe.matmul(bank(4 * s)[:, t * E:(t + 1) * E], xn[s][:, t * P:(t + 1) * P], wr_s,
                                       start=True, stop=True)
                    mm.then_inc(q["rt"][s], 1)
                for s in range(2):
                    for src, b in ((h1, 1), (xn, 3)):
                        for t in range(TT):
                            mm = pe.transpose(bank(4 * s + b)[:, t * P:(t + 1) * P], src[s][:, t * P:(t + 1) * P], ident)
                        mm.then_inc(q["turned"][s], 1)
            rounds(pe, one_round)

        @block.scalar
        def _(act):
            def one_round(k):
                act.preload_act_table_set(LOG_EXP)
                def rs(m, s):
                    act.wait_ge(q["var"][s], 3 * k + m + 1)
                    act.activation(lnb[s], bank(4 * s + 2), ACT.Ln, bias=eps).then_inc(q["logd"][s], 1)
                    act.wait_ge(q["logd"][s], 3 * k + m + 1)
                    act.activation(rsb[s], lnb[s], ACT.Exp, scale=-0.5).then_inc(q["rst"][s], 1)

                def square(m, s):
                    act.wait_ge(q["cen"][s], 2 * k + m)
                    act.activation(sqb[s], bank(4 * s + 1), ACT.Square).then_inc(q["sqd"][s], 1)

                for s in range(2):
                    act.activation(sqb[s], chunk(k, s), ACT.Square).then_inc(q["sqd"][s], 1)
                for s in range(2):
                    rs(0, s)
                for s in range(2):
                    square(1, s)
                for s in range(2):
                    rs(1, s)
                for s in range(2):
                    act.wait_ge(q["scl"][s], 2 * k + 1)
                    act.activation(tmp[s], xn[s], ACT.Identity, scale=v("ln2_w"), bias=v("ln2_b"))\
                       .then_inc(q["xn"][s], 1)
                for s in range(2):
                    for b in range(HB):
                        act.wait_ge(q["mlp1"][s], HB * k + b + 1)
                        act.activation(gel[s][:, b, :], bank(4 * s + (0, 3)[b % 2]), ACT.Gelu_apprx_tanh,
                                       bias=v("fc1_b", b)).then_inc(q["g_in"][s], 1)
                act.preload_act_table_set(LOG_EXP)
                for s in range(2):
                    square(2, s)
                for s in range(2):
                    rs(2, s)
                for s in range(2):
                    for m, dst in enumerate((h1_tok, xn_tok)):
                        act.wait_ge(q["turned"][s], 2 * k + m + 1)
                        act.activation(dst[:, k + s * CPB, :], bank(4 * s + (1, 3)[m]), ACT.Identity)\
                           .then_inc(q["flat"][s], 1)
            rounds(act, one_round)

        @block.vector
        def _(dve):
            dve.memset(zero, 0.0).then_inc(zero_in, 1)
            dve.wait_ge(w_loaded, 5 * 16)
            def one_round(k):
                def each(f):
                    for s in range(2):
                        f(s)

                def hidden(s):
                    dve.wait_ge(q["rst"][s], 3 * k + 1)
                    dve.scalar_tensor_tensor(tmp[s], chunk(k, s), v("norm_f"), rsb[s], ALU.mult, ALU.mult)\
                       .then_inc(q["hid"][s], 1)

                def hsums(s):
                    dve.wait_ge(q["hid"][s], k + 1)
                    dve.wait_ge(q["s_in"][s], 16 * (k + 1))
                    dve.tensor_tensor(hsum[s], tmp[s], s_in[s], ALU.add).then_inc(q["hsum"][s], 1)

                def scaled(m, dst):
                    def f(s):
                        dve.wait_ge(q["rst"][s], 3 * k + m + 1)
                        dve.tensor_tensor(dst[s], bank(4 * s + 1), rsb[s], ALU.mult).then_inc(q["scl"][s], 1)
                    return f

                def a1(s):
                    dve.wait_ge(q["mlp2"][s], k + 1)
                    dve.scalar_tensor_tensor(hsum[s], bank(4 * s + 2), v("fc2_b"), hsum[s], ALU.add, ALU.add)\
                       .then_inc(q["a1"][s], 1)

                def h1s(s):
                    dve.wait_ge(q["a1"][s], k + 1)
                    dve.wait_ge(q["h0_in"][s], 16 * (k + 1))
                    dve.tensor_tensor(h1[s], hsum[s], h0_in[s], ALU.add).then_inc(q["h1"][s], 1)

                each(hidden)
                each(hsums)
                each(scaled(1, xn))
                each(a1)
                each(h1s)
                each(scaled(2, xn))
                c = [k + s * CPB for s in range(2)]
                for s in range(2):
                    dve.wait_ge(q["rt"][s], k + 1)
                    dve.tensor_tensor(lg[s], bank(4 * s)[:, 0:TT * E].rearrange("p (t e) -> p t e", t=TT),
                                      br_s.unsqueeze(1).to_broadcast([P, TT, E]), ALU.add).then_inc(q["route"][s], 1)
                for s in range(2):
                    dve.wait_ge(q["route"][s], 6 * k + 1)
                    dve.reduce_max(top[:, 0, c[s], :], lg[s], AX).then_inc(q["route"][s], 1)
                for s in range(2):
                    dve.wait_ge(q["route"][s], 6 * k + 2)
                    dve.tensor_tensor(eq[s], lg[s], top[:, 0, c[s], :].unsqueeze(2).to_broadcast([P, TT, E]),
                                      ALU.is_equal).then_inc(q["route"][s], 1)
                for s in range(2):
                    dve.wait_ge(q["route"][s], 6 * k + 3)
                    dve.tensor_tensor(rk[s], eq[s], rank, ALU.mult).then_inc(q["route"][s], 1)
                for s in range(2):
                    dve.wait_ge(q["route"][s], 6 * k + 4)
                    dve.reduce_max(top[:, 1, c[s], :], rk[s], AX).then_inc(q["route"][s], 1)
                for s in range(2):
                    dve.wait_ge(q["route"][s], 6 * k + 5)
                    dve.tensor_tensor(one_hot[:, c[s], :].rearrange("p (t e) -> p t e", e=E), rk[s],
                                      top[:, 1, c[s], :].unsqueeze(2).to_broadcast([P, TT, E]),
                                      ALU.is_equal).then_inc(q["route"][s], 1)
            rounds(dve, one_round)

    experts(nc, sem, sb, bank, So, ident, x_d, y_d, wexp, out, h_ring, xn_tok, h1_tok, prod, delta, du, xs, zs, top, one_hot)


def experts(nc, sem, sb, bank, So, ident, x_d, y_d, wexp, out, h_ring, xn_tok, h1_tok, prod, delta, du, xs, zs, top, one_hot):
    ones = So[:, SORT["ones"]:SORT["ones"] + P]
    before = So[:, SORT["before"]:SORT["before"] + P]
    multiple = So[:, SORT["multiple"]:SORT["multiple"] + TOK // ET]
    number = So[:, SORT["number"]:SORT["number"] + NT]
    row = So[:, SORT["row"]:SORT["row"] + 1]
    restart = So[:, SORT["restart"]:SORT["restart"] + E * RT]
    counts = prod[:, 4:6, :].rearrange("p a b -> p (a b)")[:, 0:4 * RT * E].rearrange("p (a n) -> p a n", a=4)
    few = prod[:, 6, 0:3 * E].rearrange("p (a e) -> p a e", a=3)
    cmp_k = prod[:, 6, 128:128 + E * (TOK // ET)].rearrange("p (e n) -> p e n", e=E)
    cmp_t = prod[:, 6, 256:256 + NT * E].rearrange("p (t e) -> p t e", e=E)
    tile_e = prod[:, 7, 0:3 * NT].rearrange("p (a t) -> p a t", a=3)
    slot_f = prod[:, 7, 128:128 + RT]
    slot = sb("slot", [P, RT], U32)
    w_row = sb("w_row", [P, NT], U32)
    gate = prod[:, 7, 256:256 + 4 * RT].rearrange("p (a t) -> p a t", a=4)

    def te(t):
        return t.rearrange("p (t e) -> p t e", e=E)

    hr = h_ring[:, :, :].rearrange("p a b -> p (a b)")
    w_ring = [hr[:, i * NX:(i + 1) * NX] for i in range(4)]
    x_ring = [xs[:, i // 2, i % 2, 0:ET].rearrange("p (t c) -> p t c", c=P) for i in range(4)]
    x_t = [zs[:, i, 0, 0:ET] for i in range(2)]
    y_s = [zs[:, i, 1, 0:ET].rearrange("p (t c) -> p t c", c=P) for i in range(2)]
    hid = [t[:, :, :, :].rearrange("p a b c -> p (a b c)")[:, 0:HB * ET].rearrange("p (b c) -> p b c", b=HB)
           for t in (delta, du)]
    back = xn_tok
    sums = sem("sums")
    counted = sem("counted")
    zero_diff = sem("zero_diff")
    gate_exp = sem("gate_exp")
    gate_in = sem("gate_in")
    slots_in = sem("slots_in")
    rows_in = sem("rows_in")
    scattered = sem("scattered")
    fetched = [sem(f"fetched{i}") for i in range(4)]
    x_in = [sem(f"e_x_in{i}") for i in range(4)]
    turned = sem("e_turned")
    x_ready = sem("e_x_ready")
    up = sem("e_up")
    relu_in = sem("e_relu")
    down = sem("e_down")
    y_made = sem("e_y_made")
    y_kept = [sem(f"e_y_kept{i}") for i in range(2)]
    taken = [sem(f"taken{c}") for c in range(NCH)]
    mixed = sem("mixed")
    kept = sem("out_kept")

    def tile_rounds(eng, step):
        for i in range(4):
            step(0, i)
        with eng.Fori(1, NT // 4) as k:
            for i in range(4):
                step(k, i)
        for i in range(NT % 4):
            step(NT // 4, i)

    def tiles(t_d):
        return t_d.rearrange("(j t p) c -> j p t c", p=P, t=ET // P)

    def fixed(j):
        return isinstance(j, int)

    with nc.Block() as block:

        @block.gpsimd
        def _(pool):
            def fetch(j):
                if j >= 4:
                    pool.wait_ge(y_made, j - 3)
                pool.indirect_dma_start(out=w_ring[j % 4], out_offset=None, in_=wexp,
                                        in_offset=bass.IndirectOffsetOnAxis(ap=w_row[:, j:j + 1], axis=0))\
                    .then_inc(fetched[j % 4], 16)
            pool.wait_ge(slots_in, 1)
            for t in range(RT):
                pool.indirect_dma_start(out=x_d, out_offset=bass.IndirectOffsetOnAxis(ap=slot[:, t:t + 1], axis=0),
                                        in_=xn_tok[:, t // TT, (t % TT) * P:(t % TT + 1) * P], in_offset=None)\
                    .then_inc(scattered, 16)
                if t == RT // 2:
                    pool.wait_ge(rows_in, 1)
                    for j in range(4):
                        fetch(j)
            for j in range(4, NT):
                fetch(j)
            pool.wait_ge(scattered, 16 * RT)
            pool.wait_ge(y_kept[0], 16 * ((NT + 1) // 2))
            pool.wait_ge(y_kept[1], 16 * (NT // 2))
            for t in range(RT):
                pool.indirect_dma_start(out=back[:, t // TT, (t % TT) * P:(t % TT + 1) * P], out_offset=None, in_=y_d,
                                        in_offset=bass.IndirectOffsetOnAxis(ap=slot[:, t:t + 1], axis=0))\
                    .then_inc(taken[t // TT], 16)

        @block.sync
        def _(sp):
            def load(k, i):
                j = 4 * k + i
                sp.dma_start(x_ring[i % 4], tiles(x_d)[j, :, :, :]).then_inc(x_in[i % 4], 16)

            def store(k, i):
                j = 4 * k + i
                sp.wait_ge(y_made, j + 1)
                sp.dma_start(tiles(y_d)[j, :, :, :], y_s[i % 2])\
                  .then_inc(y_kept[i % 2], 16)

            sp.wait_ge(scattered, 16 * RT)
            for j in range(3):
                load(0, j)
            def step(k, i):
                j = 4 * k + i
                if not fixed(j) or j + 3 < NT:
                    if not fixed(j) or j > 0:
                        sp.wait_ge(turned, j)
                    load(k, i + 3)
                if not fixed(j) or j > 0:
                    store(k, i - 1)
            tile_rounds(sp, step)
            store(NT // 4, NT % 4 - 1)
            for c in range(NCH):
                sp.wait_ge(mixed, TT * (c + 1))
                sp.dma_start(out[c, :, :, :].rearrange("t p c -> p t c"),
                             back[:, c, :].rearrange("p (t c) -> p t c", t=TT)).then_inc(kept, 16)
            sp.wait_ge(kept, 16 * NCH)

        @block.tensor
        def _(pe):
            hot = one_hot[:, :, :].rearrange("p a b -> p (a b)")
            pe.matmul(bank(0)[:, 0:RT * E], before, hot, start=True, stop=True)
            pe.matmul(bank(1)[:, 0:RT * E], ones, hot, start=True, stop=True).then_inc(counted, 1)

            def turn(k, i):
                j = 4 * k + i
                pe.wait_ge(x_in[i % 4], 16 * (k + i // 4 + 1))
                if not fixed(j) or j >= 2:
                    pe.wait_ge(x_ready, j - 1)
                for t in range(ET // P):
                    mm = pe.transpose(bank(i % 2)[:, t * P:(t + 1) * P], x_ring[i % 4][:, t, :], ident)
                mm.then_inc(turned, 1)

            def ups(k, i):
                j = 4 * k + i
                pe.wait_ge(fetched[i % 4], 16 * (k + i // 4 + 1))
                pe.wait_ge(x_ready, j + 1)
                if not fixed(j) or j >= 2:
                    pe.wait_ge(relu_in, HB * (j - 1))
                for b in range(HB):
                    o = 2 + 2 * (i % 2) + b // 2
                    mm = pe.matmul(bank(o)[:, b % 2 * ET:(b % 2 + 1) * ET], w_ring[i % 4][:, b * P:(b + 1) * P],
                                   x_t[i % 2], start=True, stop=True)
                    if b % 2:
                        mm.then_inc(up, 1)

            def downs(k, i):
                j = 4 * k + i
                pe.wait_ge(relu_in, HB * (j + 1))
                if not fixed(j) or j >= 2:
                    pe.wait_ge(y_made, j - 1)
                for t in range(ET // P):
                    for b in range(HB):
                        o = HB * P + b * P
                        mm = pe.matmul(bank(6 + i % 2)[:, t * P:(t + 1) * P], hid[i % 2][:, b, t * P:(t + 1) * P],
                                       w_ring[i % 4][:, o:o + P], start=(b == 0), stop=(b == HB - 1))
                mm.then_inc(down, 1)

            pe.wait_ge(sums, 9)
            turn(0, 0)
            def step(k, i):
                j = 4 * k + i
                if not fixed(j) or j + 1 < NT:
                    turn(k, i + 1)
                ups(k, i)
                if not fixed(j) or j > 0:
                    downs(k, i - 1)
            tile_rounds(pe, step)
            downs(NT // 4, NT % 4 - 1)

        @block.scalar
        def _(act):
            act.wait_ge(zero_diff, 1)
            act.activation(gate[:, 1, :], gate[:, 0, :], ACT.Exp).then_inc(gate_exp, 1)
            def step(k, i):
                j = 4 * k + i
                for b in range(HB):
                    if b % 2 == 0:
                        act.wait_ge(up, HB // 2 * j + b // 2 + 1)
                    if b == 0 and (not fixed(j) or j >= 2):
                        act.wait_ge(down, j - 1)
                    o = 2 + 2 * (i % 2) + b // 2
                    act.activation(hid[i % 2][:, b, :], bank(o)[:, b % 2 * ET:(b % 2 + 1) * ET], ACT.Relu,
                                   bias=w_ring[i % 4][:, 2 * HB * P + b:2 * HB * P + b + 1]).then_inc(relu_in, 1)
            tile_rounds(act, step)

        @block.vector
        def _(dve):
            done = 0
            def chain(op):
                nonlocal done
                op.then_inc(sums, 1)
                done += 1
                dve.wait_ge(sums, done)
            dve.wait_ge(counted, 1)
            chain(dve.tensor_copy(counts[:, 0, :].rearrange("p (e t) -> p e t", e=E),
                                  bank(1)[:, 0:RT * E].rearrange("p (t e) -> p e t", e=E)))
            chain(dve.tensor_tensor_scan(counts[:, 1, :], restart, counts[:, 0, :], 0.0, ALU.mult, ALU.add))
            total = counts[:, 1, :].rearrange("p (e t) -> p e t", e=E)
            chain(dve.tensor_tensor(cmp_k[:, :, :], total[:, :, RT - 1:RT].to_broadcast([P, E, TOK // ET]),
                                    multiple.unsqueeze(1).to_broadcast([P, E, TOK // ET]), ALU.is_gt))
            chain(dve.reduce_sum(few[:, 0, :], cmp_k[:, :, :], AX))
            chain(dve.tensor_tensor_scan(few[:, 1, :], ones[:, 0:E], few[:, 0, :], 0.0, ALU.mult, ALU.add))
            chain(dve.tensor_tensor(few[:, 2, :], few[:, 1, :], few[:, 0, :], ALU.subtract))
            chain(dve.scalar_tensor_tensor(te(counts[:, 2, :]), few[:, 2, :].unsqueeze(1).to_broadcast([P, RT, E]),
                                           float(ET), total.rearrange("p e t -> p t e"), ALU.mult, ALU.add))
            chain(dve.tensor_tensor(te(counts[:, 2, :]), te(counts[:, 2, :]),
                                    counts[:, 0, :].rearrange("p (e t) -> p t e", e=E), ALU.subtract))
            chain(dve.tensor_tensor(counts[:, 3, :], bank(0)[:, 0:RT * E], counts[:, 2, :], ALU.add))
            chain(dve.tensor_tensor(counts[:, 3, :], counts[:, 3, :], one_hot[:, :, :].rearrange("p a b -> p (a b)"),
                                    ALU.mult))
            chain(dve.reduce_sum(slot_f[:, :], te(counts[:, 3, :]), AX))
            dve.tensor_copy(slot[:, :], slot_f[:, :]).then_inc(slots_in, 1)
            chain(dve.tensor_tensor(cmp_t[:, :, :], number.unsqueeze(2).to_broadcast([P, NT, E]),
                                    few[:, 1, :].unsqueeze(1).to_broadcast([P, NT, E]), ALU.is_ge))
            chain(dve.reduce_sum(tile_e[:, 0, :], cmp_t[:, :, :], AX))
            chain(dve.tensor_scalar(tile_e[:, 1, :], tile_e[:, 0, :], float(E - 1), float(P), ALU.min, ALU.mult))
            chain(dve.tensor_scalar(tile_e[:, 2, :], tile_e[:, 1, :], row, None, ALU.add))
            dve.tensor_copy(w_row[:, :], tile_e[:, 2, :]).then_inc(rows_in, 1)
            chosen = top[:, 0, :, :].rearrange("p a b -> p (a b)")
            dve.tensor_tensor(gate[:, 0, :], chosen, chosen, ALU.subtract).then_inc(zero_diff, 1)
            dve.wait_ge(gate_exp, 1)
            chain(dve.reciprocal(gate[:, 2, :], gate[:, 1, :]))
            dve.tensor_tensor(gate[:, 3, :], gate[:, 1, :], gate[:, 2, :], ALU.mult).then_inc(gate_in, 1)

            def rows(k, i):
                j = 4 * k + i
                dve.wait_ge(turned, j + 1)
                if not fixed(j) or j >= 2:
                    dve.wait_ge(up, HB // 2 * (j - 1))
                dve.tensor_copy(x_t[i % 2], bank(i % 2)[:, 0:ET]).then_inc(x_ready, 1)

            def result(k, i):
                j = 4 * k + i
                dve.wait_ge(down, j + 1)
                if not fixed(j) or j >= 2:
                    dve.wait_ge(y_kept[i % 2], 16 * (2 * k + i // 2))
                b2 = w_ring[i % 4][:, 2 * HB * P + HB:2 * HB * P + HB + P].unsqueeze(1).to_broadcast([P, ET // P, P])
                dve.tensor_tensor(y_s[i % 2], bank(6 + i % 2)[:, 0:ET].rearrange("p (t c) -> p t c", c=P), b2, ALU.add)\
                   .then_inc(y_made, 1)

            rows(0, 0)
            def step(k, i):
                j = 4 * k + i
                if not fixed(j) or j + 1 < NT:
                    rows(k, i + 1)
                if not fixed(j) or j > 0:
                    result(k, i - 1)
            tile_rounds(dve, step)
            result(NT // 4, NT % 4 - 1)
            dve.wait_ge(gate_in, 1)
            for t in range(RT):
                c, o = t // TT, (t % TT) * P
                if t % TT == 0:
                    dve.wait_ge(taken[c], 16 * TT)
                dve.scalar_tensor_tensor(back[:, c, o:o + P], back[:, c, o:o + P], gate[:, 3, t:t + 1],
                                         h1_tok[:, c, o:o + P], ALU.mult, ALU.add).then_inc(mixed, 1)


def kernel(**inputs):
    import concourse.bacc as _bacc
    from concourse.bass_utils import run_bass_kernel_spmd as _run

    a = {k: np.asarray(x) for k, x in inputs.items()}

    def cols(x):
        return x.reshape(-1, P).T

    pre = "L0_attn_"
    vec = np.concatenate([
        a["L0_tok_conv_w"], cols(a["L0_tok_gamma"]), cols(a["L0_tok_beta"]), cols(a[pre + "ln1_w"]),
        cols(a[pre + "ln1_b"]), cols(a[pre + "norm_f_w"]), cols(a[pre + "ln2_w"]), cols(a[pre + "ln2_b"]),
        cols(a[pre + "fc2_b"]), cols(a[pre + "block_norm_w"]), cols(a[pre + "fc1_b"]), cols(a[pre + "conv_b"]),
        cols(a[pre + "dt_proj_b"]), cols(a[pre + "D_param"]),
        a[pre + "A_log"].reshape(NL, HV, P, NS).transpose(2, 0, 1, 3).reshape(P, NL * HV * NS)], axis=1)
    con = np.zeros((P, NCON), np.float32)
    con[:, CON["ident"]:CON["ident"] + P] = np.eye(P)
    con[:, CON["mean"]:CON["mean"] + P] = 1.0 / P
    con[:, CON["center"]:CON["center"] + P] = np.eye(P) - 1.0 / P
    con[:, CON["pick"]:CON["pick"] + 2 * NS] = np.arange(P)[:, None] % (2 * NS) == np.arange(2 * NS)[None, :]
    con[:, CON["keep"]:CON["keep"] + ITEMS] = np.arange(ITEMS)[None, :] % CPB != 0
    con[:, CON["eps"]] = EPS
    con[:, CON["one"]] = 1.0
    con[:, CON["rank"]:CON["rank"] + E] = E - np.arange(E)[None, :]

    sort = np.zeros((P, NSORT), np.float32)
    sort[:, SORT["ones"]:SORT["ones"] + P] = 1.0
    sort[:, SORT["before"]:SORT["before"] + P] = np.arange(P)[:, None] < np.arange(P)[None, :]
    sort[:, SORT["multiple"]:SORT["multiple"] + TOK // ET] = ET * np.arange(TOK // ET)[None, :]
    sort[:, SORT["number"]:SORT["number"] + NT] = np.arange(NT)[None, :]
    sort[:, SORT["row"]] = np.arange(P)
    sort[:, SORT["restart"]:SORT["restart"] + E * RT] = np.arange(E * RT)[None, :] % RT != 0

    win = a[pre + "in_proj_w"].transpose(2, 0, 1)
    arrays = {
        "tok": a["x"].reshape(TOK // P, P).T.view(np.uint32) if a["x"].dtype == np.int32 else a["x"].reshape(TOK // P, P).T,
        "embed": a["L0_tok_embed_table"],
        "vec": vec,
        "con": con,
        "sort": sort,
        "win_x": win[:, :, 0:DI],
        "win_z": win[:, :, DI:2 * DI],
        "conv_w": a[pre + "conv_w"].transpose(0, 2, 1),
        "xproj": a[pre + "x_proj_w"].reshape(NL, R + 2 * NS, HV, P).transpose(0, 3, 2, 1),
        "dtw": a[pre + "dt_proj_w"].transpose(0, 2, 1),
        "outw": a[pre + "out_proj_w"].reshape(NL, P, HV, P).transpose(0, 3, 2, 1).reshape(NL, P, HV * P),
        "fc1": a[pre + "fc1_w"].T,
        "fc2": a[pre + "fc2_w"].reshape(P, HB, P).transpose(2, 1, 0),
        "wr": a["L0_ffn_Wr"],
        "br": a["L0_ffn_br"],
        "wexp": np.concatenate([
            a["L0_ffn_W1"], a["L0_ffn_W2"].reshape(E, HB, P, P).transpose(0, 2, 1, 3).reshape(E, P, HB * P),
            a["L0_ffn_b1"].reshape(E, HB, P).transpose(0, 2, 1),
            np.broadcast_to(a["L0_ffn_b2"][:, None, :], (E, P, P))], axis=2).reshape(E * P, NX),
    }
    arrays = {f"in_{k}": np.ascontiguousarray(x) for k, x in arrays.items()}
    nc = _bacc.Bacc("TRN2", target_bir_lowering=False, num_devices=1)
    args = [nc.dram_tensor(k, x.shape, mybir.dt.from_np(x.dtype), kind="ExternalInput").ap() for k, x in arrays.items()]
    args.append(nc.dram_tensor("out_0", (NCH, TT, P, P), F32, kind="ExternalOutput").ap())
    lm_tower(nc, *args)
    res = _run(nc, [arrays], core_ids=[0])
    return res.results[0]["out_0"].reshape(BATCH, TOK // BATCH, P)
```

```python
from contextlib import ExitStack

import concourse.bass as bass
import numpy as np
from concourse import mybir

F32 = mybir.dt.float32
BF16 = mybir.dt.bfloat16
U32 = mybir.dt.uint32
ALU = mybir.AluOpType
ACT = mybir.ActivationFunctionType
AX = mybir.AxisListType.X
ds = bass.ds

P = 128
TC = 512
BATCH = 2
TOK = 4096
NCH = TOK // TC
CPB = NCH // BATCH
TT = TC // P
NL = 4
HV = 2
NS = 16
KC = 4
KT = 3
R = 8
DI = HV * P
UN = HV * NS
ITEMS = NL * NCH
E = 8
HB = 4
EPS = 1e-5
SMALL = 2.0 ** -12
SQRT_HALF = 0.5 ** 0.5
LOG_EXP = "natural_log_exp_and_others"

VEC = {}
_at = 0
for _name, _n in (("tok_w", KT), ("tok_gamma", 1), ("tok_beta", 1), ("ln1_w", 1), ("ln1_b", 1), ("norm_f", 1),
                  ("ln2_w", 1), ("ln2_b", 1), ("fc2_b", 1), ("block_norm", NL), ("fc1_b", HB),
                  ("conv_b", NL * HV), ("dt_b", NL * HV), ("D", NL * HV),
                  ("A", NL * HV * NS)):
    VEC[_name] = _at
    _at += _n
NVEC = _at
CON = {}
_at = 0
for _name, _n in (("ident", P), ("mean", P), ("center", P), ("pick", 2 * NS), ("keep", ITEMS), ("eps", 1), ("one", 1)):
    CON[_name] = _at
    _at += _n
NCON = _at

ET = 256
NT = TOK // ET + E - 1
RT = TOK // P
NX = 2 * HB * P + HB + P
SORT = {}
_at = 0
for _name, _n in (("ones", P), ("before", P), ("multiple", TOK // ET), ("number", NT), ("row", 1), ("restart", E * RT), ("rank", E)):
    SORT[_name] = _at
    _at += _n
NSORT = _at

W_TAP, W_Z, W_X, W_DT = 0, KC * DI, KC * DI + DI, KC * DI + 2 * DI
NW = W_DT + DI

ND, NP = 8, 8
NB = 4
LEAD_B, LEAD_A, LAG = 3, 5, 4

CF = 11
FILLS = {0: [("C", 11), ("C", 12)], 1: [("C", 13)], 2: [("C", 14)], 3: [("C", 15)], 4: [("x1", 0)], 9: [("z1", 0)],
         14: [("xd", 0)], 16: [("dt", 0)], 21: [("stat", 0)], 23: [("dt", 1)]}
for _n in range(CF):
    FILLS.setdefault(max(21 + _n, 22), []).append(("C", _n))
BANK_USES = [use for slot in sorted(FILLS) for use in FILLS[slot]]
BANK_AT = {use: k for k, use in enumerate(BANK_USES)}
NBU = len(BANK_USES)
FIRST_USES = ([("stat", -1)] + [(what, h) for what, h in BANK_USES if what in ("x1", "z1", "xd", "dt")]
              + [("C", n) for n in range(CF)] + [("stat", 0)])
FIRST_AT = {use: k for k, use in enumerate(FIRST_USES)}
SECOND_LAST_AT = {use: k for k, use in enumerate([use for use in BANK_USES if use[0] != "stat"])}
LAST_AT = {use: k for k, use in enumerate([use for use in BANK_USES if use[0] == "C" and use[1] >= CF])}


def rounds(eng, one_round):
    one_round(0)
    with eng.Fori(1, CPB) as k:
        one_round(k)


def later(k):
    return not isinstance(k, int) or k > 0


def lm_tower(nc, tok, embed, vec, con, sort, win_x, win_z, conv_w, xproj, dtw, outw, fc1, fc2, wr, br, wexp, out):
    ctx = ExitStack()
    with ctx:
        def sb(name, shape, dt=F32):
            return ctx.enter_context(nc.sbuf_tensor(name, shape, dt))

        def sem(name):
            return ctx.enter_context(nc.semaphore(name))

        psum = ctx.enter_context(nc.psum_tensor("banks", [P, 8, TC], F32))

        def bank(b):
            return psum[:, b, :]

        h0_d = nc.dram_tensor("h0_scratch", [NCH, P, TC], F32, kind="Internal").ap()
        s_d = nc.dram_tensor("s_scratch", [NCH, P, TC], F32, kind="Internal").ap()
        x_d = nc.dram_tensor("sorted_scratch", [NT * ET, P], F32, kind="Internal").ap()
        y_d = nc.dram_tensor("results_scratch", [NT * ET, P], F32, kind="Internal").ap()
        w_d = nc.dram_tensor("front_scratch", [NL, P, NW], F32, kind="Internal").ap()

        V = sb("V", [P, NVEC])
        Cn = sb("Cn", [P, NCON])
        r = sb("r", [P, NCH, TC])
        ident = Cn[:, CON["ident"]:CON["ident"] + P]
        meanw = Cn[:, CON["mean"]:CON["mean"] + P]
        center = Cn[:, CON["center"]:CON["center"] + P]
        eps = Cn[:, CON["eps"]:CON["eps"] + 1]
        one = Cn[:, CON["one"]:CON["one"] + 1]

        def v(name, k=0):
            return V[:, VEC[name] + k:VEC[name] + k + 1]

        h_ring = sb("h_ring", [P, NS, TC])
        c_all = sb("c_all", [P, NS, TC])
        decay = sb("decay", [P, ND, TC])
        prod = sb("prod", [P, NP, TC])
        delta = sb("delta", [P, 2, HV, TC])
        du = sb("du", [P, 2, HV, TC])
        xs = sb("xs", [P, 2, HV, TC])
        zs = sb("zs", [P, 2, HV, TC])
        stack = sb("stack", [96, 2, TC], BF16)
        pick = sb("pick", [96, 2 * NS, P], BF16)
        wf = sb("wf", [P, NW])
        wo = sb("wo", [P, HV, P])
        hn = sb("hn", [P, KC - 1 + TC])
        h_init = sb("h_init", [P, HV, NS])
        sq = sb("sq", [P, TC])
        lnv = sb("lnv", [P, TC])
        rstd = sb("rstd", [P, TC])
        xd = sb("xd", [P, TC])
        rest = sb("rest", [96, TC])
        mid = sb("mid", [96, TC], BF16)
        ea = sb("ea", [P, HV, TC])
        pos = sb("pos", [P, HV, TC])
        w1p = sb("w1p", [P, HV, TC])
        lg = sb("lg", [P, HV, TC])
        small = sb("small", [P, HV, TC])
        small_pos = sb("small_pos", [P, HV, TC])
        yt = sb("yt", [P, TC])
        yz = sb("yz", [P, HV, TC])

        loaded = sem("loaded")
        gathered = [sem(f"gathered{s}") for s in range(2)]
        names0 = ["turned", "emb", "tap0", "tap1", "tap2", "cen", "sqd", "var", "rst", "scl", "h0_made",
                  "h0_kept", "s_kept", "hist"]
        q0 = {n: [sem(f"{n}_s{s}") for s in range(2)] for n in names0}
        folded = sem("folded")
        picked = sem("picked")
        neg_a = sem("neg_a")
        w_zero = sem("w_zero")
        w_in = sem("w_in")
        w_out = sem("w_out")
        r_ready = sem("r_ready")

        g_tok = h_ring[:, 0:4, :].rearrange("p (s t) c -> p s (t c)", s=2)[:, :, 0:TT * P]
        rows = sb("rows", [P, RT + NT], U32)
        idx = rows[:, 0:RT]
        emb = [h_ring[:, 4 + 2 * s:6 + 2 * s, :].rearrange("p a b -> p (a b)")[:, 0:KT - 1 + TC] for s in range(2)]
        ta = [h_ring[:, 8 + s, :] for s in range(2)]
        tb = [h_ring[:, 10 + s, :] for s in range(2)]
        s_sq = [h_ring[:, 12 + s, :] for s in range(2)]
        s_rs = [h_ring[:, 14 + s, :] for s in range(2)]
        s_ln = [decay[:, s, :] for s in range(2)]
        s_y = [decay[:, 2 + s, :] for s in range(2)]
        s_h0 = [prod[:, s, :] for s in range(2)]
        s_s = [prod[:, 2 + s, :] for s in range(2)]
        wx_all = c_all[:, :, :].rearrange("p a b -> p (a b)")[:, 0:NL * DI].rearrange("p (l d) -> p l d", l=NL)
        cw_all = c_all[:, :, :].rearrange("p a b -> p (a b)")[:, NL * DI:NL * DI * (1 + KC)]
        cw_all = cw_all.rearrange("p (l k d) -> p l k d", l=NL, k=KC)

        with nc.Block() as block:

            @block.sync
            def _(sp):
                sp.dma_start(V[:, :], vec).then_inc(loaded, 16)
                sp.dma_start(Cn[:, :], con).then_inc(loaded, 16)
                sp.dma_start(idx, tok).then_inc(w_in, 16)
                sp.dma_start(wx_all, win_x).then_inc(folded, 16)
                sp.dma_start(cw_all, conv_w.partition_broadcast(P)).then_inc(folded, 16)
                for l in range(NL):
                    sp.wait_ge(w_zero, l + 1)
                    sp.dma_start(wf[:, W_Z:W_Z + DI], win_z[:, l, :]).then_inc(w_out, 16)
                    for h in range(HV):
                        for rep in range(3):
                            sp.dma_start(wf[:, W_X + h * P + 32 * rep:W_X + h * P + 32 * rep + 32],
                                         xproj[l, :, h, R:R + 2 * NS]).then_inc(w_out, 16)
                        sp.dma_start(wf[:, W_X + h * P + 96:W_X + h * P + 96 + R], xproj[l, :, h, 0:R]).then_inc(w_out, 16)
                    sp.dma_start(wf[96:96 + R, W_DT:W_DT + DI], dtw[l, :, :]).then_inc(w_out, 16)
                    sp.wait_ge(w_out, (11 * l + 10) * 16)
                    sp.wait_ge(picked, l + 2)
                    sp.dma_start(w_d[l, :, :], wf[:, :]).then_inc(w_out, 16)
                    sp.wait_ge(w_out, (11 * l + 11) * 16)
                    sp.sem_inc(neg_a, 1)
                def one_round(k):
                    for s in range(2):
                        sp.wait_ge(q0["h0_made"][s], k + 1)
                        sp.dma_start(h0_d[k + s * CPB, :, :], s_h0[s])\
                          .then_inc(q0["h0_kept"][s], 16)
                        sp.wait_ge(q0["scl"][s], 3 * k + 2)
                        sp.dma_start(s_d[k + s * CPB, :, :], s_s[s])\
                          .then_inc(q0["s_kept"][s], 16)
                rounds(sp, one_round)
                for s in range(2):
                    sp.wait_ge(q0["h0_kept"][s], 16 * CPB)
                    sp.wait_ge(q0["s_kept"][s], 16 * CPB)

            @block.gpsimd
            def _(pool):
                pool.memset(hn[:, :], 0.0)
                pool.memset(h_init[:, :, :], 0.0)
                pool.wait_ge(w_in, 16)
                for k in range(CPB):
                    for s in range(2):
                        if k:
                            pool.wait_ge(q0["turned"][s], k)
                        for t in range(TT):
                            col = (k + s * CPB) * TT + t
                            pool.indirect_dma_start(
                                out=g_tok[:, s, t * P:(t + 1) * P], out_offset=None, in_=embed,
                                in_offset=bass.IndirectOffsetOnAxis(ap=idx[:, col:col + 1], axis=0))\
                                .then_inc(gathered[s], 16)

            @block.tensor
            def _(pe):
                pe.wait_ge(loaded, 32)
                def one_round(k):
                    for s in range(2):
                        pe.wait_ge(gathered[s], (k + 1) * 16 * TT)
                        for t in range(TT):
                            last = pe.transpose(bank(4 * s)[:, t * P:(t + 1) * P], g_tok[:, s, t * P:(t + 1) * P], ident)
                        last.then_inc(q0["turned"][s], 1)
                    for m, (src, ready, count) in enumerate(((ta, "tap2", k + 1), (s_h0, "h0_made", k + 1),
                                                             (s_s, "scl", 3 * k + 2)), 1):
                        for s in range(2):
                            pe.wait_ge(q0[ready][s], count)
                            pe.matmul(bank(4 * s + 1), center, src[s], start=True, stop=True)\
                              .then_inc(q0["cen"][s], 1)
                        for s in range(2):
                            pe.wait_ge(q0["sqd"][s], 3 * k + m)
                            pe.matmul(bank(4 * s + 2), meanw, s_sq[s], start=True, stop=True)\
                              .then_inc(q0["var"][s], 1)
                rounds(pe, one_round)

            @block.scalar
            def _(act):
                act.preload_act_table_set(LOG_EXP)
                act.wait_ge(loaded, 32)
                a_all = V[:, VEC["A"]:VEC["A"] + NL * HV * NS]
                act.activation(a_all, a_all, ACT.Exp).then_inc(picked, 1)
                def one_round(k):
                    for s in range(2):
                        act.wait_ge(q0["turned"][s], k + 1)
                        act.wait_ge(q0["hist"][s], k + 1)
                        act.activation(emb[s][:, KT - 1:KT - 1 + TC], bank(4 * s), ACT.Copy).then_inc(q0["emb"][s], 1)
                    for m in (1, 2, 3):
                        for s in range(2):
                            act.wait_ge(q0["cen"][s], 3 * k + m)
                            act.activation(s_sq[s], bank(4 * s + 1), ACT.Square).then_inc(q0["sqd"][s], 1)
                        for s in range(2):
                            act.wait_ge(q0["var"][s], 3 * k + m)
                            act.activation(s_ln[s], bank(4 * s + 2), ACT.Ln, bias=eps).then_inc(q0["rst"][s], 1)
                            act.wait_ge(q0["rst"][s], 6 * k + 2 * m - 1)
                            act.activation(s_rs[s], s_ln[s], ACT.Exp, scale=-0.5).then_inc(q0["rst"][s], 1)
                        if m == 1:
                            for s in range(2):
                                act.wait_ge(q0["scl"][s], 3 * k + 1)
                                if later(k):
                                    act.wait_ge(q0["h0_kept"][s], 16 * k)
                                act.activation(s_h0[s], s_y[s], ACT.Relu, scale=v("tok_gamma"), bias=v("tok_beta"))\
                                   .then_inc(q0["h0_made"][s], 1)
                        if m == 3:
                            for s in range(2):
                                act.wait_ge(q0["scl"][s], 3 * k + 3)
                                act.activation(r[:, k + s * CPB, :], s_y[s],
                                               ACT.Identity, scale=v("ln1_w"), bias=v("ln1_b")).then_inc(r_ready, 1)
                rounds(act, one_round)

            @block.vector
            def _(dve):
                dve.wait_ge(loaded, 32)
                pk = Cn[0:96, CON["pick"]:CON["pick"] + 2 * NS]
                dve.tensor_copy(pick[:, :, :], pk.unsqueeze(2).to_broadcast([96, 2 * NS, P]))
                dve.memset(wf[:, W_X:NW], 0.0).then_inc(w_zero, 1)
                dve.wait_ge(picked, 1)
                a_all = V[:, VEC["A"]:VEC["A"] + NL * HV * NS]
                dve.tensor_scalar(a_all, a_all, -1.0, None, ALU.mult)
                dve.wait_ge(folded, 32)
                for l in range(NL):
                    if l:
                        dve.wait_ge(neg_a, l)
                    src = wx_all[:, l, :].unsqueeze(1).to_broadcast([P, KC, DI])
                    dve.tensor_tensor(wf[:, 0:KC * DI].rearrange("p (k d) -> p k d", k=KC), src, cw_all[:, l, :, :],
                                      ALU.mult).then_inc(picked, 1)
                    if l + 1 < NL:
                        dve.wait_ge(neg_a, l + 1)
                        dve.sem_inc(w_zero, 1)
                for s in range(2):
                    dve.memset(emb[s][:, TC:TC + KT - 1], 0.0).then_inc(q0["tap0"][s], 1)
                    dve.wait_ge(q0["tap0"][s], 1)
                def one_round(k):
                    for s in range(2):
                        if later(k):
                            dve.wait_ge(q0["tap2"][s], k)
                        dve.tensor_copy(emb[s][:, 0:KT - 1], emb[s][:, TC:TC + KT - 1]).then_inc(q0["hist"][s], 1)
                    for s in range(2):
                        dve.wait_ge(q0["emb"][s], k + 1)
                        dve.wait_ge(q0["hist"][s], k + 1)
                        dve.tensor_scalar(ta[s], emb[s][:, 0:TC], v("tok_w", 0), None, ALU.mult)\
                           .then_inc(q0["tap0"][s], 1)
                        dve.wait_ge(q0["tap0"][s], k + 2)
                        dve.scalar_tensor_tensor(tb[s], emb[s][:, 1:1 + TC], v("tok_w", 1), ta[s], ALU.mult, ALU.add)\
                           .then_inc(q0["tap1"][s], 1)
                        dve.wait_ge(q0["tap1"][s], k + 1)
                        dve.scalar_tensor_tensor(ta[s], emb[s][:, 2:2 + TC], v("tok_w", 2), tb[s], ALU.mult, ALU.add)\
                           .then_inc(q0["tap2"][s], 1)
                    for m in (1, 2, 3):
                        for s in range(2):
                            dve.wait_ge(q0["rst"][s], 6 * k + 2 * m)
                            if m == 2:
                                if later(k):
                                    dve.wait_ge(q0["s_kept"][s], 16 * k)
                            dve.tensor_tensor(s_s[s] if m == 2 else s_y[s], bank(4 * s + 1), s_rs[s], ALU.mult)\
                               .then_inc(q0["scl"][s], 1)
                rounds(dve, one_round)

        front_in = sem("front_in")
        dt_w_in = sem("dt_w_in")
        ahead_full = sem("ahead_full")
        ahead_out = sem("ahead_out")
        out_in = sem("out_in")
        squared = sem("squared")
        logged = sem("logged")
        rstd_in = sem("rstd_in")
        hist_in = sem("hist_in")
        hn_in = sem("hn_in")
        z_in = sem("z_in")
        z1_in = sem("z1_in")
        xs_in = sem("xs_in")
        xd_in = sem("xd_in")
        part_in = sem("part_in")
        stack_in = sem("stack_in")
        abs_in = sem("abs_in")
        exp_in = sem("exp_in")
        plus_in = sem("plus_in")
        ln_in = sem("ln_in")
        half_sq = sem("half_sq")
        small_in = sem("small_in")
        err_in = sem("err_in")
        base_in = sem("base_in")
        pos_in = sem("pos_in")
        diff_in = sem("diff_in")
        chosen = sem("chosen")
        delta_in = sem("delta_in")
        du_in = sem("du_in")
        bank_full = sem("bank_full")
        bank_free = sem("bank_free")
        b_full = sem("b_full")
        decay_in = sem("decay_in")
        c_in = sem("c_in")
        drive_in = sem("drive_in")
        scanned = sem("scanned")
        kept = sem("kept")
        prod_in = sem("prod_in")
        prod_used = sem("prod_used")
        yt_in = sem("yt_in")
        yz_in = sem("yz_in")
        o_full = sem("o_full")

        def col(t, k):
            return t[:, ds(k, 1)] if not isinstance(k, int) else t[:, k:k + 1]

        def par(t, i, h):
            return t[:, i % 2, h, :]

        def par_s(i, a, b):
            return stack[a:b, i % 2, :]

        def par2(t, i):
            return t[:, i % 2, :, :]

        def chunk(i):
            return r[:, i % NCH, :]

        def place(i, use):
            if isinstance(i, int) and i in (-1, ITEMS - 2, ITEMS - 1):
                return {-1: FIRST_AT, ITEMS - 2: SECOND_LAST_AT, ITEMS - 1: LAST_AT}[i][use]
            return BANK_AT[use]

        def fill(i, use):
            if isinstance(i, int) and i < 0:
                return place(i, use)
            less = isinstance(i, int) and i == ITEMS - 1
            return NBU * i + len(FIRST_USES) + place(i, use) - less

        def shared(i, use):
            less = isinstance(i, int) and i == ITEMS - 1
            return bank(6 + (place(i, use) + less) % 2)

        Y, BB = (0, 1), (2, 3, 4, 5)

        with nc.Block() as block:

            @block.sync
            def _(sp):
                def load_in(j):
                    l = j // NCH
                    if not isinstance(j, int) or j > 0:
                        sp.wait_ge(bank_full, fill(j - 2, ("z1", 0)) + 1)
                    sp.dma_start(wf[:, 0:W_X], w_d[l, :, 0:W_X]).then_inc(front_in, 16)

                def load_dt(j):
                    l = j // NCH
                    if not isinstance(j, int) or j > 0:
                        sp.wait_ge(bank_full, fill(j - 2, ("dt", 1)) + 1)
                    sp.dma_start(wf[:, W_X:NW], w_d[l, :, W_X:NW]).then_inc(dt_w_in, 16)

                def load_out(j):
                    l = j // NCH
                    if not isinstance(j, int) or j > 0:
                        sp.wait_ge(o_full, j)
                    src = outw[l, :, :]
                    sp.dma_start(wo[:, :, :].rearrange("p h n -> p (h n)"), src).then_inc(out_in, 16)

                load_in(0)
                load_dt(0)
                load_out(0)
                for j in (1, 2):
                    load_in(j)
                    load_dt(j)
                with sp.Fori(1, ITEMS - 2) as i:
                    load_in(i + 2)
                    load_out(i)
                    load_dt(i + 2)
                load_out(ITEMS - 2)
                load_out(ITEMS - 1)

            @block.tensor
            def _(pe):
                def take(i, use):
                    f = fill(i, use)
                    if not isinstance(f, int) or f >= 2:
                        pe.wait_ge(bank_free, f - 1)

                def bring(i, u):
                    g = UN * i + u
                    h, n = (u % UN) // NS, u % NS
                    ii = i + u // UN
                    if u % UN == 0:
                        pe.wait_ge(stack_in, ii + 1)
                    if not isinstance(g, int) or g >= NB:
                        pe.wait_ge(scanned, g - NB + 1)
                    pe.matmul(bank(BB[u % NB]), pick[:, n, :], par_s(ii, 0, 96), start=True, stop=True).then_inc(b_full, 1)

                def bring_c(i, j, n, use):
                    take(i, use)
                    if n == 0:
                        pe.wait_ge(stack_in, j + 1)
                    pe.matmul(shared(i, use), pick[:, NS + n, :], par_s(j, 0, 96), start=True, stop=True)\
                      .then_inc(bank_full, 1)

                def add_up(i, u):
                    g, h, n = UN * i + u, u // NS, u % NS
                    if n == 0 and h == 0 and (not isinstance(i, int) or i > 0):
                        pe.wait_ge(yt_in, 2 * i - 1)
                    if n == 0 and h == 1 and (not isinstance(i, int) or i > 0):
                        pe.wait_ge(r_ready, NCH + i)
                    pe.wait_ge(prod_in, g + 1)
                    if n == 0 and h == 0 and (not isinstance(i, int) or i < ITEMS - 1):
                        pe.wait_ge(ahead_out, 2 * (i + 2))
                    pe.matmul(bank(Y[h]), ident, prod[:, u % NP, :], start=(n == 0), stop=(n == NS - 1)).then_inc(prod_used, 1)

                def project(i):
                    pe.wait_ge(yz_in, 2 * i + 2)
                    pe.wait_ge(out_in, 16 * (i + 1))
                    for h in range(HV):
                        mm = pe.matmul(bank(Y[1]), wo[:, h, :], yz[:, h, :], start=(h == 0), stop=(h == HV - 1))
                    mm.then_inc(o_full, 1)

                def taps(to, h, k, full):
                    o = W_TAP + k * DI + h * P
                    mm = pe.matmul(to, wf[:, o:o + P], hn[:, k:k + TC], start=(k == 0), stop=(k == KC - 1))
                    if k == KC - 1:
                        mm.then_inc(full, 1)

                def front(i, step):
                    j = i + 1
                    what, h = step[0], step[1]
                    n = j + h + 1
                    if what == "stat":
                        take(i, step)
                        pe.wait_ge(squared, n + 1)
                        pe.matmul(shared(i, step), meanw, sq[:, :], start=True, stop=True).then_inc(bank_full, 1)
                    elif what == "z0":
                        pe.wait_ge(hn_in, n + 1)
                        pe.wait_ge(front_in, 16 * (n + 1))
                        if not isinstance(n, int) or n > 1:
                            pe.wait_ge(yt_in, 2 * (n - 2) + 1)
                        elif n == 1:
                            pe.wait_ge(ahead_out, 2)
                        pe.matmul(bank(Y[0]), wf[:, W_Z:W_Z + P], hn[:, KC - 1:KC - 1 + TC],
                                  start=True, stop=True).then_inc(ahead_full, 1)
                    elif what == "x0":
                        if step[2] == 0:
                            pe.wait_ge(ahead_out, 2 * n + 1)
                        taps(bank(Y[0]), 0, step[2], ahead_full)
                    elif what == "z1":
                        take(i, step)
                        pe.matmul(shared(i, step), wf[:, W_Z + P:W_Z + 2 * P], hn[:, KC - 1:KC - 1 + TC],
                                  start=True, stop=True).then_inc(bank_full, 1)
                    elif what == "x1":
                        if step[2] == 0:
                            take(i, ("x1", 0))
                        taps(shared(i, ("x1", 0)), 1, step[2], bank_full)
                    elif what == "xd":
                        if h == 0:
                            take(i, ("xd", 0))
                            pe.wait_ge(xs_in, 2 * j + 2)
                            pe.wait_ge(dt_w_in, 16 * (j + 1))
                        mm = pe.matmul(shared(i, ("xd", 0)), wf[:, W_X + h * P:W_X + h * P + P], par(xs, j, h),
                                       start=(h == 0), stop=(h == HV - 1))
                        if h == HV - 1:
                            mm.then_inc(bank_full, 1)
                    elif what == "dt":
                        take(i, ("dt", h))
                        if h == 0:
                            pe.wait_ge(xd_in, j + 1)
                        pe.matmul(shared(i, ("dt", h)), wf[:, W_DT + h * P:W_DT + h * P + P], xd[:, :],
                                  start=True, stop=True).then_inc(bank_full, 1)

                FRONT = {13: [("xd", 0)], 14: [("xd", 1)], 25: [("z0", 0)]}
                for k in range(KC):
                    FRONT.setdefault((4, 6, 8, 10)[k], []).append(("x1", 0, k))
                    FRONT.setdefault((27, 28, 30, 31)[k], []).append(("x0", 0, k))

                def body(i, ahead):
                    for u in range(UN):
                        w = u - LAG
                        if w >= 0:
                            add_up(i, w)
                        elif not isinstance(i, int) or i > 0:
                            add_up(i - 1, w + UN)
                        if u + LEAD_B < UN or ahead:
                            bring(i, u + LEAD_B)
                        for use in FILLS.get(u, []):
                            if use[0] == "C" and (use[1] >= CF or ahead):
                                bring_c(i, i if use[1] >= CF else i + 1, use[1], use)
                            elif use[0] in ("z1", "dt", "stat") and ahead > (use[0] == "stat"):
                                front(i, use)
                        for step in FRONT.get(u, []):
                            if ahead > (step[0] in ("z0", "x0")):
                                front(i, step)
                        if u == 12 and (not isinstance(i, int) or i > 0):
                            project(i - 1)

                front(-1, ("stat", -1))
                front(-1, ("z0", -1))
                for k in range(KC):
                    front(-1, ("x0", -1, k))
                for k in range(KC):
                    front(-1, ("x1", 0, k))
                for step in (("z1", 0), ("xd", 0), ("xd", 1), ("dt", 0), ("dt", 1)):
                    front(-1, step)
                for n in range(CF):
                    bring_c(-1, 0, n, ("C", n))
                front(-1, ("stat", 0))
                front(-1, ("z0", 0))
                for k in range(KC):
                    front(-1, ("x0", 0, k))
                for u in range(LEAD_B):
                    bring(0, u)
                body(0, 2)
                with pe.Fori(1, ITEMS - 2) as i:
                    body(i, 2)
                body(ITEMS - 2, 1)
                body(ITEMS - 1, 0)
                for u in range(UN - LAG, UN):
                    add_up(ITEMS - 1, u)
                project(ITEMS - 1)

            @block.scalar
            def _(act):
                def decays(i, u):
                    g, h, n = UN * i + u, (u % UN) // NS, u % NS
                    ii = i + u // UN
                    if n == 0:
                        act.wait_ge(delta_in, HV * ii + h + 1)
                    if not isinstance(g, int) or g >= ND:
                        act.wait_ge(scanned, g - ND + 1)
                    act.activation(decay[:, u % ND, :], par(delta, ii, h), ACT.Exp,
                                   scale=col(V, VEC["A"] + (ii // NCH) * UN + h * NS + n)).then_inc(decay_in, 1)

                def copy_c(i, j, n, use):
                    act.wait_ge(bank_full, fill(i, use) + 1)
                    if not isinstance(j, int) or j > 0:
                        act.wait_ge(prod_in, UN * (j - 1) + NS + n + 1)
                    act.activation(c_all[:, n, :], shared(i, use), ACT.Copy).then_inc(c_in, 1)
                    act.wait_ge(c_in, NS * j + n + 1)
                    act.sem_inc(bank_free, 1)

                def front(i, step):
                    what, h = step
                    j = i + 1
                    l = j // NCH
                    n = j + h + 1
                    if what == "square":
                        act.wait_ge(r_ready, n + 1)
                        act.activation(sq[:, :], chunk(n), ACT.Square).then_inc(squared, 1)
                    elif what == "stat":
                        act.wait_ge(bank_full, fill(i, step) + 1)
                        act.activation(lnv[:, :], shared(i, step), ACT.Ln, bias=eps).then_inc(bank_free, 1)
                        act.wait_ge(bank_free, fill(i, step) + 1)
                        act.activation(rstd[:, :], lnv[:, :], ACT.Exp, scale=-0.5).then_inc(rstd_in, 1)
                    elif what == "z0":
                        if not isinstance(n, int) or n > 1:
                            act.wait_ge(yz_in, 2 * (n - 2) + 1)
                        act.wait_ge(ahead_full, 2 * n + 1)
                        act.activation(par(zs, n, 0), bank(Y[0]), ACT.Copy).then_inc(ahead_out, 1)
                    elif what == "x0":
                        act.wait_ge(ahead_full, 2 * n + 2)
                        act.activation(par(xs, n, 0), bank(Y[0]), ACT.Copy).then_inc(ahead_out, 1)
                    elif what == "z1":
                        if not isinstance(j, int) or j > 1:
                            act.wait_ge(yz_in, 2 * j - 2)
                        act.wait_ge(bank_full, fill(i, step) + 1)
                        act.activation(par(zs, j, 1), shared(i, step), ACT.Copy).then_inc(z1_in, 1)
                    elif what == "silu":
                        x1 = ("x1", 0)
                        cb = [col(V, VEC["conv_b"] + l * HV + h) for h in range(HV)]
                        act.wait_ge(ahead_out, 2 * j + 2)
                        act.activation(par(xs, j, 0), par(xs, j, 0), ACT.Silu, bias=cb[0]).then_inc(xs_in, 1)
                        act.wait_ge(bank_full, fill(i, x1) + 1)
                        act.activation(par(xs, j, 1), shared(i, x1), ACT.Silu, bias=cb[1]).then_inc(xs_in, 1)
                        act.wait_ge(xs_in, 2 * j + 2)
                        act.wait_ge(z1_in, j + 1)
                        act.sem_inc(bank_free, 2)
                        act.activation(par2(zs, j), par2(zs, j), ACT.Silu).then_inc(z_in, 1)
                        act.preload_act_table_set(LOG_EXP)
                    elif what == "xd":
                        act.wait_ge(bank_full, fill(i, ("xd", 0)) + 1)
                        act.activation(xd[:, :], shared(i, ("xd", 0)), ACT.Copy).then_inc(xd_in, 1)
                        act.activation(par_s(j, 0, 96), shared(i, ("xd", 0))[0:96, :], ACT.Copy).then_inc(part_in, 1)
                        act.wait_ge(xd_in, j + 1)
                        act.wait_ge(part_in, 3 * j + 1)
                        act.sem_inc(bank_free, 1)
                    elif what == "mid":
                        act.wait_ge(part_in, 3 * j + 2)
                        act.activation(mid[:, :], rest[:, :], ACT.Copy).then_inc(part_in, 1)
                    elif what == "dt":
                        act.wait_ge(bank_full, fill(i, ("dt", h)) + 1)
                        if not isinstance(j, int) or j > 0:
                            act.wait_ge(delta_in, HV * (j - 1) + h + 1)
                        dtb = col(V, VEC["dt_b"] + l * HV + h)
                        act.activation(ea[:, h, :], shared(i, ("dt", h)), ACT.Abs, bias=dtb).then_inc(abs_in, 1)
                        act.activation(pos[:, h, :], shared(i, ("dt", h)), ACT.Relu, bias=dtb).then_inc(bank_free, 1)
                    elif what == "exp":
                        act.wait_ge(abs_in, HV * j + h + 1)
                        act.activation(ea[:, h, :], ea[:, h, :], ACT.Exp, scale=-1.0).then_inc(exp_in, 1)
                        act.wait_ge(exp_in, HV * j + h + 1)
                        act.activation(w1p[:, h, :], ea[:, h, :], ACT.Identity, bias=one).then_inc(plus_in, 1)
                        act.activation(small[:, h, :], ea[:, h, :], ACT.Square, scale=SQRT_HALF).then_inc(half_sq, 1)
                    elif what == "ln":
                        act.wait_ge(plus_in, HV * j + h + 1)
                        act.activation(lg[:, h, :], w1p[:, h, :], ACT.Ln).then_inc(ln_in, 1)

                FRONT = {12: [("silu", 0)], 15: [("xd", 0)], 17: [("mid", 0)], 18: [("exp", 0)], 19: [("ln", 0)],
                         16: [("square", 0)], 25: [("exp", 1)], 26: [("ln", 1), ("z0", 0)]}

                def body(i, ahead):
                    for u in range(UN):
                        if u + LEAD_A < UN or ahead:
                            decays(i, u + LEAD_A)
                        if u == 0 and (not isinstance(i, int) or i > 0):
                            copy_c(i - 1, i, CF - 1, ("C", CF - 1))
                            if ahead:
                                front(i - 1, ("x0", 0))
                        for use in FILLS.get(u - 1, []):
                            if use[0] == "C" and (use[1] >= CF or ahead):
                                copy_c(i, i if use[1] >= CF else i + 1, use[1], use)
                            elif use[0] in ("z1", "dt", "stat") and ahead > (use[0] == "stat"):
                                front(i, use)
                        for step in FRONT.get(u, []):
                            if ahead > (step[0] in ("square", "z0")):
                                front(i, step)

                act.preload_act_table_set(LOG_EXP)
                for step in (("square", -1), ("stat", -1), ("z0", -1), ("x0", -1), ("z1", 0), ("silu", 0), ("xd", 0),
                             ("mid", 0), ("dt", 0), ("dt", 1), ("exp", 0), ("exp", 1), ("ln", 0), ("ln", 1), ("square", 0)):
                    front(-1, step)
                for n in range(CF):
                    copy_c(-1, 0, n, ("C", n))
                for step in (("stat", 0), ("z0", 0), ("x0", 0)):
                    front(-1, step)
                for u in range(LEAD_A):
                    decays(0, u)
                body(0, 2)
                with act.Fori(1, ITEMS - 2) as i:
                    body(i, 2)
                body(ITEMS - 2, 1)
                body(ITEMS - 1, 0)


            @block.vector
            def _(dve):
                def drive(i, u):
                    g, h = UN * i + u, (u % UN) // NS
                    ii = i + u // UN
                    if u % NS == 0:
                        dve.wait_ge(du_in, HV * ii + h + 1)
                    dve.wait_ge(b_full, g + 1)
                    dve.tensor_tensor(bank(BB[u % NB]), par(du, ii, h), bank(BB[u % NB]), ALU.mult).then_inc(drive_in, 1)

                def scan(i, u, keeps):
                    g, h, n = UN * i + u, u // NS, u % NS
                    dve.wait_ge(decay_in, g + 1)
                    dve.wait_ge(drive_in, g + 1)
                    if not isinstance(g, int) or g >= NS:
                        dve.wait_ge(prod_in, g - NS + 1)
                    if n == 0 and (not isinstance(g, int) or g > 0):
                        dve.wait_ge(kept, 2 * i + h if h == 0 or keeps else 2 * i)
                    dve.tensor_tensor_scan(h_ring[:, n, :], decay[:, u % ND, :], bank(BB[u % NB]),
                                           h_init[:, h, n:n + 1], ALU.mult, ALU.add).then_inc(scanned, 1)

                def keep(i, h):
                    j = i + 1
                    dve.wait_ge(scanned, UN * i + NS * (h + 1))
                    dve.tensor_scalar(h_init[:, h, :], h_ring[:, :, TC - 1:TC].rearrange("p n a -> p (n a)"),
                                      col(Cn, CON["keep"] + j), None, ALU.mult).then_inc(kept, 1)

                def gate(i, h):
                    dve.wait_ge(prod_used, UN * i + NS * (h + 1))
                    dve.scalar_tensor_tensor(yt[:, :], par(xs, i, h), col(V, VEC["D"] + (i // NCH) * HV + h),
                                             bank(Y[h]), ALU.mult, ALU.add).then_inc(yt_in, 1)
                    dve.wait_ge(yt_in, 2 * i + h + 1)
                    if h == 0 and (not isinstance(i, int) or i > 0):
                        dve.wait_ge(o_full, i)
                    dve.tensor_tensor(yz[:, h, :], yt[:, :], par(zs, i, h), ALU.mult).then_inc(yz_in, 1)

                def residual(i):
                    dve.wait_ge(o_full, i + 1)
                    dve.tensor_tensor(chunk(i), chunk(i), bank(Y[1]), ALU.add).then_inc(r_ready, 1)

                def front(i, step, h=0):
                    j = i + 1
                    l = j // NCH
                    if step == "hn":
                        n = j + h + 1
                        l = n // NCH
                        if not isinstance(n, int) or n > 0:
                            dve.wait_ge(bank_full, fill(n - 2, ("z1", 0)) + 1)
                        dve.tensor_scalar(hn[:, 0:KC - 1], hn[:, TC:TC + KC - 1], col(Cn, CON["keep"] + n), None,
                                          ALU.mult).then_inc(hist_in, 1)
                        dve.wait_ge(hist_in, n + 1)
                        dve.wait_ge(rstd_in, n + 1)
                        dve.scalar_tensor_tensor(hn[:, KC - 1:KC - 1 + TC], chunk(n), col(V, VEC["block_norm"] + l),
                                                 rstd[:, :], ALU.mult, ALU.mult).then_inc(hn_in, 1)
                    elif step == "rest":
                        dve.wait_ge(part_in, 3 * j + 1)
                        dve.tensor_tensor(rest[:, :], xd[0:96, :], par_s(j, 0, 96), ALU.subtract).then_inc(part_in, 1)
                    elif step == "lo":
                        dve.wait_ge(part_in, 3 * j + 3)
                        dve.tensor_copy(par_s(j, 32, 64), mid[32:64, :])
                        dve.tensor_tensor(par_s(j, 64, 96), rest[64:96, :], mid[64:96, :], ALU.subtract)\
                           .then_inc(stack_in, 1)
                    elif step == "err":
                        dve.wait_ge(ln_in, HV * j + h + 1)
                        dve.scalar_tensor_tensor(w1p[:, h, :], w1p[:, h, :], -1.0, ea[:, h, :], ALU.add, ALU.subtract)\
                           .then_inc(err_in, 1)
                    elif step == "diff":
                        dve.wait_ge(base_in, HV * j + h + 1)
                        dve.tensor_tensor(lg[:, h, :], lg[:, h, :], w1p[:, h, :], ALU.subtract).then_inc(diff_in, 1)
                    elif step == "choose":
                        dve.wait_ge(diff_in, HV * j + h + 1)
                        dve.scalar_tensor_tensor(lg[:, h, :], ea[:, h, :], SMALL, lg[:, h, :], ALU.is_ge, ALU.mult)\
                           .then_inc(chosen, 1)
                    elif step == "delta":
                        dve.wait_ge(chosen, HV * j + h + 1)
                        dve.wait_ge(pos_in, HV * j + h + 1)
                        dve.tensor_tensor(par(delta, j, h), lg[:, h, :], small_pos[:, h, :], ALU.add)\
                           .then_inc(delta_in, 1)

                FRONT = {17: [("rest", 0)], 19: [("lo", 0)], 21: [("err", 0)], 23: [("diff", 0)],
                         24: [("choose", 0)], 25: [("hn", 0)], 26: [("delta", 0)], 28: [("err", 1)]}
                LATE = {0: "diff", 1: "choose", 3: "delta"}

                def body(i, ahead):
                    first = isinstance(i, int) and i == 0
                    for u in range(UN):
                        if u + 1 < UN or ahead:
                            drive(i, u + 1)
                        if u == 0 and not first:
                            keep(i - 1, 1)
                        if u == NS and ahead:
                            keep(i, 0)
                        scan(i, u, ahead > 0)
                        if u in LATE and not first:
                            front(i - 1, LATE[u], 1)
                        if u == 6 and not first:
                            gate(i - 1, 1)
                        if u == 15 and not first:
                            residual(i - 1)
                        if u == 22:
                            gate(i, 0)
                        for step, h in FRONT.get(u, []):
                            if ahead > (step == "hn"):
                                front(i, step, h)

                front(-1, "hn", -1)
                for slot in sorted(FRONT):
                    for step, h in FRONT[slot]:
                        if step != "hn":
                            front(-1, step, h)
                for step in LATE.values():
                    front(-1, step, 1)
                front(-1, "hn", 0)
                drive(0, 0)
                body(0, 2)
                with dve.Fori(1, ITEMS - 2) as i:
                    body(i, 2)
                body(ITEMS - 2, 1)
                body(ITEMS - 1, 0)
                gate(ITEMS - 1, 1)
                residual(ITEMS - 1)

            @block.gpsimd
            def _(pool):
                def weigh(i, u):
                    g, h, n = UN * i + u, u // NS, u % NS
                    if h == 0:
                        pool.wait_ge(c_in, NS * i + n + 1)
                    pool.wait_ge(scanned, g + 1)
                    if not isinstance(g, int) or g >= NP:
                        pool.wait_ge(prod_used, g - NP + 1)
                    pool.tensor_tensor(prod[:, u % NP, :], h_ring[:, n, :], c_all[:, n, :], ALU.mult).then_inc(prod_in, 1)

                def front(i, step, h):
                    j = i + 1
                    if step == "small":
                        pool.wait_ge(half_sq, HV * j + h + 1)
                        pool.tensor_tensor(small[:, h, :], ea[:, h, :], small[:, h, :], ALU.subtract)\
                            .then_inc(small_in, 1)
                    elif step == "small_pos":
                        pool.wait_ge(small_in, HV * j + h + 1)
                        pool.tensor_tensor(small_pos[:, h, :], small[:, h, :], pos[:, h, :], ALU.add)\
                            .then_inc(pos_in, 1)
                    elif step == "base":
                        pool.wait_ge(err_in, HV * j + h + 1)
                        pool.wait_ge(small_in, HV * j + h + 1)
                        pool.tensor_tensor(w1p[:, h, :], w1p[:, h, :], small[:, h, :], ALU.add).then_inc(base_in, 1)
                    elif step == "du":
                        pool.wait_ge(delta_in, HV * j + h + 1)
                        pool.wait_ge(xs_in, HV * j + h + 1)
                        if not isinstance(j, int) or j > 1:
                            pool.wait_ge(drive_in, UN * (j - 2) + NS * (h + 1))
                        pool.tensor_tensor(par(du, j, h), par(delta, j, h), par(xs, j, h), ALU.mult).then_inc(du_in, 1)

                FRONT = {19: ("small", 0), 21: ("base", 0), 22: ("small_pos", 0), 26: ("small", 1), 28: ("du", 0),
                         29: ("base", 1)}
                LATE = {0: "small_pos", 5: "du"}

                def body(i, last):
                    for u in range(UN):
                        weigh(i, u)
                        if u in LATE and (not isinstance(i, int) or i > 0):
                            front(i - 1, LATE[u], 1)
                        if not last and u in FRONT:
                            front(i, *FRONT[u])

                for slot in sorted(FRONT):
                    front(-1, *FRONT[slot])
                for step in LATE.values():
                    front(-1, step, 1)
                body(0, False)
                with pool.Fori(1, ITEMS - 1) as i:
                    body(i, False)
                body(ITEMS - 1, True)

        tail(nc, ctx, sem, bank, v, V, Cn, r, ident, meanw, center, eps, h0_d, s_d, x_d, y_d, sort, fc1, fc2, wr, br, wexp, out,
             h_ring, c_all, decay, prod, delta, du, xs, zs, rows)


def tail(nc, ctx, sem, bank, v, V, Cn, r, ident, meanw, center, eps, h0_d, s_d, x_d, y_d, sort, fc1, fc2, wr, br, wexp, out,
         h_ring, c_all, decay, prod, delta, du, xs, zs, row_numbers):
    names = ["s_in", "h0_in", "sqd", "var", "rst", "cen", "scl", "hid", "hsum", "mlp1", "g_in", "mlp2", "a1", "h1",
             "xn", "rt", "route", "turned", "flat"]
    q = {n: [sem(f"t_{n}_s{s}") for s in range(2)] for n in names}
    w_loaded = sem("t_w_loaded")
    zero_in = sem("zero_in")
    zeroed = sem("zeroed")

    fc1_s = decay[:, 0, :]
    fc2_s = decay[:, 1, :].rearrange("p (k o) -> p k o", k=HB)
    wr_s = decay[:, 2, 0:E]
    br_s = decay[:, 2, E:2 * E]
    zero = decay[:, 3, 0:P]
    So = prod[:, 2:4, :].rearrange("p a b -> p (a b)")[:, 0:NSORT]
    D = [delta[:, s, :, :] for s in range(2)]
    s_in = [D[s][:, 0, :] for s in range(2)]
    h0_in = [D[s][:, 1, :] for s in range(2)]
    sqb = [du[:, s, 0, :] for s in range(2)]
    lnb = [du[:, s, 1, :] for s in range(2)]
    rsb = [xs[:, s, 0, :] for s in range(2)]
    tmp = [xs[:, s, 1, :] for s in range(2)]
    hsum = [zs[:, s, 0, :] for s in range(2)]
    xn = [zs[:, s, 1, :] for s in range(2)]
    gel = [h_ring[:, 4 * s:4 * s + 4, :] for s in range(2)]
    h1 = [prod[:, s, :] for s in range(2)]
    xn_tok = c_all[:, 0:NCH, :]
    h1_tok = c_all[:, NCH:2 * NCH, :]
    route = decay[:, 4, 0:2 * 3 * TT * E].rearrange("p (s a t e) -> p s a t e", s=2, a=3, t=TT)
    top = decay[:, 5, 0:2 * NCH * TT].rearrange("p (a c t) -> p a c t", a=2, c=NCH)
    one_hot = decay[:, 6, 0:NCH * TT * E].rearrange("p (c n) -> p c n", c=NCH)
    lg = [route[:, s, 0] for s in range(2)]
    eq = [route[:, s, 1] for s in range(2)]
    rk = [route[:, s, 2] for s in range(2)]
    rank = So[:, SORT["rank"]:SORT["rank"] + E].unsqueeze(1).to_broadcast([P, TT, E])

    def chunk_d(t, k, s):
        return t[k + s * CPB, :, :]

    def chunk(k, s):
        return r[:, k + s * CPB, :]

    with nc.Block() as block:

        @block.sync
        def _(sp):
            sp.dma_start(fc1_s, fc1).then_inc(w_loaded, 16)
            sp.dma_start(fc2_s, fc2).then_inc(w_loaded, 16)
            sp.dma_start(wr_s, wr).then_inc(w_loaded, 16)
            sp.dma_start(br_s, br.partition_broadcast(P)).then_inc(w_loaded, 16)
            sp.dma_start(So, sort).then_inc(w_loaded, 16)
            sp.wait_ge(zero_in, 1)
            sp.dma_start(x_d.rearrange("(p n) c -> p n c", p=P), zero.unsqueeze(1).to_broadcast([P, NT * ET // P, P]))\
              .then_inc(zeroed, 16)
            def one_round(k):
                for s in range(2):
                    if later(k):
                        sp.wait_ge(q["a1"][s], k)
                        sp.wait_ge(q["h1"][s], k)
                    sp.dma_start(s_in[s], chunk_d(s_d, k, s)).then_inc(q["s_in"][s], 16)
                    sp.dma_start(h0_in[s], chunk_d(h0_d, k, s)).then_inc(q["h0_in"][s], 16)
            rounds(sp, one_round)
            sp.wait_ge(zeroed, 16)

        @block.tensor
        def _(pe):
            pe.wait_ge(w_loaded, 5 * 16)
            def one_round(k):
                def each(ready, f, count=None):
                    for s in range(2):
                        pe.wait_ge(q[ready][s], k + 1 if count is None else count)
                        f(s)
                each("sqd", lambda s: pe.matmul(bank(4 * s + 2), meanw, sqb[s], start=True, stop=True)
                     .then_inc(q["var"][s], 1), 3 * k + 1)
                each("hsum", lambda s: pe.matmul(bank(4 * s + 1), center, hsum[s], start=True, stop=True)
                     .then_inc(q["cen"][s], 1))
                each("sqd", lambda s: pe.matmul(bank(4 * s + 2), meanw, sqb[s], start=True, stop=True)
                     .then_inc(q["var"][s], 1), 3 * k + 2)
                for s in range(2):
                    pe.wait_ge(q["xn"][s], k + 1)
                    for b in range(HB):
                        if b >= 2:
                            pe.wait_ge(q["g_in"][s], HB * k + b - 1)
                        pe.matmul(bank(4 * s + (0, 3)[b % 2]), fc1_s[:, b * P:(b + 1) * P], tmp[s], start=True,
                                  stop=True).then_inc(q["mlp1"][s], 1)
                for s in range(2):
                    for b in range(HB):
                        pe.wait_ge(q["g_in"][s], HB * k + b + 1)
                        mm = pe.matmul(bank(4 * s + 2), fc2_s[:, b, :], gel[s][:, b, :], start=(b == 0),
                                       stop=(b == HB - 1))
                    mm.then_inc(q["mlp2"][s], 1)
                each("h1", lambda s: pe.matmul(bank(4 * s + 1), center, h1[s], start=True, stop=True)
                     .then_inc(q["cen"][s], 1))
                each("sqd", lambda s: pe.matmul(bank(4 * s + 2), meanw, sqb[s], start=True, stop=True)
                     .then_inc(q["var"][s], 1), 3 * k + 3)
                for s in range(2):
                    pe.wait_ge(q["scl"][s], 2 * k + 2)
                    for t in range(TT):
                        mm = pe.matmul(bank(4 * s)[:, t * E:(t + 1) * E], xn[s][:, t * P:(t + 1) * P], wr_s,
                                       start=True, stop=True)
                    mm.then_inc(q["rt"][s], 1)
                for s in range(2):
                    for src, b in ((h1, 1), (xn, 3)):
                        for t in range(TT):
                            mm = pe.transpose(bank(4 * s + b)[:, t * P:(t + 1) * P], src[s][:, t * P:(t + 1) * P], ident)
                        mm.then_inc(q["turned"][s], 1)
            rounds(pe, one_round)

        @block.scalar
        def _(act):
            def one_round(k):
                act.preload_act_table_set(LOG_EXP)
                def rs(m, s):
                    act.wait_ge(q["var"][s], 3 * k + m + 1)
                    act.activation(lnb[s], bank(4 * s + 2), ACT.Ln, bias=eps).then_inc(q["rst"][s], 1)
                    act.wait_ge(q["rst"][s], 6 * k + 2 * m + 1)
                    act.activation(rsb[s], lnb[s], ACT.Exp, scale=-0.5).then_inc(q["rst"][s], 1)

                def square(m, s):
                    act.wait_ge(q["cen"][s], 2 * k + m)
                    act.activation(sqb[s], bank(4 * s + 1), ACT.Square).then_inc(q["sqd"][s], 1)

                for s in range(2):
                    act.activation(sqb[s], chunk(k, s), ACT.Square).then_inc(q["sqd"][s], 1)
                for s in range(2):
                    rs(0, s)
                for s in range(2):
                    square(1, s)
                for s in range(2):
                    rs(1, s)
                for s in range(2):
                    act.wait_ge(q["scl"][s], 2 * k + 1)
                    act.activation(tmp[s], xn[s], ACT.Identity, scale=v("ln2_w"), bias=v("ln2_b"))\
                       .then_inc(q["xn"][s], 1)
                for s in range(2):
                    for b in range(HB):
                        act.wait_ge(q["mlp1"][s], HB * k + b + 1)
                        act.activation(gel[s][:, b, :], bank(4 * s + (0, 3)[b % 2]), ACT.Gelu_apprx_tanh,
                                       bias=v("fc1_b", b)).then_inc(q["g_in"][s], 1)
                act.preload_act_table_set(LOG_EXP)
                for s in range(2):
                    square(2, s)
                for s in range(2):
                    rs(2, s)
                for s in range(2):
                    for m, dst in enumerate((h1_tok, xn_tok)):
                        act.wait_ge(q["turned"][s], 2 * k + m + 1)
                        act.activation(dst[:, k + s * CPB, :], bank(4 * s + (1, 3)[m]), ACT.Identity)\
                           .then_inc(q["flat"][s], 1)
            rounds(act, one_round)

        @block.vector
        def _(dve):
            dve.memset(zero, 0.0).then_inc(zero_in, 1)
            dve.wait_ge(w_loaded, 5 * 16)
            def one_round(k):
                def each(f):
                    for s in range(2):
                        f(s)

                def hidden(s):
                    dve.wait_ge(q["rst"][s], 6 * k + 2)
                    dve.scalar_tensor_tensor(tmp[s], chunk(k, s), v("norm_f"), rsb[s], ALU.mult, ALU.mult)\
                       .then_inc(q["hid"][s], 1)

                def hsums(s):
                    dve.wait_ge(q["hid"][s], k + 1)
                    dve.wait_ge(q["s_in"][s], 16 * (k + 1))
                    dve.tensor_tensor(hsum[s], tmp[s], s_in[s], ALU.add).then_inc(q["hsum"][s], 1)

                def scaled(m, dst):
                    def f(s):
                        dve.wait_ge(q["rst"][s], 6 * k + 2 * m + 2)
                        dve.tensor_tensor(dst[s], bank(4 * s + 1), rsb[s], ALU.mult).then_inc(q["scl"][s], 1)
                    return f

                def a1(s):
                    dve.wait_ge(q["mlp2"][s], k + 1)
                    dve.scalar_tensor_tensor(hsum[s], bank(4 * s + 2), v("fc2_b"), hsum[s], ALU.add, ALU.add)\
                       .then_inc(q["a1"][s], 1)

                def h1s(s):
                    dve.wait_ge(q["a1"][s], k + 1)
                    dve.wait_ge(q["h0_in"][s], 16 * (k + 1))
                    dve.tensor_tensor(h1[s], hsum[s], h0_in[s], ALU.add).then_inc(q["h1"][s], 1)

                each(hidden)
                each(hsums)
                each(scaled(1, xn))
                each(a1)
                each(h1s)
                each(scaled(2, xn))
                c = [k + s * CPB for s in range(2)]
                for s in range(2):
                    dve.wait_ge(q["rt"][s], k + 1)
                    dve.tensor_tensor(lg[s], bank(4 * s)[:, 0:TT * E].rearrange("p (t e) -> p t e", t=TT),
                                      br_s.unsqueeze(1).to_broadcast([P, TT, E]), ALU.add).then_inc(q["route"][s], 1)
                for s in range(2):
                    dve.wait_ge(q["route"][s], 6 * k + 1)
                    dve.reduce_max(top[:, 0, c[s], :], lg[s], AX).then_inc(q["route"][s], 1)
                for s in range(2):
                    dve.wait_ge(q["route"][s], 6 * k + 2)
                    dve.tensor_tensor(eq[s], lg[s], top[:, 0, c[s], :].unsqueeze(2).to_broadcast([P, TT, E]),
                                      ALU.is_equal).then_inc(q["route"][s], 1)
                for s in range(2):
                    dve.wait_ge(q["route"][s], 6 * k + 3)
                    dve.tensor_tensor(rk[s], eq[s], rank, ALU.mult).then_inc(q["route"][s], 1)
                for s in range(2):
                    dve.wait_ge(q["route"][s], 6 * k + 4)
                    dve.reduce_max(top[:, 1, c[s], :], rk[s], AX).then_inc(q["route"][s], 1)
                for s in range(2):
                    dve.wait_ge(q["route"][s], 6 * k + 5)
                    dve.tensor_tensor(one_hot[:, c[s], :].rearrange("p (t e) -> p t e", e=E), rk[s],
                                      top[:, 1, c[s], :].unsqueeze(2).to_broadcast([P, TT, E]),
                                      ALU.is_equal).then_inc(q["route"][s], 1)
            rounds(dve, one_round)

    experts(nc, sem, row_numbers, bank, So, ident, x_d, y_d, wexp, out, h_ring, xn_tok, h1_tok, prod, delta, du, xs, zs, top, one_hot)


def experts(nc, sem, row_numbers, bank, So, ident, x_d, y_d, wexp, out, h_ring, xn_tok, h1_tok, prod, delta, du, xs, zs, top, one_hot):
    ones = So[:, SORT["ones"]:SORT["ones"] + P]
    before = So[:, SORT["before"]:SORT["before"] + P]
    multiple = So[:, SORT["multiple"]:SORT["multiple"] + TOK // ET]
    number = So[:, SORT["number"]:SORT["number"] + NT]
    row = So[:, SORT["row"]:SORT["row"] + 1]
    restart = So[:, SORT["restart"]:SORT["restart"] + E * RT]
    counts = prod[:, 4:6, :].rearrange("p a b -> p (a b)")[:, 0:4 * RT * E].rearrange("p (a n) -> p a n", a=4)
    few = prod[:, 6, 0:3 * E].rearrange("p (a e) -> p a e", a=3)
    cmp_k = prod[:, 6, 128:128 + E * (TOK // ET)].rearrange("p (e n) -> p e n", e=E)
    cmp_t = prod[:, 6, 256:256 + NT * E].rearrange("p (t e) -> p t e", e=E)
    tile_e = prod[:, 7, 0:3 * NT].rearrange("p (a t) -> p a t", a=3)
    slot_f = prod[:, 7, 128:128 + RT]
    slot = row_numbers[:, 0:RT]
    w_row = row_numbers[:, RT:RT + NT]
    gate = prod[:, 7, 256:256 + 4 * RT].rearrange("p (a t) -> p a t", a=4)

    def te(t):
        return t.rearrange("p (t e) -> p t e", e=E)

    hr = h_ring[:, :, :].rearrange("p a b -> p (a b)")
    w_ring = [hr[:, i * NX:(i + 1) * NX] for i in range(4)]
    x_ring = [xs[:, i // 2, i % 2, 0:ET].rearrange("p (t c) -> p t c", c=P) for i in range(4)]
    x_t = [zs[:, i, 0, 0:ET] for i in range(2)]
    y_s = [zs[:, i, 1, 0:ET].rearrange("p (t c) -> p t c", c=P) for i in range(2)]
    hid = [t[:, :, :, :].rearrange("p a b c -> p (a b c)")[:, 0:HB * ET].rearrange("p (b c) -> p b c", b=HB)
           for t in (delta, du)]
    back = xn_tok
    sums = sem("sums")
    counted = sem("counted")
    zero_diff = sem("zero_diff")
    gate_exp = sem("gate_exp")
    gate_in = sem("gate_in")
    slots_in = sem("slots_in")
    rows_in = sem("rows_in")
    scattered = sem("scattered")
    fetched = [sem(f"fetched{i}") for i in range(4)]
    x_in = [sem(f"e_x_in{i}") for i in range(4)]
    turned = sem("e_turned")
    x_ready = sem("e_x_ready")
    up = sem("e_up")
    relu_in = sem("e_relu")
    down = sem("e_down")
    y_made = sem("e_y_made")
    y_kept = [sem(f"e_y_kept{i}") for i in range(2)]
    taken = [sem(f"taken{c}") for c in range(NCH)]
    mixed = sem("mixed")
    kept = sem("out_kept")

    def tile_rounds(eng, step):
        for i in range(4):
            step(0, i)
        with eng.Fori(1, NT // 4) as k:
            for i in range(4):
                step(k, i)
        for i in range(NT % 4):
            step(NT // 4, i)

    def tiles(t_d):
        return t_d.rearrange("(j t p) c -> j p t c", p=P, t=ET // P)

    def fixed(j):
        return isinstance(j, int)

    with nc.Block() as block:

        @block.gpsimd
        def _(pool):
            def fetch(j):
                if j >= 4:
                    pool.wait_ge(y_made, j - 3)
                pool.indirect_dma_start(out=w_ring[j % 4], out_offset=None, in_=wexp,
                                        in_offset=bass.IndirectOffsetOnAxis(ap=w_row[:, j:j + 1], axis=0))\
                    .then_inc(fetched[j % 4], 16)
            pool.wait_ge(slots_in, 1)
            for t in range(RT):
                pool.indirect_dma_start(out=x_d, out_offset=bass.IndirectOffsetOnAxis(ap=slot[:, t:t + 1], axis=0),
                                        in_=xn_tok[:, t // TT, (t % TT) * P:(t % TT + 1) * P], in_offset=None)\
                    .then_inc(scattered, 16)
                if t == RT // 2:
                    pool.wait_ge(rows_in, 1)
                    for j in range(4):
                        fetch(j)
            for j in range(4, NT):
                fetch(j)
            pool.wait_ge(scattered, 16 * RT)
            pool.wait_ge(y_kept[0], 16 * ((NT + 1) // 2))
            pool.wait_ge(y_kept[1], 16 * (NT // 2))
            for t in range(RT):
                pool.indirect_dma_start(out=back[:, t // TT, (t % TT) * P:(t % TT + 1) * P], out_offset=None, in_=y_d,
                                        in_offset=bass.IndirectOffsetOnAxis(ap=slot[:, t:t + 1], axis=0))\
                    .then_inc(taken[t // TT], 16)

        @block.sync
        def _(sp):
            def load(k, i):
                j = 4 * k + i
                sp.dma_start(x_ring[i % 4], tiles(x_d)[j, :, :, :]).then_inc(x_in[i % 4], 16)

            def store(k, i):
                j = 4 * k + i
                sp.wait_ge(y_made, j + 1)
                sp.dma_start(tiles(y_d)[j, :, :, :], y_s[i % 2])\
                  .then_inc(y_kept[i % 2], 16)

            sp.wait_ge(scattered, 16 * RT)
            for j in range(3):
                load(0, j)
            def step(k, i):
                j = 4 * k + i
                if not fixed(j) or j + 3 < NT:
                    if not fixed(j) or j > 0:
                        sp.wait_ge(turned, j)
                    load(k, i + 3)
                if not fixed(j) or j > 0:
                    store(k, i - 1)
            tile_rounds(sp, step)
            store(NT // 4, NT % 4 - 1)
            for c in range(NCH):
                sp.wait_ge(mixed, TT * (c + 1))
                sp.dma_start(out[c, :, :, :].rearrange("t p c -> p t c"),
                             back[:, c, :].rearrange("p (t c) -> p t c", t=TT)).then_inc(kept, 16)
            sp.wait_ge(kept, 16 * NCH)

        @block.tensor
        def _(pe):
            hot = one_hot[:, :, :].rearrange("p a b -> p (a b)")
            pe.matmul(bank(0)[:, 0:RT * E], before, hot, start=True, stop=True)
            pe.matmul(bank(1)[:, 0:RT * E], ones, hot, start=True, stop=True).then_inc(counted, 1)

            def turn(k, i):
                j = 4 * k + i
                pe.wait_ge(x_in[i % 4], 16 * (k + i // 4 + 1))
                if not fixed(j) or j >= 2:
                    pe.wait_ge(x_ready, j - 1)
                for t in range(ET // P):
                    mm = pe.transpose(bank(i % 2)[:, t * P:(t + 1) * P], x_ring[i % 4][:, t, :], ident)
                mm.then_inc(turned, 1)

            def ups(k, i):
                j = 4 * k + i
                pe.wait_ge(fetched[i % 4], 16 * (k + i // 4 + 1))
                pe.wait_ge(x_ready, j + 1)
                if not fixed(j) or j >= 2:
                    pe.wait_ge(relu_in, HB * (j - 1))
                for b in range(HB):
                    o = 2 + 2 * (i % 2) + b // 2
                    mm = pe.matmul(bank(o)[:, b % 2 * ET:(b % 2 + 1) * ET], w_ring[i % 4][:, b * P:(b + 1) * P],
                                   x_t[i % 2], start=True, stop=True)
                    if b % 2:
                        mm.then_inc(up, 1)

            def downs(k, i):
                j = 4 * k + i
                pe.wait_ge(relu_in, HB * (j + 1))
                if not fixed(j) or j >= 2:
                    pe.wait_ge(y_made, j - 1)
                for t in range(ET // P):
                    for b in range(HB):
                        o = HB * P + b * P
                        mm = pe.matmul(bank(6 + i % 2)[:, t * P:(t + 1) * P], hid[i % 2][:, b, t * P:(t + 1) * P],
                                       w_ring[i % 4][:, o:o + P], start=(b == 0), stop=(b == HB - 1))
                mm.then_inc(down, 1)

            pe.wait_ge(sums, 9)
            turn(0, 0)
            def step(k, i):
                j = 4 * k + i
                if not fixed(j) or j + 1 < NT:
                    turn(k, i + 1)
                ups(k, i)
                if not fixed(j) or j > 0:
                    downs(k, i - 1)
            tile_rounds(pe, step)
            downs(NT // 4, NT % 4 - 1)

        @block.scalar
        def _(act):
            act.wait_ge(zero_diff, 1)
            act.activation(gate[:, 1, :], gate[:, 0, :], ACT.Exp).then_inc(gate_exp, 1)
            def step(k, i):
                j = 4 * k + i
                for b in range(HB):
                    if b % 2 == 0:
                        act.wait_ge(up, HB // 2 * j + b // 2 + 1)
                    if b == 0 and (not fixed(j) or j >= 2):
                        act.wait_ge(down, j - 1)
                    o = 2 + 2 * (i % 2) + b // 2
                    act.activation(hid[i % 2][:, b, :], bank(o)[:, b % 2 * ET:(b % 2 + 1) * ET], ACT.Relu,
                                   bias=w_ring[i % 4][:, 2 * HB * P + b:2 * HB * P + b + 1]).then_inc(relu_in, 1)
            tile_rounds(act, step)

        @block.vector
        def _(dve):
            done = 0
            def chain(op):
                nonlocal done
                op.then_inc(sums, 1)
                done += 1
                dve.wait_ge(sums, done)
            dve.wait_ge(counted, 1)
            chain(dve.tensor_copy(counts[:, 0, :].rearrange("p (e t) -> p e t", e=E),
                                  bank(1)[:, 0:RT * E].rearrange("p (t e) -> p e t", e=E)))
            chain(dve.tensor_tensor_scan(counts[:, 1, :], restart, counts[:, 0, :], 0.0, ALU.mult, ALU.add))
            total = counts[:, 1, :].rearrange("p (e t) -> p e t", e=E)
            chain(dve.tensor_tensor(cmp_k[:, :, :], total[:, :, RT - 1:RT].to_broadcast([P, E, TOK // ET]),
                                    multiple.unsqueeze(1).to_broadcast([P, E, TOK // ET]), ALU.is_gt))
            chain(dve.reduce_sum(few[:, 0, :], cmp_k[:, :, :], AX))
            chain(dve.tensor_tensor_scan(few[:, 1, :], ones[:, 0:E], few[:, 0, :], 0.0, ALU.mult, ALU.add))
            chain(dve.tensor_tensor(few[:, 2, :], few[:, 1, :], few[:, 0, :], ALU.subtract))
            chain(dve.scalar_tensor_tensor(te(counts[:, 2, :]), few[:, 2, :].unsqueeze(1).to_broadcast([P, RT, E]),
                                           float(ET), total.rearrange("p e t -> p t e"), ALU.mult, ALU.add))
            chain(dve.tensor_tensor(te(counts[:, 2, :]), te(counts[:, 2, :]),
                                    counts[:, 0, :].rearrange("p (e t) -> p t e", e=E), ALU.subtract))
            chain(dve.tensor_tensor(counts[:, 3, :], bank(0)[:, 0:RT * E], counts[:, 2, :], ALU.add))
            chain(dve.tensor_tensor(counts[:, 3, :], counts[:, 3, :], one_hot[:, :, :].rearrange("p a b -> p (a b)"),
                                    ALU.mult))
            chain(dve.reduce_sum(slot_f[:, :], te(counts[:, 3, :]), AX))
            dve.tensor_copy(slot[:, :], slot_f[:, :]).then_inc(slots_in, 1)
            chain(dve.tensor_tensor(cmp_t[:, :, :], number.unsqueeze(2).to_broadcast([P, NT, E]),
                                    few[:, 1, :].unsqueeze(1).to_broadcast([P, NT, E]), ALU.is_ge))
            chain(dve.reduce_sum(tile_e[:, 0, :], cmp_t[:, :, :], AX))
            chain(dve.tensor_scalar(tile_e[:, 1, :], tile_e[:, 0, :], float(E - 1), float(P), ALU.min, ALU.mult))
            chain(dve.tensor_scalar(tile_e[:, 2, :], tile_e[:, 1, :], row, None, ALU.add))
            dve.tensor_copy(w_row[:, :], tile_e[:, 2, :]).then_inc(rows_in, 1)
            chosen = top[:, 0, :, :].rearrange("p a b -> p (a b)")
            dve.tensor_tensor(gate[:, 0, :], chosen, chosen, ALU.subtract).then_inc(zero_diff, 1)
            dve.wait_ge(gate_exp, 1)
            chain(dve.reciprocal(gate[:, 2, :], gate[:, 1, :]))
            dve.tensor_tensor(gate[:, 3, :], gate[:, 1, :], gate[:, 2, :], ALU.mult).then_inc(gate_in, 1)

            def rows(k, i):
                j = 4 * k + i
                dve.wait_ge(turned, j + 1)
                if not fixed(j) or j >= 2:
                    dve.wait_ge(up, HB // 2 * (j - 1))
                dve.tensor_copy(x_t[i % 2], bank(i % 2)[:, 0:ET]).then_inc(x_ready, 1)

            def result(k, i):
                j = 4 * k + i
                dve.wait_ge(down, j + 1)
                if not fixed(j) or j >= 2:
                    dve.wait_ge(y_kept[i % 2], 16 * (2 * k + i // 2))
                b2 = w_ring[i % 4][:, 2 * HB * P + HB:2 * HB * P + HB + P].unsqueeze(1).to_broadcast([P, ET // P, P])
                dve.tensor_tensor(y_s[i % 2], bank(6 + i % 2)[:, 0:ET].rearrange("p (t c) -> p t c", c=P), b2, ALU.add)\
                   .then_inc(y_made, 1)

            rows(0, 0)
            def step(k, i):
                j = 4 * k + i
                if not fixed(j) or j + 1 < NT:
                    rows(k, i + 1)
                if not fixed(j) or j > 0:
                    result(k, i - 1)
            tile_rounds(dve, step)
            result(NT // 4, NT % 4 - 1)
            dve.wait_ge(gate_in, 1)
            for t in range(RT):
                c, o = t // TT, (t % TT) * P
                if t % TT == 0:
                    dve.wait_ge(taken[c], 16 * TT)
                dve.scalar_tensor_tensor(back[:, c, o:o + P], back[:, c, o:o + P], gate[:, 3, t:t + 1],
                                         h1_tok[:, c, o:o + P], ALU.mult, ALU.add).then_inc(mixed, 1)


def kernel(**inputs):
    import concourse.bacc as _bacc
    from concourse.bass_utils import run_bass_kernel_spmd as _run

    a = {k: np.asarray(x) for k, x in inputs.items()}

    def cols(x):
        return x.reshape(-1, P).T

    pre = "L0_attn_"
    vec = np.concatenate([
        a["L0_tok_conv_w"], cols(a["L0_tok_gamma"]), cols(a["L0_tok_beta"]), cols(a[pre + "ln1_w"]),
        cols(a[pre + "ln1_b"]), cols(a[pre + "norm_f_w"]), cols(a[pre + "ln2_w"]), cols(a[pre + "ln2_b"]),
        cols(a[pre + "fc2_b"]), cols(a[pre + "block_norm_w"]), cols(a[pre + "fc1_b"]), cols(a[pre + "conv_b"]),
        cols(a[pre + "dt_proj_b"]), cols(a[pre + "D_param"]),
        a[pre + "A_log"].reshape(NL, HV, P, NS).transpose(2, 0, 1, 3).reshape(P, NL * HV * NS)], axis=1)
    con = np.zeros((P, NCON), np.float32)
    con[:, CON["ident"]:CON["ident"] + P] = np.eye(P)
    con[:, CON["mean"]:CON["mean"] + P] = 1.0 / P
    con[:, CON["center"]:CON["center"] + P] = np.eye(P) - 1.0 / P
    con[:, CON["pick"]:CON["pick"] + 2 * NS] = np.arange(P)[:, None] % (2 * NS) == np.arange(2 * NS)[None, :]
    con[:, CON["keep"]:CON["keep"] + ITEMS] = np.arange(ITEMS)[None, :] % CPB != 0
    con[:, CON["eps"]] = EPS
    con[:, CON["one"]] = 1.0

    sort = np.zeros((P, NSORT), np.float32)
    sort[:, SORT["rank"]:SORT["rank"] + E] = E - np.arange(E)[None, :]
    sort[:, SORT["ones"]:SORT["ones"] + P] = 1.0
    sort[:, SORT["before"]:SORT["before"] + P] = np.arange(P)[:, None] < np.arange(P)[None, :]
    sort[:, SORT["multiple"]:SORT["multiple"] + TOK // ET] = ET * np.arange(TOK // ET)[None, :]
    sort[:, SORT["number"]:SORT["number"] + NT] = np.arange(NT)[None, :]
    sort[:, SORT["row"]] = np.arange(P)
    sort[:, SORT["restart"]:SORT["restart"] + E * RT] = np.arange(E * RT)[None, :] % RT != 0

    win = a[pre + "in_proj_w"].transpose(2, 0, 1)
    arrays = {
        "tok": a["x"].reshape(TOK // P, P).T.view(np.uint32) if a["x"].dtype == np.int32 else a["x"].reshape(TOK // P, P).T,
        "embed": a["L0_tok_embed_table"],
        "vec": vec,
        "con": con,
        "sort": sort,
        "win_x": win[:, :, 0:DI],
        "win_z": win[:, :, DI:2 * DI],
        "conv_w": a[pre + "conv_w"].transpose(0, 2, 1),
        "xproj": a[pre + "x_proj_w"].reshape(NL, R + 2 * NS, HV, P).transpose(0, 3, 2, 1),
        "dtw": a[pre + "dt_proj_w"].transpose(0, 2, 1),
        "outw": a[pre + "out_proj_w"].reshape(NL, P, HV, P).transpose(0, 3, 2, 1).reshape(NL, P, HV * P),
        "fc1": a[pre + "fc1_w"].T,
        "fc2": a[pre + "fc2_w"].reshape(P, HB, P).transpose(2, 1, 0),
        "wr": a["L0_ffn_Wr"],
        "br": a["L0_ffn_br"],
        "wexp": np.concatenate([
            a["L0_ffn_W1"], a["L0_ffn_W2"].reshape(E, HB, P, P).transpose(0, 2, 1, 3).reshape(E, P, HB * P),
            a["L0_ffn_b1"].reshape(E, HB, P).transpose(0, 2, 1),
            np.broadcast_to(a["L0_ffn_b2"][:, None, :], (E, P, P))], axis=2).reshape(E * P, NX),
    }
    arrays = {f"in_{k}": np.ascontiguousarray(x) for k, x in arrays.items()}
    nc = _bacc.Bacc("TRN2", target_bir_lowering=False, num_devices=1)
    args = [nc.dram_tensor(k, x.shape, mybir.dt.from_np(x.dtype), kind="ExternalInput").ap() for k, x in arrays.items()]
    args.append(nc.dram_tensor("out_0", (NCH, TT, P, P), F32, kind="ExternalOutput").ap())
    lm_tower(nc, *args)
    res = _run(nc, [arrays], core_ids=[0])
    return res.results[0]["out_0"].reshape(BATCH, TOK // BATCH, P)
```
